# Optimizing a Trainium2 kernel written in Bass

```python
import numpy as np
import jax
import jax.numpy as jnp

def _softmax(x, axis=-1):
    return jax.nn.softmax(x, axis=axis)

def _gelu(x):
    return jax.nn.gelu(x, approximate=True)

def _silu(x):
    return jax.nn.silu(x)

def _sigmoid(x):
    return jax.nn.sigmoid(x)

def _layernorm(x, axis=-1, eps=1e-05):
    m = jnp.mean(x, axis=axis, keepdims=True)
    v = jnp.var(x, axis=axis, keepdims=True)
    return (x - m) / jnp.sqrt(v + eps)

def _scatter_add(tgt, idx, src, axis=0):
    return tgt.at[idx].add(src)

def _segment_sum(src, seg, n):
    return jax.ops.segment_sum(src, seg, n)
kernel_name = 'mk_gnn_preln_d2_gnn_r8_1c6ff8'

def setup_inputs(seed: int=0):
    np.random.seed(seed)
    _w = jnp.asarray

    def _rec_inputs():
        import jax
        import jax.numpy as jnp
        _gk = jax.random.key(seed)
        x = -8.776e-05 + 1 * jax.random.normal(jax.random.fold_in(_gk, 1), (1250, 512), jnp.float32)
        _s = jax.random.randint(jax.random.fold_in(_gk, 2), (20000,), 0, 1250, jnp.int32)
        _d = jax.random.randint(jax.random.fold_in(_gk, 3), (20000,), 0, 1250, jnp.int32)
        _loop = jnp.arange(1250, dtype=jnp.int32)
        src = jnp.concatenate([_s, _d, _loop])
        dst = jnp.concatenate([_d, _s, _loop])
        _o = jnp.argsort(dst, stable=True)
        src = src[_o]
        dst = dst[_o]
        edge_attr_128 = 0.000283511 + 1.00007 * jax.random.normal(jax.random.fold_in(_gk, 12), (41250, 128), jnp.float32)
        edge_attr_20 = 0.000389844 + 1.00025 * jax.random.normal(jax.random.fold_in(_gk, 13), (41250, 20), jnp.float32)
        edge_attr_4 = -0.00185629 + 0.998788 * jax.random.normal(jax.random.fold_in(_gk, 14), (41250, 4), jnp.float32)
        edge_weight = jax.random.uniform(jax.random.fold_in(_gk, 16), (41250,), jnp.float32, 0.0, 0.999993)
        return (x, src, dst, edge_attr_128, edge_attr_20, edge_attr_4, edge_weight)
    x, src, dst, edge_attr_128, edge_attr_20, edge_attr_4, edge_weight = _rec_inputs()

    def _L0_gnn_setup():
        import jax, jax.numpy as jnp
        import numpy as np
        N, E = (1250, 18750)
        HD, ED = (512, 128)
        BN_EPS = 1e-05
        key = jax.random.key(seed)
        ks = jax.random.split(key, 16)
        s = 0.02
        return {'h': jax.random.normal(ks[0], (N, HD), jnp.float32), 'edge_index': jax.random.randint(ks[1], (2, E), 0, N, jnp.int32), 'edge_attr': jax.random.normal(ks[2], (E, ED), jnp.float32), 'W1': jax.random.normal(ks[3], (HD, HD + ED), jnp.float32) * s, 'b1': jnp.zeros((HD,), jnp.float32), 'W2': jax.random.normal(ks[4], (HD, HD), jnp.float32) * s, 'b2': jnp.zeros((HD,), jnp.float32), 'W_ih': jax.random.normal(ks[5], (3 * HD, HD), jnp.float32) * s, 'W_hh': jax.random.normal(ks[6], (3 * HD, HD), jnp.float32) * s, 'b_ih': jnp.zeros((3 * HD,), jnp.float32), 'b_hh': jnp.zeros((3 * HD,), jnp.float32), 'gamma': jnp.ones((HD,), jnp.float32), 'beta': jnp.zeros((HD,), jnp.float32), 'run_mean': jnp.zeros((HD,), jnp.float32), 'run_var': jnp.ones((HD,), jnp.float32)}
    _L0_gnn_all = _L0_gnn_setup()
    _L0_gnn_in = {k: v for k, v in _L0_gnn_all.items() if k in ('W1', 'b1', 'W2', 'b2', 'W_ih', 'W_hh', 'b_ih', 'b_hh', 'gamma', 'beta', 'run_mean', 'run_var')}
    del _L0_gnn_all

    def _L1_gnn_setup():
        import jax, jax.numpy as jnp
        import numpy as np
        import math
        B = 128
        F = 32
        R = 20
        N = 2048
        E = 32768
        LOG2 = 0.6931471805599453
        IS2 = 1.0 / math.sqrt(2.0)
        IS3 = 1.0 / math.sqrt(3.0)
        IS6 = 1.0 / math.sqrt(6.0)

        def ssp(x):
            return jax.nn.softplus(x) - LOG2
        key = jax.random.key(seed)
        ks = jax.random.split(key, 14)
        return dict(x=jax.random.normal(ks[0], (N, 4 * B), jnp.float32), idx_i=jax.random.randint(ks[1], (E,), 0, N), idx_j=jax.random.randint(ks[2], (E,), 0, N), f_ij=jax.random.normal(ks[3], (E, R), jnp.float32), rcut_ij=jax.random.uniform(ks[4], (E,), jnp.float32), Yr_ij=jax.random.normal(ks[5], (E, 4), jnp.float32), w_in2f_s=jax.random.normal(ks[6], (B, F), jnp.float32), w_in2f_v=jax.random.normal(ks[7], (B, F), jnp.float32), W1=jax.random.normal(ks[8], (R, F), jnp.float32) / math.sqrt(R), b1=jnp.zeros((F,), jnp.float32), W2=jax.random.normal(ks[9], (F, 6 * F), jnp.float32) / math.sqrt(F), b2=jnp.zeros((6 * F,), jnp.float32), w_f2o1_s=jax.random.normal(ks[10], (2 * F, B), jnp.float32), w_f2o1_v=jax.random.normal(ks[11], (2 * F, B), jnp.float32), w_f2o2_s=jax.random.normal(ks[12], (B, B), jnp.float32), w_f2o2_v=jax.random.normal(ks[13], (B, B), jnp.float32))
    _L1_gnn_all = _L1_gnn_setup()
    _L1_gnn_in = {k: v for k, v in _L1_gnn_all.items() if k in ('w_in2f_s', 'w_in2f_v', 'W1', 'b1', 'W2', 'b2', 'w_f2o1_s', 'w_f2o1_v', 'w_f2o2_s', 'w_f2o2_v')}
    del _L1_gnn_all
    return {'x': x, 'src': src, 'dst': dst, 'edge_attr_128': edge_attr_128, 'edge_attr_20': edge_attr_20, 'edge_attr_4': edge_attr_4, 'edge_weight': edge_weight, 'L0_gnn_W1': _L0_gnn_in['W1'], 'L0_gnn_b1': _L0_gnn_in['b1'], 'L0_gnn_W2': _L0_gnn_in['W2'], 'L0_gnn_b2': _L0_gnn_in['b2'], 'L0_gnn_W_ih': _L0_gnn_in['W_ih'], 'L0_gnn_W_hh': _L0_gnn_in['W_hh'], 'L0_gnn_b_ih': _L0_gnn_in['b_ih'], 'L0_gnn_b_hh': _L0_gnn_in['b_hh'], 'L0_gnn_gamma': _L0_gnn_in['gamma'], 'L0_gnn_beta': _L0_gnn_in['beta'], 'L0_gnn_run_mean': _L0_gnn_in['run_mean'], 'L0_gnn_run_var': _L0_gnn_in['run_var'], 'L1_gnn_w_in2f_s': _L1_gnn_in['w_in2f_s'], 'L1_gnn_w_in2f_v': _L1_gnn_in['w_in2f_v'], 'L1_gnn_W1': _L1_gnn_in['W1'], 'L1_gnn_b1': _L1_gnn_in['b1'], 'L1_gnn_W2': _L1_gnn_in['W2'], 'L1_gnn_b2': _L1_gnn_in['b2'], 'L1_gnn_w_f2o1_s': _L1_gnn_in['w_f2o1_s'], 'L1_gnn_w_f2o1_v': _L1_gnn_in['w_f2o1_v'], 'L1_gnn_w_f2o2_s': _L1_gnn_in['w_f2o2_s'], 'L1_gnn_w_f2o2_v': _L1_gnn_in['w_f2o2_v']}

def reference(x, src, dst, edge_attr_128, edge_attr_20, edge_attr_4, edge_weight, L0_gnn_W1, L0_gnn_b1, L0_gnn_W2, L0_gnn_b2, L0_gnn_W_ih, L0_gnn_W_hh, L0_gnn_b_ih, L0_gnn_b_hh, L0_gnn_gamma, L0_gnn_beta, L0_gnn_run_mean, L0_gnn_run_var, L1_gnn_w_in2f_s, L1_gnn_w_in2f_v, L1_gnn_W1, L1_gnn_b1, L1_gnn_W2, L1_gnn_b2, L1_gnn_w_f2o1_s, L1_gnn_w_f2o1_v, L1_gnn_w_f2o2_s, L1_gnn_w_f2o2_v):
    import jax
    import jax.numpy as jnp

    def _L0_gnn_ref(h, edge_index, edge_attr, W1, b1, W2, b2, W_ih, W_hh, b_ih, b_hh, gamma, beta, run_mean, run_var):
        import jax, jax.numpy as jnp
        import numpy as np
        N, E = (1250, 18750)
        HD, ED = (512, 128)
        BN_EPS = 1e-05
        src, dst = (edge_index[0], edge_index[1])
        m_in = jnp.concatenate([h[src], edge_attr], axis=1)
        m = jax.nn.relu(m_in @ W1.T + b1) @ W2.T + b2
        agg = jax.ops.segment_sum(m, dst, num_segments=h.shape[0])
        gi = agg @ W_ih.T + b_ih
        gh = h @ W_hh.T + b_hh
        i_r, i_z, i_n = jnp.split(gi, 3, axis=1)
        h_r, h_z, h_n = jnp.split(gh, 3, axis=1)
        r = jax.nn.sigmoid(i_r + h_r)
        z = jax.nn.sigmoid(i_z + h_z)
        n = jnp.tanh(i_n + r * h_n)
        h_new = (1.0 - z) * n + z * h
        bn = gamma * (h_new - run_mean) * jax.lax.rsqrt(run_var + BN_EPS) + beta
        return h + bn

    def _L1_gnn_ref(x, idx_i, idx_j, f_ij, rcut_ij, Yr_ij, w_in2f_s, w_in2f_v, W1, b1, W2, b2, w_f2o1_s, w_f2o1_v, w_f2o2_s, w_f2o2_v):
        import jax, jax.numpy as jnp
        import numpy as np
        import math
        B = 128
        F = 32
        R = 20
        N = 2048
        E = 32768
        LOG2 = 0.6931471805599453
        IS2 = 1.0 / math.sqrt(2.0)
        IS3 = 1.0 / math.sqrt(3.0)
        IS6 = 1.0 / math.sqrt(6.0)

        def ssp(x):
            return jax.nn.softplus(x) - LOG2
        n = x.shape[0]
        xs = x[:, :B]
        xv = x[:, B:].reshape(n, B, 3)
        hs = xs @ w_in2f_s / math.sqrt(B)
        hv = jnp.einsum('nbc,bf->nfc', xv, w_in2f_v) / math.sqrt(B)
        s = hs[idx_j]
        v = hv[idx_j]
        ys = Yr_ij[:, 0]
        yv = Yr_ij[:, 1:4]
        t_s1 = s * ys[:, None]
        t_s2 = jnp.einsum('efc,ec->ef', v, yv) * IS3
        t_v1 = s[:, :, None] * yv[:, None, :]
        t_v2 = v * ys[:, None, None]
        t_pv = jnp.cross(v, yv[:, None, :]) * IS2
        ax, ay, az = (v[..., 0], v[..., 1], v[..., 2])
        bx, by, bz = (yv[:, None, 0:1], yv[:, None, 1:2], yv[:, None, 2:3])
        bx, by, bz = (bx[..., 0], by[..., 0], bz[..., 0])
        t_q = jnp.stack([(ax * by + ay * bx) * IS2, (ay * bz + az * by) * IS2, (2.0 * az * bz - ax * bx - ay * by) * IS6, (ax * bz + az * bx) * IS2, (ax * bx - ay * by) * IS2], axis=-1)
        h = ssp(f_ij @ W1 + b1)
        Wij = (h @ W2 + b2) * rcut_ij[:, None]
        Wf = Wij.reshape(-1, F, 6)
        edge = jnp.concatenate([(t_s1 * Wf[..., 0])[..., None], (t_s2 * Wf[..., 1])[..., None], t_v1 * Wf[..., 2:3], t_v2 * Wf[..., 3:4], t_pv * Wf[..., 4:5], t_q * Wf[..., 5:6]], axis=-1)
        agg = jax.ops.segment_sum(edge.reshape(edge.shape[0], -1), idx_i, num_segments=n).reshape(n, F, 16)
        s_in = jnp.concatenate([agg[..., 0], agg[..., 1]], axis=1)
        v_in = jnp.concatenate([agg[..., 2:5], agg[..., 5:8]], axis=1)
        os1 = s_in @ w_f2o1_s / math.sqrt(2 * F)
        ov1 = jnp.einsum('nmc,mb->nbc', v_in, w_f2o1_v) / math.sqrt(2 * F)
        os1 = ssp(os1)
        os2 = os1 @ w_f2o2_s / math.sqrt(B)
        ov2 = jnp.einsum('nbc,bd->ndc', ov1, w_f2o2_v) / math.sqrt(B)
        return jnp.concatenate([os2, ov2.reshape(n, -1)], axis=-1)
    edge_index = jnp.stack([src, dst])
    h = jnp.maximum(_layernorm(x, axis=-1), 0.0)
    x = x + _L0_gnn_ref(h, edge_index, edge_attr_128, L0_gnn_W1, L0_gnn_b1, L0_gnn_W2, L0_gnn_b2, L0_gnn_W_ih, L0_gnn_W_hh, L0_gnn_b_ih, L0_gnn_b_hh, L0_gnn_gamma, L0_gnn_beta, L0_gnn_run_mean, L0_gnn_run_var)
    h = jnp.maximum(_layernorm(x, axis=-1), 0.0)
    x = x + _L1_gnn_ref(h, src, dst, edge_attr_20, edge_weight, edge_attr_4, L1_gnn_w_in2f_s, L1_gnn_w_in2f_v, L1_gnn_W1, L1_gnn_b1, L1_gnn_W2, L1_gnn_b2, L1_gnn_w_f2o1_s, L1_gnn_w_f2o1_v, L1_gnn_w_f2o2_s, L1_gnn_w_f2o2_v)
    return x

_drawn_inputs = setup_inputs


def setup_inputs(seed=0):
    import zlib

    import numpy as np

    out = dict(_drawn_inputs(seed))
    spreads = {'L0_gnn_b1': (0.0, 0.1),
     'L0_gnn_b2': (0.0, 0.1),
     'L0_gnn_b_ih': (0.0, 0.425),
     'L0_gnn_b_hh': (0.0, 0.616),
     'L0_gnn_gamma': (1.0, 0.2),
     'L0_gnn_beta': (0.0, 0.1),
     'L0_gnn_run_mean': (0.0, 0.1),
     'L0_gnn_run_var': (1.0, 0.2),
     'L1_gnn_b1': (0.0, 0.1),
     'L1_gnn_b2': (0.0, 0.1)}
    factors = {}
    for name, (base, spread) in spreads.items():
        noise = np.random.default_rng([zlib.crc32(name.encode()), seed]).standard_normal(out[name].shape)
        drawn = base * np.exp(spread * noise) if base else spread * noise
        out[name] = jnp.asarray(drawn.astype(out[name].dtype))
    for name, factor in factors.items():
        out[name] = (out[name] * factor).astype(out[name].dtype)
    return out
```

```python
import concourse.bass as bass
from concourse import mybir
from contextlib import ExitStack

P = 128
N, HD, ED = 1250, 512, 128
KC = HD // P
F, R = 32, 20
NE = 41250
GT = 4
GE = GT * P
NG = 2 * (-(-NE // (2 * GE)))
NT = NG * GT
W = 32
NW = N + W
NC = 250
NCH = N // NC
NTL = 125
NTT = N // NTL
ROW = 136
MSG = 320
PIECES = [(0, 417), (417, 417), (834, 416)]
LN_EPS, BN_EPS = 1e-5, 1e-5
LOG2 = 0.6931471805599453


def graph_kernel(nc, a, out):
    f32, i32 = mybir.dt.float32, mybir.dt.int32
    ALU, ACT, AX = mybir.AluOpType, mybir.ActivationFunctionType, mybir.AxisListType
    ds = bass.ds

    with ExitStack() as ctx:
        def sb(name, shape, dt=f32):
            return ctx.enter_context(nc.sbuf_tensor(name, shape, dt))

        def sem(name):
            return ctx.enter_context(nc.semaphore(name))

        xT = sb("xT", [P, KC, N])
        hT = sb("hT", [P, KC, N])
        aggT = sb("aggT", [P, KC, NW])
        degree = sb("degree", [1, NW])
        w1h = sb("w1h", [P, KC, HD])
        w1e = sb("w1e", [P, HD])
        b1_all = sb("b1_all", [P, HD])
        w2 = sb("w2", [P, KC, HD])
        b2_row = sb("b2_row", [1, HD])
        wih = sb("wih", [P, KC, 3 * HD])
        whh = sb("whh", [P, KC, 3 * HD])
        b_ih = sb("b_ih", [P, 3 * KC])
        b_hh = sb("b_hh", [P, 3 * KC])
        b_rz = sb("b_rz", [P, 2 * KC])
        bn = sb("bn", [P, 4, KC])
        bn_scale = sb("bn_scale", [P, KC])
        bn_shift = sb("bn_shift", [P, KC])
        w_in = sb("w_in", [P, 2, F])
        fw1 = sb("fw1", [R, F])
        fb1 = sb("fb1", [F, 1])
        fw2 = sb("fw2", [F + 1, 4 * F])
        wo1s = sb("wo1s", [P, P])
        wo1v = sb("wo1v", [P, 2, P])
        wo2 = sb("wo2", [P, 2, P])
        src0 = sb("src0", [P, NT], i32)
        dst0 = sb("dst0", [P, NT], i32)
        srcm = sb("srcm", [P, NT], i32)
        dstm = sb("dstm", [P, NT], i32)
        dst_f = sb("dst_f", [P, NT])
        src_f = sb("src_f", [P, NT])
        base_i = sb("base_i", [P, NG], i32)
        base_f = sb("base_f", [P, NG])
        rel = sb("rel", [P, NT])
        left_key = sb("left_key", [P, NT])
        in_win = sb("in_win", [P, NT])
        tmp_e = sb("tmp_e", [P, NT])
        y4 = sb("y4", [P, NT, 4])
        rcut = sb("rcut", [P, NT])
        n_left = sb("n_left", [P, 1])
        flag = sb("flag", [1, 1], i32)
        iota = sb("iota", [P, N])
        ones = sb("ones", [P, P])
        onesm = sb("onesm", [P, P])
        epsb = sb("epsb", [P, 1])
        work = sb("work", [P, 8, HD])
        ea = sb("ea", [P, 2, GE])
        hid = sb("hid", [F + 1, 2, GE])
        oh = sb("oh", [P, 2, GT, W])
        flag2 = sb("flag2", [1, 1])
        idx = sb("idx", [P, 2, GT], i32)
        ohf = sb("ohf", [P, N])
        iota_i = ohf[:, :].bitcast(i32)

        def slots(first, count, width):
            return work[:, first:first + count, :].rearrange("p a b -> p (a b)")[:, 0:width]

        dev = slots(0, 2, KC * NC).rearrange("p (k n) -> p k n", k=KC)
        sq = slots(2, 2, KC * NC).rearrange("p (k n) -> p k n", k=KC)
        std, rstd = work[:, 4, 0:NC], work[:, 4, 256:256 + NC]
        stage = [work[:, q, :].rearrange("p (k n) -> p k n", k=KC) for q in range(2)]
        tab = [work[:, 2 + q, :] for q in range(2)]
        hid_abs = [work[0:F, q, :] for q in range(2)]
        hid_pos = [work[0:F, 2 + q, :] for q in range(2)]
        frow = [slots(4 + 2 * q, 2, GT * ROW).rearrange("p (t r) -> p t r", t=GT) for q in range(2)]
        agg2 = sq
        gate = [[work[:, 4 + q, 0:NC], work[:, 4 + q, 256:256 + NC]] for q in range(2)]
        cand = [[work[:, 6 + q, 0:NC], work[:, 6 + q, 256:256 + NC]] for q in range(2)]
        rows = slots(0, 2, GT * ROW).rearrange("p (t r) -> p t r", t=GT)
        feat = work[:, 2, :].rearrange("p (t f) -> p t f", t=GT)
        msg = slots(3, 3, GT * MSG).rearrange("p (t m) -> p t m", t=GT)
        prod = slots(6, 2, GT * 256).rearrange("p (t m) -> p t m", t=GT)
        acc2 = aggT[:, 0:3, :]
        banks = [ctx.enter_context(nc.psum_tensor(f"bank{b}", [P, 512], f32)) for b in range(8)]
        seg = [banks[4 + q][:, 0:KC * W].rearrange("p (k w) -> p k w", k=KC) for q in range(2)]
        seg_deg = [banks[4 + q][0:1, KC * W:(KC + 1) * W] for q in range(2)]

        P_d = nc.dram_tensor("P_d", (N, HD), f32, kind="Internal").ap()
        G_d = nc.dram_tensor("G_d", (N, P), f32, kind="Internal").ap()
        rows_d = nc.dram_tensor("rows_d", (NT * P, ROW), f32, kind="Internal").ap()

        x_loaded, weights_loaded, edges_loaded = sem("x_loaded"), sem("weights_loaded"), sem("edges_loaded")
        zeroed, prep_done, iota_done = sem("zeroed"), sem("prep_done"), sem("iota_done")
        bn_var, bn_std, miss_sum, miss_total, flag_set = (sem(k) for k in ("bn_var", "bn_std", "miss_sum", "miss_total", "flag_set"))
        dve_link = sem("dve_link")
        ln = [{k: sem(f"ln{l}_{k}") for k in ("mean", "dev", "sq", "var", "std", "rstd", "norm", "done")} for l in range(2)]
        tb = [{k: sem(f"tab{l}_{k}") for k in ("stage", "mm", "out", "st0", "st1")} for l in range(2)]
        f_ld = [sem("f_ld0"), sem("f_ld1")]
        f_h, f_abs, f_exp, f_ln, f_pos, f_hid, f_w, f_roww, f_rowy = (sem("f_" + k) for k in ("h", "abs", "exp", "ln", "pos", "hid", "w", "roww", "rowy"))
        f_st = [sem("f_st0"), sem("f_st1")]
        gathered = [sem(f"gathered{k}") for k in range(8)]
        ea_s = [sem("ea_s0"), sem("ea_s1")]
        c_idx, c_e, c_add, c_relu, c_oh, c_seg, c_acc = (sem("c_" + k) for k in ("idx", "e", "add", "relu", "oh", "seg", "acc"))
        l_ld, l_e, l_add, l_relu, l_oh, l_seg, l_acc, l_gat, l_idx = (sem("l_" + k) for k in ("ld", "e", "add", "relu", "oh", "seg", "acc", "gat", "idx"))
        d_mm2, d_agg2, d_rz, d_n, d_sig, d_hn, d_t, d_tanh, d_x1 = (sem("d_" + k) for k in ("mm2", "agg2", "rz", "n", "sig", "hn", "t", "tanh", "x1"))
        m_ld, m_idx, m_gat, m_msg, m_oh, m_seg, m_acc = (sem("m_" + k) for k in ("ld", "idx", "gat", "msg", "oh", "seg", "acc"))
        o_mm1, o_ev, o_abs, o_exp, o_ln, o_pos, o_ssp, o_mm2, o_out = (sem("o_" + k) for k in ("mm1", "ev", "abs", "exp", "ln", "pos", "ssp", "mm2", "out"))
        pool_passed, pe_passed = sem("pool_passed"), sem("pe_passed")
        stored, big_loaded, agg_ready, m_prod = sem("stored"), sem("big_loaded"), sem("agg_ready"), sem("m_prod")
        d_s = [sem(f"d_s{k}") for k in range(4)]
        WL, EL = 21, 7
        LCH, MCH = 5, 3

        block = ctx.enter_context(nc.Block())

        @block.sync
        def _(sp):
            def load(dst, name, done):
                sp.dma_start(dst, a[name]).then_inc(done, 16)

            load(xT[:, :, :], "xT", x_loaded)
            load(w1h[:, :, :], "w1h", weights_loaded)
            load(b_ih[:, :], "b_ih", weights_loaded)
            load(b_hh[:, :], "b_hh", weights_loaded)
            load(w1e[:, :], "w1e", weights_loaded)
            load(fw1[:, :], "fw1", weights_loaded)
            load(fb1[:, :], "fb1", weights_loaded)
            for k, name in enumerate(("gamma", "beta", "run_mean", "run_var")):
                load(bn[:, k, :], name, weights_loaded)
            sp.dma_start(b1_all[:, :], a["b1"].broadcast_to([P, HD])).then_inc(weights_loaded, 16)
            load(b2_row[:, :], "b2", weights_loaded)
            load(w_in[:, 0, :], "w_in_s", weights_loaded)
            load(w_in[:, 1, :], "w_in_v", weights_loaded)
            load(fw2[:, :], "fw2", weights_loaded)
            load(wo1s[:, :], "wo1s", weights_loaded)
            sp.wait_ge(zeroed, 1)
            load(wo1v[0:64, 0, :], "wo1v", weights_loaded)
            load(wo1v[64:128, 1, :], "wo1v", weights_loaded)
            load(wo2[:, 0, :], "wo2s", weights_loaded)
            load(wo2[:, 1, :], "wo2v", weights_loaded)
            load(w2[:, :, :], "w2", weights_loaded)
            for dst, name in ((src0, "src0"), (dst0, "dst0"), (srcm, "srcm"), (dstm, "dstm"), (rcut, "rcut")):
                load(dst[:, :], name, edges_loaded)
            load(y4[:, :, :], "y4", edges_loaded)
            sp.dma_start(base_i[:, :], a["base"].broadcast_to([P, NG])).then_inc(edges_loaded, 16)
            load(wih[:, :, :], "wih", big_loaded)
            load(whh[:, :, :], "whh", big_loaded)

            def store_table(l, dram, width):
                with sp.Fori(0, NTT // 2) as i:
                    for q in range(2):
                        sp.wait_ge(tb[l]["out"], 2 * i + q + 1)
                        sp.dma_start(dram[ds((2 * i + q) * NTL, NTL), :], tab[q][0:NTL, 0:width]).then_inc(tb[l][f"st{q}"], 16)

            store_table(0, P_d, HD)

            def filter_load(i, first):
                for q in range(2):
                    if not first:
                        sp.wait_ge(f_h, 2 * i + q - 1)
                    sp.dma_start(ea[0:R, q, :], a["fT"][:, ds((2 * i + q) * GE, GE)]).then_inc(f_ld[q], 16)

            def filter_store(i):
                for q in range(2):
                    g = 2 * i + q
                    sp.wait_ge(f_roww, g + 2)
                    sp.wait_ge(f_rowy, g + 2)
                    sp.dma_start(rows_d[ds(g * GE, GE), :].rearrange("(t p) r -> p t r", p=P), frow[q]).then_inc(f_st[q], 16)

            filter_load(0, True)
            with sp.Fori(0, NG // 2 - 1) as i:
                filter_load(i + 1, False)
                filter_store(i)
            filter_store(NG // 2 - 1)
            sp.wait_ge(f_h, NG)

            def edge_load(i, first):
                for q in range(2):
                    g = 2 * i + q
                    if not first:
                        sp.wait_ge(c_e, GT * (g - 1))
                    sp.dma_start(ea[:, q, :], a["eaT"][:, ds(g * GE, GE)]).then_inc(ea_s[q], 16)

            edge_load(0, True)
            with sp.Fori(1, NG // 2) as i:
                edge_load(i, False)
            sp.wait_ge(c_e, NT)

            sp.wait_ge(flag_set, 1)
            missed = sp.value_load(flag[0:1, 0:1], min_val=0, max_val=NT * P)
            with sp.If(missed != 0):
                with sp.Fori(0, NT) as t:
                    sp.wait_ge(l_acc, LCH * t + 1)
                    sp.dma_start(ea[:, 0, 0:P], a["eaT"][:, ds(t * P, P)]).then_inc(l_ld, 16)

            store_table(1, G_d, P)
            for q in range(2):
                sp.wait_ge(tb[1][f"st{q}"], 16 * (NTT // 2))
                sp.wait_ge(f_st[q], 16 * (NG // 2))
            with sp.Fori(0, NG) as g:
                sp.wait_ge(m_msg, g + 1)
                sp.dma_start(rows, rows_d[ds(g * GE, GE), :].rearrange("(t p) r -> p t r", p=P)).then_inc(m_ld, 16)
            sp.wait_ge(o_out, NCH)
            sp.dma_start(out, xT[:, :, :]).then_inc(stored, 16)
            sp.wait_ge(stored, 16)

        @block.gpsimd
        def _(gp):
            nc.gpsimd.memset(wo1v[:, :, :], 0.0).then_inc(zeroed, 1)
            nc.gpsimd.iota(iota_i, pattern=[[1, N]], base=0, channel_multiplier=0).then_inc(iota_done, 1)
            gp.wait_ge(edges_loaded, 16 * EL)
            for q in range(2):
                gp.wait_ge(tb[0][f"st{q}"], 16 * (NTT // 2))
                gp.wait_ge(f_st[q], 16 * (NG // 2))

            def gather(i, first):
                for q in range(2):
                    g = 2 * i + q
                    if not first:
                        gp.wait_ge(c_seg, g - 1)
                    nc.gpsimd.tensor_copy(idx[:, q, :], src0[:, ds(g * GT, GT)]).then_inc(c_idx, 1)
                    gp.wait_ge(c_idx, g + 1)
                    gp.sem_inc(pool_passed, 1)
                    for j in range(GT):
                        s = GT * q + j
                        gp.indirect_dma_start(work[:, s, :], None, P_d[:, :],
                                              bass.IndirectOffsetOnAxis(ap=idx[:, q, j:j + 1], axis=0)).then_inc(gathered[s], 16)

            gather(0, True)
            with gp.Fori(1, NG // 2) as i:
                gather(i, False)

            gp.wait_ge(flag_set, 1)
            missed = gp.value_load(flag[0:1, 0:1], min_val=0, max_val=NT * P)
            with gp.If(missed != 0):
                gp.wait_ge(c_seg, NG)
                with gp.Fori(0, NT) as t:
                    gp.wait_ge(l_acc, LCH * t + 1)
                    nc.gpsimd.tensor_copy(idx[:, 0, 0:1], src0[:, ds(t, 1)]).then_inc(l_idx, 1)
                    gp.wait_ge(l_idx, t + 1)
                    gp.sem_inc(pool_passed, 1)
                    gp.indirect_dma_start(work[:, 0, :], None, P_d[:, :],
                                          bass.IndirectOffsetOnAxis(ap=idx[:, 0, 0:1], axis=0)).then_inc(l_gat, 16)

            for q in range(2):
                gp.wait_ge(tb[1][f"st{q}"], 16 * (NTT // 2))
            with gp.Fori(0, NG) as g:
                gp.wait_ge(m_msg, g + 1)
                nc.gpsimd.tensor_copy(idx[:, 0, :], dst0[:, ds(g * GT, GT)]).then_inc(m_idx, 1)
                gp.wait_ge(m_idx, g + 1)
                gp.sem_inc(pool_passed, 1)
                for j in range(GT):
                    gp.indirect_dma_start(feat[:, j, :], None, G_d[:, :],
                                          bass.IndirectOffsetOnAxis(ap=idx[:, 0, j:j + 1], axis=0)).then_inc(m_gat, 16)

        @block.scalar
        def _(act):
            def layer_norm(l):
                with act.Fori(0, NCH) as c:
                    act.wait_ge(ln[l]["dev"], c + 1)
                    nc.scalar.activation(sq, dev, ACT.Square).then_inc(ln[l]["sq"], 1)
                    act.wait_ge(ln[l]["var"], c + 1)
                    nc.scalar.activation(std, banks[1][:, 0:NC], ACT.Sqrt, bias=epsb[:, :]).then_inc(ln[l]["std"], 1)

            def table_stage(l):
                def body(i, first):
                    for q in range(2):
                        if not first:
                            act.wait_ge(tb[l]["mm"], 2 * i + q - 1)
                        nc.scalar.activation(stage[q][:, :, 0:NTL], hT[:, :, ds((2 * i + q) * NTL, NTL)], ACT.Copy).then_inc(tb[l]["stage"], 1)
                act.wait_ge(ln[l]["done"], NCH + 1)
                body(0, True)
                with act.Fori(1, NTT // 2) as i:
                    body(i, False)

            act.wait_ge(prep_done, 1)
            layer_norm(0)
            table_stage(0)
            act.wait_ge(bn_var, 1)
            nc.scalar.activation(bn_scale[:, :], bn_scale[:, :], ACT.Sqrt).then_inc(bn_std, 1)
            act.wait_ge(weights_loaded, 16 * WL)
            act.wait_ge(tb[0]["mm"], NTT)

            def filter_act(i, first):
                for q in range(2):
                    g = 2 * i + q
                    act.wait_ge(f_h, g + 1)
                    if not first:
                        act.wait_ge(f_hid, g - 1)
                    nc.scalar.activation(hid_abs[q], banks[q][0:F, :], ACT.Abs, bias=fb1[:, :]).then_inc(f_abs, 1)
                    act.wait_ge(f_abs, g + 1)
                    nc.scalar.activation(hid_abs[q], hid_abs[q], ACT.Exp, scale=-1.0).then_inc(f_exp, 1)
                    act.wait_ge(f_exp, g + 1)
                    nc.scalar.activation(hid_abs[q], hid_abs[q], ACT.Ln, bias=1.0).then_inc(f_ln, 1)
                    if not first or q:
                        filter_out(i if q else i - 1, 1 - q, first)

            def filter_out(i, q, first):
                act.wait_ge(f_w, 2 * i + q + 1)
                if not first:
                    act.wait_ge(f_st[q], 16 * i)
                nc.scalar.activation(frow[q][:, :, 0:P], banks[2 + q][:, :].rearrange("p (t r) -> p t r", t=GT), ACT.Copy).then_inc(f_roww, 1)

            act.sem_inc(f_roww, 1)
            filter_act(0, True)
            with act.Fori(1, NG // 2) as i:
                filter_act(i, False)
            filter_out(NG // 2 - 1, 1, False)

            with act.Fori(0, NG // 2) as i:
                for q in range(2):
                    for j in range(GT):
                        act.wait_ge(c_add, GT * (2 * i + q) + j + 1)
                        nc.scalar.activation(work[:, GT * q + j, :], work[:, GT * q + j, :], ACT.Relu).then_inc(c_relu, 1)

            act.wait_ge(flag_set, 1)
            missed = act.value_load(flag[0:1, 0:1], min_val=0, max_val=NT * P)
            with act.If(missed != 0):
                with act.Fori(0, NT) as t:
                    act.wait_ge(l_add, t + 1)
                    nc.scalar.activation(work[:, 0, :], work[:, 0, :], ACT.Relu).then_inc(l_relu, 1)

            with act.Fori(0, NCH) as c:
                act.wait_ge(d_mm2, c + 1)
                for j in range(KC):
                    last = nc.scalar.activation(agg2[:, j, :], banks[j][:, 0:NC], ACT.Copy)
                last.then_inc(d_agg2, 1)
                for j in range(KC):
                    q = j % 2
                    act.wait_ge(d_rz, KC * c + j + 1)
                    if j >= 2:
                        act.wait_ge(d_x1, KC * c + j - 1)
                    nc.scalar.activation(gate[q][0], banks[4 + 2 * q][:, 0:NC], ACT.Sigmoid, bias=b_rz[:, j:j + 1])
                    nc.scalar.activation(gate[q][1], banks[4 + 2 * q][:, 256:256 + NC], ACT.Sigmoid,
                                         bias=b_rz[:, KC + j:KC + j + 1]).then_inc(d_sig, 1)
                    act.wait_ge(d_t, KC * c + j + 1)
                    nc.scalar.activation(cand[q][0], cand[q][0], ACT.Tanh, bias=b_ih[:, 2 * KC + j:2 * KC + j + 1]).then_inc(d_tanh, 1)
                act.wait_ge(d_x1, KC * c + KC)

            layer_norm(1)
            table_stage(1)

            with act.Fori(0, NCH) as c:
                act.wait_ge(o_mm1, c + 1)
                nc.scalar.activation(work[:, 0, 0:NC], banks[0][:, 0:NC], ACT.Abs, scale=0.125).then_inc(o_abs, 1)
                act.wait_ge(o_abs, c + 1)
                nc.scalar.activation(work[:, 0, 0:NC], work[:, 0, 0:NC], ACT.Exp, scale=-1.0).then_inc(o_exp, 1)
                act.wait_ge(o_exp, c + 1)
                nc.scalar.activation(work[:, 0, 0:NC], work[:, 0, 0:NC], ACT.Ln, bias=1.0).then_inc(o_ln, 1)
                for k in range(3):
                    last = nc.scalar.activation(work[:, 2 + k, 0:NC], banks[1 + k][:, 0:NC], ACT.Copy, scale=0.125)
                last.then_inc(o_ev, 1)
                act.wait_ge(o_out, c + 1)

        @block.vector
        def _(dve):
            v = nc.vector
            chain = [0]

            def link(ins):
                chain[0] += 1
                ins.then_inc(dve_link, 1)
                dve.wait_ge(dve_link, chain[0])

            v.memset(ones[:, :], 1.0)
            v.memset(onesm[:, :], 1.0 / HD)
            v.memset(aggT[:, :, :], 0.0)
            v.memset(degree[:, :], 0.0)
            v.memset(epsb[:, :], LN_EPS)
            v.memset(hid[F:F + 1, :, :], 1.0)
            link(v.memset(work[:, :, :], 0.0))
            v.memset(idx[:, :, :], 0).then_inc(prep_done, 1)

            def layer_norm(l):
                v.memset(work[:, 4, :], 0.0).then_inc(ln[l]["done"], 1)
                with dve.Fori(0, NCH) as c:
                    dve.wait_ge(ln[l]["mean"], c + 1)
                    v.tensor_tensor(dev, xT[:, :, ds(c * NC, NC)], banks[0][:, 0:NC].unsqueeze(1).broadcast_to([P, KC, NC]),
                                    ALU.subtract).then_inc(ln[l]["dev"], 1)
                    dve.wait_ge(ln[l]["std"], c + 1)
                    v.reciprocal(rstd, std).then_inc(ln[l]["rstd"], 1)
                    dve.wait_ge(ln[l]["rstd"], c + 1)
                    v.tensor_tensor(dev, dev, rstd.unsqueeze(1).broadcast_to([P, KC, NC]), ALU.mult).then_inc(ln[l]["norm"], 1)
                    dve.wait_ge(ln[l]["norm"], c + 1)
                    v.tensor_scalar(hT[:, :, ds(c * NC, NC)], dev, 0.0, None, ALU.max).then_inc(ln[l]["done"], 1)
                dve.wait_ge(ln[l]["done"], NCH + 1)

            dve.wait_ge(x_loaded, 16)
            layer_norm(0)
            dve.wait_ge(weights_loaded, 16 * WL)

            def table_out(l):
                def body(i, first):
                    for q in range(2):
                        dve.wait_ge(tb[l]["mm"], 2 * i + q + 1)
                        if not first:
                            dve.wait_ge(tb[l][f"st{q}"], 16 * i)
                        if l == 0:
                            v.tensor_tensor(tab[q][0:NTL, :], banks[2 + q][0:NTL, :], b1_all[0:NTL, :], ALU.add).then_inc(tb[l]["out"], 1)
                        else:
                            v.tensor_scalar(tab[q][0:NTL, 0:P], banks[2 + q][0:NTL, 0:P], float(P) ** -0.5, None, ALU.mult).then_inc(tb[l]["out"], 1)
                body(0, True)
                with dve.Fori(1, NTT // 2) as i:
                    body(i, False)

            table_out(0)

            dve.wait_ge(edges_loaded, 16 * EL)
            dve.wait_ge(iota_done, 1)
            v.tensor_copy(iota[:, :], iota_i)
            v.tensor_copy(src_f[:, :], srcm[:, :])
            v.tensor_copy(dst_f[:, :], dstm[:, :])
            v.tensor_tensor(y4[:, :, :], y4[:, :, :], rcut[:, :].unsqueeze(2).broadcast_to([P, NT, 4]), ALU.mult)
            link(v.tensor_copy(base_f[:, :], base_i[:, :]))
            link(v.tensor_tensor(rel[:, :].rearrange("p (g t) -> p g t", t=GT), dst_f[:, :].rearrange("p (g t) -> p g t", t=GT),
                                 base_f[:, :].unsqueeze(2).broadcast_to([P, NG, GT]), ALU.subtract))
            v.tensor_scalar(in_win[:, :], rel[:, :], 0.0, None, ALU.is_ge)
            link(v.tensor_scalar(tmp_e[:, :], rel[:, :], float(W), None, ALU.is_lt))
            link(v.tensor_tensor(in_win[:, :], in_win[:, :], tmp_e[:, :], ALU.mult))
            link(v.tensor_scalar(tmp_e[:, :], dst_f[:, :], 0.0, None, ALU.is_ge))
            link(v.tensor_tensor(in_win[:, :], tmp_e[:, :], in_win[:, :], ALU.subtract))
            v.tensor_reduce(n_left[:, :], in_win[:, :], AX.X, ALU.add).then_inc(miss_sum, 1)
            link(v.tensor_scalar(left_key[:, :], dst_f[:, :], 1.0, None, ALU.add))
            link(v.tensor_tensor(left_key[:, :], left_key[:, :], in_win[:, :], ALU.mult))
            link(v.tensor_scalar(left_key[:, :], left_key[:, :], -1.0, None, ALU.add))
            for part in range(1, 4):
                v.tensor_scalar(wo1s[part * F:part * F + F, :], wo1s[part * F:part * F + F, :], 3.0 ** -0.5, None, ALU.mult)
            v.tensor_tensor(b_rz[:, :], b_ih[:, 0:2 * KC], b_hh[:, 0:2 * KC], ALU.add)
            v.tensor_scalar(bn_scale[:, :], bn[:, 3, :], BN_EPS, None, ALU.add).then_inc(bn_var, 1)
            dve.wait_ge(bn_std, 1)
            link(v.reciprocal(bn_shift[:, :], bn_scale[:, :]))
            link(v.tensor_tensor(bn_scale[:, :], bn_shift[:, :], bn[:, 0, :], ALU.mult))
            link(v.tensor_tensor(bn_shift[:, :], bn_scale[:, :], bn[:, 2, :], ALU.mult))
            link(v.tensor_tensor(bn_shift[:, :], bn[:, 1, :], bn_shift[:, :], ALU.subtract))
            dve.wait_ge(miss_total, 1)
            v.tensor_copy(flag[0:1, 0:1], banks[7][0:1, 0:1]).then_inc(flag_set, 1)

            for q in range(2):
                dve.wait_ge(tb[0][f"st{q}"], 16 * (NTT // 2))

            def filter_dve(i, first):
                for q in range(2):
                    g = 2 * i + q
                    dve.wait_ge(f_h, g + 1)
                    if not first:
                        dve.wait_ge(f_w, g - 1)
                    dve.wait_ge(f_abs, g + 1)
                    v.tensor_scalar(hid_pos[q], banks[q][0:F, :], fb1[:, :], 0.0, ALU.add, ALU.max).then_inc(f_pos, 1)
                    dve.wait_ge(f_pos, g + 1)
                    dve.wait_ge(f_ln, g + 1)
                    v.scalar_tensor_tensor(hid[0:F, q, :], hid_pos[q], -LOG2, hid_abs[q], ALU.add, ALU.add).then_inc(f_hid, 1)
                    if not first:
                        dve.wait_ge(f_st[q], 16 * i)
                    v.tensor_copy(frow[q][:, :, P:P + 4], y4[:, ds(g * GT, GT), :]).then_inc(f_rowy, 1)

            dve.sem_inc(f_rowy, 1)
            filter_dve(0, True)
            with dve.Fori(1, NG // 2) as i:
                filter_dve(i, False)

            def edge_dve(i, first):
                for q in range(2):
                    g = 2 * i + q
                    if not first:
                        dve.wait_ge(c_seg, g - 1)
                    v.tensor_tensor(oh[:, q, :, :], iota[:, 0:W].unsqueeze(1).broadcast_to([P, GT, W]),
                                    rel[:, ds(g * GT, GT)].unsqueeze(2).broadcast_to([P, GT, W]), ALU.is_equal).then_inc(c_oh, 1)
                    for j in range(GT):
                        s = GT * q + j
                        dve.wait_ge(gathered[s], 16 * (i + 1))
                        dve.wait_ge(c_e, GT * g + j + 1)
                        v.tensor_tensor(work[:, s, :], work[:, s, :], banks[j][:, :], ALU.add).then_inc(c_add, 1)
                    if q or not first:
                        take_up(g - 1, 1 - q, first)

            def take_up(g, q, first):
                dve.wait_ge(c_seg, g + 1)
                if not first:
                    dve.wait_ge(c_acc, 2 * g + 1)
                base = dve.value_load(base_i[0:1, ds(g, 1)], min_val=0, max_val=N - 1)
                v.tensor_tensor(aggT[:, :, ds(base, W)], aggT[:, :, ds(base, W)], seg[q], ALU.add).then_inc(c_acc, 1)
                v.tensor_tensor(degree[0:1, ds(base, W)], degree[0:1, ds(base, W)], seg_deg[q], ALU.add).then_inc(c_acc, 1)

            dve.sem_inc(c_acc, 1)
            edge_dve(0, True)
            with dve.Fori(1, NG // 2) as i:
                edge_dve(i, False)
            take_up(NG - 1, 1, False)
            dve.wait_ge(c_acc, 2 * NG + 1)

            missed = dve.value_load(flag[0:1, 0:1], min_val=0, max_val=NT * P)
            with dve.If(missed != 0):
                v.memset(epsb[:, :], LN_EPS).then_inc(l_acc, 1)
                with dve.Fori(0, NT) as t:
                    dve.wait_ge(l_acc, LCH * t + 1)
                    v.tensor_scalar(ohf[:, :], iota[:, :], left_key[:, ds(t, 1)], None, ALU.is_equal).then_inc(l_oh, 1)
                    dve.wait_ge(l_gat, 16 * (t + 1))
                    dve.wait_ge(l_e, t + 1)
                    v.tensor_tensor(work[:, 0, :], work[:, 0, :], banks[0][:, :], ALU.add).then_inc(l_add, 1)
                    for k in range(LCH):
                        dve.wait_ge(l_seg, LCH * t + k + 1)
                        for b, (n0, nn) in enumerate(PIECES):
                            if k < KC:
                                last = v.tensor_tensor(aggT[:, k, n0:n0 + nn], aggT[:, k, n0:n0 + nn], banks[1 + b][:, 0:nn], ALU.add)
                            else:
                                last = v.tensor_tensor(degree[0:1, n0:n0 + nn], degree[0:1, n0:n0 + nn], banks[1 + b][0:1, 0:nn], ALU.add)
                        last.then_inc(l_acc, 1)
                dve.wait_ge(l_acc, LCH * NT + 1)
            v.memset(flag2[:, :], 0.0).then_inc(agg_ready, 1)

            with dve.Fori(0, NCH) as c:
                for j in range(KC):
                    q, n = j % 2, KC * c + j
                    x1, h = xT[:, j, ds(c * NC, NC)], hT[:, j, ds(c * NC, NC)]
                    r, z = gate[q]
                    cnd, dif = cand[q]
                    dve.wait_ge(d_sig, n + 1)
                    dve.wait_ge(d_n, n + 1)
                    v.scalar_tensor_tensor(cnd, banks[5 + 2 * q][:, 256:256 + NC], b_hh[:, 2 * KC + j:2 * KC + j + 1], r, ALU.add, ALU.mult).then_inc(d_hn, 1)
                    dve.wait_ge(d_hn, n + 1)
                    v.tensor_tensor(cnd, cnd, banks[5 + 2 * q][:, 0:NC], ALU.add).then_inc(d_t, 1)
                    dve.wait_ge(d_tanh, n + 1)
                    v.tensor_tensor(dif, h, cnd, ALU.subtract).then_inc(d_s[0], 1)
                    dve.wait_ge(d_s[0], n + 1)
                    v.tensor_tensor(dif, dif, z, ALU.mult).then_inc(d_s[1], 1)
                    dve.wait_ge(d_s[1], n + 1)
                    v.tensor_tensor(dif, dif, cnd, ALU.add).then_inc(d_s[2], 1)
                    dve.wait_ge(d_s[2], n + 1)
                    v.scalar_tensor_tensor(dif, dif, bn_scale[:, j:j + 1], x1, ALU.mult, ALU.add).then_inc(d_s[3], 1)
                    dve.wait_ge(d_s[3], n + 1)
                    v.scalar_tensor_tensor(x1, dif, bn_shift[:, j:j + 1], h, ALU.add, ALU.add).then_inc(d_x1, 1)
            dve.wait_ge(d_x1, NCH * KC)

            layer_norm(1)
            link(v.memset(acc2, 0.0))
            table_out(1)
            for q in range(2):
                dve.wait_ge(tb[1][f"st{q}"], 16 * (NTT // 2))

            v.memset(epsb[:, :], LN_EPS).then_inc(m_msg, 1)
            v.memset(n_left[:, :], 0.0).then_inc(m_acc, 1)
            with dve.Fori(0, NG) as g:
                dve.wait_ge(m_ld, 16 * (g + 1))
                dve.wait_ge(m_gat, 16 * GT * (g + 1))
                s = feat[:, :, 0:F]
                vec = feat[:, :, F:P].rearrange("p t (c f) -> p t c f", c=3)
                flt = [rows[:, :, k * F:(k + 1) * F] for k in range(4)]
                ys = rows[:, :, P:P + 1]
                yv = rows[:, :, P + 1:P + 4]
                def over_c(x):
                    return x.unsqueeze(2).broadcast_to([P, GT, 3, F])
                def over_f(x):
                    return x.unsqueeze(3).broadcast_to([P, GT, 3, F])
                m0, m1 = msg[:, :, 0:F], msg[:, :, F:P].rearrange("p t (c f) -> p t c f", c=3)
                mb = msg[:, :, P:MSG].rearrange("p t (c k f) -> p t c k f", c=3, k=2)
                p0, p2 = prod[:, :, 0:F], prod[:, :, F:2 * F]
                p1 = prod[:, :, 2 * F:5 * F].rearrange("p t (c f) -> p t c f", c=3)
                p3 = prod[:, :, 5 * F:8 * F].rearrange("p t (c f) -> p t c f", c=3)
                v.tensor_tensor(p0, s, flt[0], ALU.mult)
                v.tensor_tensor(p2, s, flt[2], ALU.mult)
                for j in range(GT):
                    jv = vec[:, j, :, :]
                    v.tensor_tensor(p1[:, j], jv, flt[1][:, j].unsqueeze(1).broadcast_to([P, 3, F]), ALU.mult)
                    last = v.tensor_tensor(p3[:, j], jv, flt[3][:, j].unsqueeze(1).broadcast_to([P, 3, F]), ALU.mult)
                last.then_inc(m_prod, 1)
                dve.wait_ge(m_prod, g + 1)
                v.tensor_tensor(m0, p0, ys.broadcast_to([P, GT, F]), ALU.mult)
                for j in range(GT):
                    v.tensor_tensor(m1[:, j], p1[:, j], yv[:, j].unsqueeze(2).broadcast_to([P, 3, F]), ALU.mult)
                    v.tensor_tensor(mb[:, j, :, 0], p2[:, j].unsqueeze(1).broadcast_to([P, 3, F]),
                                    yv[:, j].unsqueeze(2).broadcast_to([P, 3, F]), ALU.mult)
                    last = v.tensor_scalar(mb[:, j, :, 1], p3[:, j], ys[:, j], None, ALU.mult)
                last.then_inc(m_msg, 1)
                for j in range(GT):
                    dve.wait_ge(m_acc, MCH * (GT * g + j) + 1)
                    v.tensor_scalar(ohf[:, :], iota[:, :], src_f[:, ds(GT * g + j, 1)], None, ALU.is_equal).then_inc(m_oh, 1)
                    for k in range(MCH):
                        dve.wait_ge(m_seg, MCH * (GT * g + j) + k + 1)
                        rows_k = slice(0, P if k < 2 else MSG - 2 * P)
                        for b, (n0, nn) in enumerate(PIECES):
                            last = v.tensor_tensor(acc2[rows_k, k, n0:n0 + nn], acc2[rows_k, k, n0:n0 + nn], banks[1 + b][rows_k, 0:nn], ALU.add)
                        last.then_inc(m_acc, 1)
            dve.wait_ge(m_acc, MCH * NT + 1)

            with dve.Fori(0, NCH) as c:
                dve.wait_ge(o_abs, c + 1)
                v.tensor_scalar(work[:, 1, 0:NC], banks[0][:, 0:NC], 0.125, 0.0, ALU.mult, ALU.max).then_inc(o_pos, 1)
                dve.wait_ge(o_pos, c + 1)
                dve.wait_ge(o_ln, c + 1)
                v.scalar_tensor_tensor(work[:, 1, 0:NC], work[:, 1, 0:NC], -LOG2, work[:, 0, 0:NC], ALU.add, ALU.add).then_inc(o_ssp, 1)
                dve.wait_ge(o_mm2, c + 1)
                for k in range(KC):
                    xk = xT[:, k, ds(c * NC, NC)]
                    last = v.scalar_tensor_tensor(xk, banks[4 + k][:, 0:NC], float(P) ** -0.5, xk, ALU.mult, ALU.add)
                last.then_inc(o_out, 1)

        @block.tensor
        def _(pe):
            mm = nc.tensor.matmul

            def layer_norm(l):
                with pe.Fori(0, NCH) as c:
                    pe.wait_ge(ln[l]["done"], c + 1)
                    for k in range(KC):
                        last = mm(banks[0][:, 0:NC], onesm[:, :], xT[:, k, ds(c * NC, NC)], start=(k == 0), stop=(k == KC - 1))
                    last.then_inc(ln[l]["mean"], 1)
                    pe.wait_ge(ln[l]["sq"], c + 1)
                    for k in range(KC):
                        last = mm(banks[1][:, 0:NC], onesm[:, :], sq[:, k, :], start=(k == 0), stop=(k == KC - 1))
                    last.then_inc(ln[l]["var"], 1)

            def table_product(l):
                def body(i, first):
                    for q in range(2):
                        pe.wait_ge(tb[l]["stage"], 2 * i + q + 1)
                        if not first:
                            pe.wait_ge(tb[l]["out"], 2 * i + q - 1)
                        if l == 0:
                            for k in range(KC):
                                last = mm(banks[2 + q][0:NTL, :], stage[q][:, k, 0:NTL], w1h[:, k, :], start=(k == 0), stop=(k == KC - 1))
                        else:
                            for k in range(KC):
                                last = mm(banks[2 + q][0:NTL, k * F:(k + 1) * F], stage[q][:, k, 0:NTL], w_in[:, min(k, 1), :], start=True, stop=True)
                        last.then_inc(tb[l]["mm"], 1)
                body(0, True)
                with pe.Fori(1, NTT // 2) as i:
                    body(i, False)

            pe.wait_ge(prep_done, 1)
            pe.wait_ge(x_loaded, 16)
            layer_norm(0)
            pe.wait_ge(weights_loaded, 16 * WL)
            table_product(0)
            pe.wait_ge(miss_sum, 1)
            mm(banks[7][:, 0:1], ones[:, :], n_left[:, :], start=True, stop=True).then_inc(miss_total, 1)

            pe.wait_ge(tb[0]["out"], NTT)

            def filter_pe(i, first):
                for q in range(2):
                    g = 2 * i + q
                    pe.wait_ge(f_ld[q], 16 * (i + 1))
                    if not first:
                        pe.wait_ge(f_hid, g - 1)
                    pe.sem_inc(pe_passed, 1)
                    mm(banks[q][0:F, :], fw1[:, :], ea[0:R, q, :], start=True, stop=True).then_inc(f_h, 1)
                    if q or not first:
                        filter_w(g - 1, 1 - q, first)

            def filter_w(g, q, first):
                pe.wait_ge(f_hid, g + 1)
                if not first:
                    pe.wait_ge(f_roww, g)
                for j in range(GT):
                    last = mm(banks[2 + q][:, j * P:(j + 1) * P], hid[:, q, j * P:(j + 1) * P], fw2[:, :], start=True, stop=True)
                last.then_inc(f_w, 1)

            filter_pe(0, True)
            with pe.Fori(1, NG // 2) as i:
                filter_pe(i, False)
            filter_w(NG - 1, 1, False)
            pe.wait_ge(f_roww, NG + 1)

            def edge_pe(i, first):
                for q in range(2):
                    g = 2 * i + q
                    pe.wait_ge(ea_s[q], 16 * (i + 1))
                    for j in range(GT):
                        if q or not first:
                            pe.wait_ge(c_add, GT * (g - 1) + j + 1)
                        mm(banks[j][:, :], ea[:, q, j * P:(j + 1) * P], w1e[:, :], start=True, stop=True).then_inc(c_e, 1)
                    if q or not first:
                        segment(g - 1, 1 - q, first)

            def segment(g, q, first):
                pe.wait_ge(c_oh, g + 1)
                if not first:
                    pe.wait_ge(c_acc, 2 * (g - 1) + 1)
                for j in range(GT):
                    pe.wait_ge(c_relu, GT * g + j + 1)
                    for k in range(KC):
                        mm(seg[q][:, k, :], work[:, GT * q + j, k * P:(k + 1) * P], oh[:, q, j, :],
                           start=(j == 0 and k == 0), stop=(j == GT - 1), skip_group_check=True)
                    last = mm(seg_deg[q], ones[:, 0:1], oh[:, q, j, :], start=False, stop=(j == GT - 1),
                              skip_group_check=True)
                last.then_inc(c_seg, 1)

            edge_pe(0, True)
            with pe.Fori(1, NG // 2) as i:
                edge_pe(i, False)
            segment(NG - 1, 1, False)

            pe.wait_ge(flag_set, 1)
            missed = pe.value_load(flag[0:1, 0:1], min_val=0, max_val=NT * P)
            with pe.If(missed != 0):
                with pe.Fori(0, NT) as t:
                    pe.wait_ge(l_acc, LCH * t + 1)
                    pe.wait_ge(l_ld, 16 * (t + 1))
                    mm(banks[0][:, :], ea[:, 0, 0:P], w1e[:, :], start=True, stop=True).then_inc(l_e, 1)
                    pe.wait_ge(l_oh, t + 1)
                    pe.wait_ge(l_relu, t + 1)
                    for k in range(LCH):
                        if k:
                            pe.wait_ge(l_acc, LCH * t + k + 1)
                        for b, (n0, nn) in enumerate(PIECES):
                            if k < KC:
                                last = mm(banks[1 + b][:, 0:nn], work[:, 0, k * P:(k + 1) * P], ohf[:, n0:n0 + nn], start=True, stop=True)
                            else:
                                last = mm(banks[1 + b][0:1, 0:nn], ones[:, 0:1], ohf[:, n0:n0 + nn], start=True, stop=True)
                        last.then_inc(l_seg, 1)

            pe.wait_ge(agg_ready, 1)
            pe.wait_ge(big_loaded, 32)
            with pe.Fori(0, NCH) as c:
                cols = ds(c * NC, NC)
                for j in range(KC):
                    for k in range(KC):
                        mm(banks[j][:, 0:NC], w2[:, k, j * P:(j + 1) * P], aggT[:, k, cols], start=(k == 0), stop=False)
                    last = mm(banks[j][:, 0:NC], b2_row[:, j * P:(j + 1) * P], degree[:, cols], start=False, stop=True)
                last.then_inc(d_mm2, 1)
                pe.wait_ge(d_agg2, c + 1)
                for j in range(KC):
                    q, n = j % 2, KC * c + j
                    if j >= 2:
                        pe.wait_ge(d_t, n - 1)
                    for part in range(2):
                        o = banks[4 + 2 * q][:, 256 * part:256 * part + NC]
                        w = slice(part * HD + j * P, part * HD + (j + 1) * P)
                        for k in range(KC):
                            mm(o, wih[:, k, w], agg2[:, k, :], start=(k == 0), stop=False)
                        for k in range(KC):
                            last = mm(o, whh[:, k, w], hT[:, k, cols], start=False, stop=(k == KC - 1))
                    last.then_inc(d_rz, 1)
                    w = slice(2 * HD + j * P, 2 * HD + (j + 1) * P)
                    for k in range(KC):
                        mm(banks[5 + 2 * q][:, 0:NC], wih[:, k, w], agg2[:, k, :], start=(k == 0), stop=(k == KC - 1))
                    for k in range(KC):
                        last = mm(banks[5 + 2 * q][:, 256:256 + NC], whh[:, k, w], hT[:, k, cols], start=(k == 0), stop=(k == KC - 1))
                    last.then_inc(d_n, 1)
                pe.wait_ge(d_t, KC * c + KC)

            pe.wait_ge(d_x1, NCH * KC)
            layer_norm(1)
            table_product(1)
            pe.wait_ge(tb[1]["out"], NTT)

            with pe.Fori(0, NG) as g:
                pe.wait_ge(m_msg, g + 2)
                for j in range(GT):
                    pe.wait_ge(m_oh, GT * g + j + 1)
                    for k in range(MCH):
                        pe.wait_ge(m_acc, MCH * (GT * g + j) + k + 1)
                        width = P if k < 2 else MSG - 2 * P
                        for b, (n0, nn) in enumerate(PIECES):
                            last = mm(banks[1 + b][0:width, 0:nn], msg[:, j, k * P:k * P + width], ohf[:, n0:n0 + nn], start=True, stop=True)
                        last.then_inc(m_seg, 1)
            pe.wait_ge(m_acc, MCH * NT + 1)

            def output(c, first):
                cols = ds(c * NC, NC)
                mm(banks[0][:, 0:NC], wo1s[:, :], acc2[:, 0, cols], start=True, stop=True)
                mm(banks[1][:, 0:NC], wo1v[:, 0, :], acc2[:, 1, cols], start=True, stop=True)
                mm(banks[2][:, 0:NC], wo1v[:, 1, :], acc2[:, 1, cols], start=True, stop=True)
                mm(banks[3][:, 0:NC], wo1v[:, 0, :], acc2[:, 2, cols], start=True, stop=True).then_inc(o_mm1, 1)
                pe.wait_ge(o_ssp, c + 1)
                mm(banks[4][:, 0:NC], wo2[:, 0, :], work[:, 1, 0:NC], start=True, stop=True)
                pe.wait_ge(o_ev, c + 1)
                for k in range(3):
                    last = mm(banks[5 + k][:, 0:NC], wo2[:, 1, :], work[:, 2 + k, 0:NC], start=True, stop=True)
                last.then_inc(o_mm2, 1)
                pe.wait_ge(o_out, c + 1)
            with pe.Fori(0, NCH) as c:
                output(c, False)


def kernel(**inputs):
    import numpy as np
    import concourse.bacc as bacc
    from concourse import mybir as mb
    from concourse.bass_utils import run_bass_kernel_spmd as run

    g = {k: np.asarray(v) for k, v in inputs.items()}

    def perm(w):
        return np.concatenate([w[..., :P], np.moveaxis(w[..., P:].reshape(*w.shape[:-1], P, 3), -1, -2).reshape(*w.shape[:-1], 3 * P)], axis=-1)

    def chunks(w):
        return w.reshape(KC, P, -1).transpose(1, 0, 2)

    def gates(w):
        return np.concatenate([perm(x) for x in np.split(w, 3, axis=-1)], axis=-1)

    def by_edge(v, fill):
        out = np.full((NT * P,) + v.shape[1:], fill, v.dtype)
        out[:NE] = v
        return out

    def tiles(v):
        return np.moveaxis(v.reshape(NT, P, *v.shape[1:]), 1, 0)

    L0 = {k[7:]: v for k, v in g.items() if k.startswith("L0_gnn_")}
    L1 = {k[7:]: v for k, v in g.items() if k.startswith("L1_gnn_")}
    src, dst = g["src"], g["dst"]
    dst_pad = by_edge(dst, 0)
    arrays = {
        "xT": chunks(perm(g["x"]).T),
        "w1h": chunks(perm(L0["W1"][:, :HD]).T), "w1e": L0["W1"][:, HD:].T, "b1": L0["b1"][None],
        "w2": chunks(L0["W2"].T), "b2": L0["b2"][None],
        "wih": chunks(gates(L0["W_ih"].T)), "whh": chunks(gates(perm(L0["W_hh"]).T)),
        "b_ih": gates(L0["b_ih"]).reshape(3 * KC, P).T, "b_hh": gates(L0["b_hh"]).reshape(3 * KC, P).T,
        **{k: perm(L0[k]).reshape(KC, P).T for k in ("gamma", "beta", "run_mean", "run_var")},
        "w_in_s": L1["w_in2f_s"], "w_in_v": L1["w_in2f_v"],
        "fw1": L1["W1"], "fb1": L1["b1"][:, None],
        "fw2": np.concatenate([L1["W2"], L1["b2"][None]]).reshape(F + 1, F, 6).transpose(0, 2, 1)[:, :4].reshape(F + 1, 4 * F),
        "wo1s": np.concatenate([L1["w_f2o1_s"]] + [L1["w_f2o1_s"][F:]] * 2), "wo1v": L1["w_f2o1_v"],
        "wo2s": L1["w_f2o2_s"], "wo2v": L1["w_f2o2_v"],
        "src0": tiles(by_edge(src, 0)), "dst0": tiles(dst_pad),
        "srcm": tiles(by_edge(src, -1)), "dstm": tiles(by_edge(dst, -1)),
        "base": dst_pad[None, ::GE],
        "rcut": tiles(by_edge(g["edge_weight"], 0)), "y4": tiles(by_edge(g["edge_attr_4"], 0)),
        "fT": by_edge(g["edge_attr_20"], 0).T, "eaT": by_edge(g["edge_attr_128"], 0).T,
    }
    nc = bacc.Bacc("TRN2", target_bir_lowering=False, num_devices=1)
    fed, aps = {}, {}
    for name, v in arrays.items():
        v = np.ascontiguousarray(v)
        fed[name + "_in"] = v
        aps[name] = nc.dram_tensor(name + "_in", v.shape, mb.dt.from_np(v.dtype), kind="ExternalInput").ap()
    out = nc.dram_tensor("out_dram", (P, KC, N), mb.dt.float32, kind="ExternalOutput").ap()
    graph_kernel(nc, aps, out)
    r = run(nc, [fed], core_ids=[0])
    y = np.asarray(r.results[0]["out_dram"]).transpose(1, 0, 2).reshape(HD, N).T
    return np.concatenate([y[:, :P], y[:, P:].reshape(N, 3, P).transpose(0, 2, 1).reshape(N, 3 * P)], axis=1)
```

```python
import concourse.bass as bass
from concourse import mybir
from contextlib import ExitStack

P = 128
N, HD, ED = 1250, 512, 128
KC = HD // P
F, R = 32, 20
NE = 41250
GT = 4
GE = GT * P
NG = 2 * (-(-NE // (2 * GE)))
NT = NG * GT
W = 32
NW = N + 2 * W
HI, LO = 40, 32
PAD_KEY = HI * LO - 1
SORT = NT * LO
NC = 250
NCH = N // NC
NTL = 125
NTT = N // NTL
ROW = 136
MSG = 320
LCH, MCH = 5, 3
PIECES = [(0, 417), (417, 417), (834, 416)]
LN_EPS, BN_EPS = 1e-5, 1e-5
LOG2 = 0.6931471805599453


def graph_kernel(nc, a, out):
    f32, i32, bf16 = mybir.dt.float32, mybir.dt.int32, mybir.dt.bfloat16
    ALU, ACT, AX = mybir.AluOpType, mybir.ActivationFunctionType, mybir.AxisListType
    ds = bass.ds

    with ExitStack() as ctx:
        def sb(name, shape, dt=f32):
            return ctx.enter_context(nc.sbuf_tensor(name, shape, dt))

        def sem(name):
            return ctx.enter_context(nc.semaphore(name))

        xT = sb("xT", [P, KC, N])
        hT = sb("hT", [P, KC, N])
        aggT = sb("aggT", [P, KC, NW])
        degree = sb("degree", [1, NW])
        w1h = sb("w1h", [P, KC, HD])
        w1e = sb("w1e", [P, HD])
        b1_all = sb("b1_all", [P, HD])
        w2 = sb("w2", [P, KC, HD])
        b2_row = sb("b2_row", [1, HD])
        big = sb("big", [P, 2 * KC * 3 * HD])
        wih = big[:, 0:KC * 3 * HD].rearrange("p (k n) -> p k n", k=KC)
        whh = big[:, KC * 3 * HD:].rearrange("p (k n) -> p k n", k=KC)
        offsets = big[0:HI, 0:SORT]
        b_ih = sb("b_ih", [P, 3 * KC])
        b_hh = sb("b_hh", [P, 3 * KC])
        b_rz = sb("b_rz", [P, 2 * KC])
        bn = sb("bn", [P, 4, KC])
        bn_scale = sb("bn_scale", [P, KC])
        bn_shift = sb("bn_shift", [P, KC])
        w_in = sb("w_in", [P, 2, F])
        fw1 = sb("fw1", [R, F])
        fb1 = sb("fb1", [F, 1])
        fw2 = sb("fw2", [F + 1, 4 * F])
        wo1s = sb("wo1s", [P, P])
        wo1v = sb("wo1v", [P, 2, P])
        wo2 = sb("wo2", [P, 2, P])
        src0 = sb("src0", [P, NT], i32)
        dst0 = sb("dst0", [P, NT], i32)
        srck = sb("srck", [P, NT], i32)
        high = sb("high", [P, NT])
        low = sb("low", [P, NT])
        place = sb("place", [P, NT], i32)
        dstm = sb("dstm", [P, NT], i32)
        dst_f = sb("dst_f", [P, NT])
        src_f = sb("src_f", [P, NT])
        base_i = sb("base_i", [P, NG], i32)
        base_f = sb("base_f", [P, NG])
        rel = sb("rel", [P, NT])
        left_key = sb("left_key", [P, NT])
        in_win = sb("in_win", [P, NT])
        tmp_e = sb("tmp_e", [P, NT])
        y4 = sb("y4", [P, NT, 4])
        rcut = sb("rcut", [P, NT])
        n_left = sb("n_left", [P, 1])
        flag = sb("flag", [1, 1], i32)
        iota = sb("iota", [P, N])
        ones = sb("ones", [P, P])
        onesm = sb("onesm", [P, P])
        epsb = sb("epsb", [P, 1])
        work = sb("work", [P, 8, HD])
        ea = sb("ea", [P, 2, GE])
        mid = sb("mid", [P, 2, GE])
        hid = mid[0:F + 1, :, :]
        oh_high = sb("oh_high", [P, 2, GT, HI], bf16)
        oh_low = sb("oh_low", [P, 2, GT, LO], bf16)
        rank = sb("rank", [P, 2, GT])
        before = sb("before", [P, 2, GT])
        lows = sb("lows", [P, 2, GT, LO])
        eq = sb("eq", [P, 2, GT, P], bf16)
        lane = sb("lane", [P, 1], i32)
        lane_f = sb("lane_f", [P, 1])
        earlier = sb("earlier", [P, P])
        smaller = sb("smaller", [P, HI])
        ident = sb("ident", [P, P], bf16)
        zero = sb("zero", [P, 1])
        row_total = sb("row_total", [P, 1])
        row_start = sb("row_start", [P, 1])
        base2_f = sb("base2_f", [P, NG])
        first_key = sb("first_key", [1, NG, 2])
        base2_i = sb("base2_i", [P, NG], i32)
        oh = sb("oh", [P, 2, GT, W])
        flag2 = sb("flag2", [1, 1], i32)
        idx = sb("idx", [P, 2, GT], i32)
        ohf = sb("ohf", [P, N])
        iota_i = ohf[:, :].bitcast(i32)

        def slots(first, count, width):
            return work[:, first:first + count, :].rearrange("p a b -> p (a b)")[:, 0:width]

        dev = slots(0, 2, KC * NC).rearrange("p (k n) -> p k n", k=KC)
        sq = slots(2, 2, KC * NC).rearrange("p (k n) -> p k n", k=KC)
        std, rstd = work[:, 4, 0:NC], work[:, 4, 256:256 + NC]
        stage = [work[:, q, :].rearrange("p (k n) -> p k n", k=KC) for q in range(2)]
        tab = [work[:, 2 + q, :] for q in range(2)]
        hid_abs = [work[0:F, q, :] for q in range(2)]
        hid_pos = [work[0:F, 2 + q, :] for q in range(2)]
        frow = [slots(4 + 2 * q, 2, GT * ROW).rearrange("p (t r) -> p t r", t=GT) for q in range(2)]
        agg2 = sq
        gate = [[work[:, 4 + q, 0:NC], work[:, 4 + q, 256:256 + NC]] for q in range(2)]
        cand = [[work[:, 6 + q, 0:NC], work[:, 6 + q, 256:256 + NC]] for q in range(2)]
        key_row = [ea[:, q, :].bitcast(i32) for q in range(2)]
        high_T = [mid[0:HI, q, :] for q in range(2)]
        counts = aggT[:, :, :].rearrange("p k n -> p (k n)").bitcast(bf16)[0:HI, 0:SORT]
        flat = work[:, :, :].rearrange("p a b -> p (a b)")
        rows = [flat[:, q * GT * ROW:(q + 1) * GT * ROW].rearrange("p (t r) -> p t r", t=GT) for q in range(2)]
        msg = [flat[:, 2 * GT * ROW + q * GT * MSG:2 * GT * ROW + (q + 1) * GT * MSG].rearrange("p (t m) -> p t m", t=GT) for q in range(2)]
        feat = [mid[:, q, :].rearrange("p (t f) -> p t f", t=GT) for q in range(2)]
        prod = ea[:, :, :].rearrange("p a b -> p (a b)").rearrange("p (t m) -> p t m", t=GT)
        key2, rel2, left2 = high, low, tmp_e[:, :]
        acc2 = aggT[:, 0:3, :]
        left_msg = msg[0][:, 0, :]
        banks = [ctx.enter_context(nc.psum_tensor(f"bank{b}", [P, 512], f32)) for b in range(8)]
        seg = [banks[4 + q][:, 0:KC * W].rearrange("p (k w) -> p k w", k=KC) for q in range(2)]
        seg2 = [banks[4 + q][:, 0:MCH * W].rearrange("p (k w) -> p k w", k=MCH) for q in range(2)]

        def tr_bank(q):
            return banks[q][:, 0:GE // 2].bitcast(bf16)[0:HI, :]

        idx_tab = tmp_e[:, :].bitcast(i32)
        seg_deg = [banks[4 + q][0:1, KC * W:(KC + 1) * W] for q in range(2)]

        P_d = nc.dram_tensor("P_d", (N, HD), f32, kind="Internal").ap()
        G_d = nc.dram_tensor("G_d", (N, P), f32, kind="Internal").ap()
        rows_d = nc.dram_tensor("rows_d", (NT * P, ROW), f32, kind="Internal").ap()

        x_loaded, weights_loaded, edges_loaded = sem("x_loaded"), sem("weights_loaded"), sem("edges_loaded")
        zeroed, prep_done, iota_done = sem("zeroed"), sem("prep_done"), sem("iota_done")
        bn_var, bn_std, miss_sum, miss_total, flag_set = (sem(k) for k in ("bn_var", "bn_std", "miss_sum", "miss_total", "flag_set"))
        dve_link = sem("dve_link")
        ln = [{k: sem(f"ln{l}_{k}") for k in ("mean", "dev", "sq", "var", "std", "rstd", "norm", "done")} for l in range(2)]
        tb = [{k: sem(f"tab{l}_{k}") for k in ("stage", "mm", "out", "st0", "st1")} for l in range(2)]
        s_oh, s_count, s_hist, s_scan, s_total, s_start, s_off = (sem("s_" + k) for k in ("oh", "count", "hist", "scan", "total", "start", "off"))
        t_key = [sem("t_key0"), sem("t_key1")]
        t_oh, t_tr, t_hT, t_look, t_low, t_place, t_rank = (sem("t_" + k) for k in ("oh", "tr", "hT", "look", "low", "place", "rank"))
        f_idx = sem("f_idx")
        f_ld = [sem("f_ld0"), sem("f_ld1")]
        f_h, f_abs, f_exp, f_ln, f_pos, f_hid, f_w, f_roww, f_rowy = (sem("f_" + k) for k in ("h", "abs", "exp", "ln", "pos", "hid", "w", "roww", "rowy"))
        f_st = [sem("f_st0"), sem("f_st1")]
        gathered = [sem(f"gathered{k}") for k in range(8)]
        ea_s = [sem("ea_s0"), sem("ea_s1")]
        c_idx, c_e, c_add, c_relu, c_oh, c_seg, c_acc = (sem("c_" + k) for k in ("idx", "e", "add", "relu", "oh", "seg", "acc"))
        l_ld, l_e, l_add, l_relu, l_oh, l_seg, l_acc, l_gat, l_idx = (sem("l_" + k) for k in ("ld", "e", "add", "relu", "oh", "seg", "acc", "gat", "idx"))
        d_mm2, d_agg2, d_rz, d_n, d_sig, d_hn, d_t, d_tanh, d_x1 = (sem("d_" + k) for k in ("mm2", "agg2", "rz", "n", "sig", "hn", "t", "tanh", "x1"))
        m_ld, m_gat = [sem("m_ld0"), sem("m_ld1")], [sem("m_gat0"), sem("m_gat1")]
        m_base, m_idx, m_msg, m_rel, m_oh, m_seg, m_acc = (sem("m_" + k) for k in ("base", "idx", "msg", "rel", "oh", "seg", "acc"))
        n_ld, n_idx, n_gat, n_prod, n_msg, n_oh, n_seg, n_acc = (sem("n_" + k) for k in ("ld", "idx", "gat", "prod", "msg", "oh", "seg", "acc"))
        flag2_set, acc2_ready, m_spread = sem("flag2_set"), sem("acc2_ready"), sem("m_spread")
        o_mm1, o_ev, o_abs, o_exp, o_ln, o_pos, o_ssp, o_mm2, o_out = (sem("o_" + k) for k in ("mm1", "ev", "abs", "exp", "ln", "pos", "ssp", "mm2", "out"))
        pool_passed, pe_passed = sem("pool_passed"), sem("pe_passed")
        stored, big_loaded, agg_ready, m_prod = sem("stored"), sem("big_loaded"), sem("agg_ready"), sem("m_prod")
        d_s = [sem(f"d_s{k}") for k in range(4)]
        WL, EL = 21, 7

        block = ctx.enter_context(nc.Block())

        @block.sync
        def _(sp):
            def load(dst, name, done):
                sp.dma_start(dst, a[name]).then_inc(done, 16)

            load(xT[:, :, :], "xT", x_loaded)
            load(w1h[:, :, :], "w1h", weights_loaded)
            load(b_ih[:, :], "b_ih", weights_loaded)
            load(b_hh[:, :], "b_hh", weights_loaded)
            load(w1e[:, :], "w1e", weights_loaded)
            load(fw1[:, :], "fw1", weights_loaded)
            load(fb1[:, :], "fb1", weights_loaded)
            for k, name in enumerate(("gamma", "beta", "run_mean", "run_var")):
                load(bn[:, k, :], name, weights_loaded)
            sp.dma_start(b1_all[:, :], a["b1"].broadcast_to([P, HD])).then_inc(weights_loaded, 16)
            load(b2_row[:, :], "b2", weights_loaded)
            load(w_in[:, 0, :], "w_in_s", weights_loaded)
            load(w_in[:, 1, :], "w_in_v", weights_loaded)
            load(fw2[:, :], "fw2", weights_loaded)
            load(wo1s[:, :], "wo1s", weights_loaded)
            sp.wait_ge(zeroed, 1)
            load(wo1v[0:64, 0, :], "wo1v", weights_loaded)
            load(wo1v[64:128, 1, :], "wo1v", weights_loaded)
            load(wo2[:, 0, :], "wo2s", weights_loaded)
            load(wo2[:, 1, :], "wo2v", weights_loaded)
            load(w2[:, :, :], "w2", weights_loaded)
            for dst, name in ((src0, "src0"), (dst0, "dst0"), (srck, "srck"), (dstm, "dstm"), (rcut, "rcut")):
                load(dst[:, :], name, edges_loaded)
            load(y4[:, :, :], "y4", edges_loaded)
            sp.dma_start(base_i[:, :], a["base"].broadcast_to([P, NG])).then_inc(edges_loaded, 16)
            def store_table(l, dram, width):
                with sp.Fori(0, NTT // 2) as i:
                    for q in range(2):
                        sp.wait_ge(tb[l]["out"], 2 * i + q + 1)
                        sp.dma_start(dram[ds((2 * i + q) * NTL, NTL), :], tab[q][0:NTL, 0:width]).then_inc(tb[l][f"st{q}"], 16)

            store_table(0, P_d, HD)

            def key_load(i, first):
                for q in range(2):
                    if not first:
                        sp.wait_ge(t_rank, 2 * i + q - 1)
                    sp.dma_start(key_row[q], a["keys"][:, ds((2 * i + q) * GE, GE)].broadcast_to([P, GE])).then_inc(t_key[q], 16)

            key_load(0, True)
            with sp.Fori(1, NG // 2) as i:
                key_load(i, False)
            sp.wait_ge(t_place, NG)
            load(wih, "wih", big_loaded)
            load(whh, "whh", big_loaded)

            def filter_load(i, first):
                for q in range(2):
                    if not first:
                        sp.wait_ge(f_h, 2 * i + q - 1)
                    sp.dma_start(ea[0:R, q, :], a["fT"][:, ds((2 * i + q) * GE, GE)]).then_inc(f_ld[q], 16)

            filter_load(0, True)
            with sp.Fori(1, NG // 2) as i:
                filter_load(i, False)
            sp.wait_ge(f_h, NG)

            def edge_load(i, first):
                for q in range(2):
                    g = 2 * i + q
                    if not first:
                        sp.wait_ge(c_e, GT * (g - 1))
                    sp.dma_start(ea[:, q, :], a["eaT"][:, ds(g * GE, GE)]).then_inc(ea_s[q], 16)

            edge_load(0, True)
            with sp.Fori(1, NG // 2) as i:
                edge_load(i, False)
            sp.wait_ge(c_e, NT)

            sp.wait_ge(flag_set, 1)
            missed = sp.value_load(flag[0:1, 0:1], min_val=0, max_val=NT * P)
            with sp.If(missed != 0):
                with sp.Fori(0, NT) as t:
                    sp.wait_ge(l_acc, LCH * t + 1)
                    sp.dma_start(ea[:, 0, 0:P], a["eaT"][:, ds(t * P, P)]).then_inc(l_ld, 16)

            store_table(1, G_d, P)
            for q in range(2):
                sp.wait_ge(f_st[q], 64 * (NG // 2))
            sp.dma_start(first_key[0:1, :, :], rows_d[0:NT * P:GE, P + 4:P + 6].rearrange("(o g) k -> o g k", o=1)).then_inc(m_base, 16)
            for q in range(2):
                sp.wait_ge(tb[1][f"st{q}"], 16 * (NTT // 2))

            def row_load(i, first):
                for q in range(2):
                    g = 2 * i + q
                    if not first:
                        sp.wait_ge(m_msg, g - 1)
                    sp.dma_start(rows[q], rows_d[ds(g * GE, GE), :].rearrange("(t p) r -> p t r", p=P)).then_inc(m_ld[q], 16)

            row_load(0, True)
            with sp.Fori(1, NG // 2) as i:
                row_load(i, False)

            sp.wait_ge(flag2_set, 1)
            missed = sp.value_load(flag2[0:1, 0:1], min_val=0, max_val=NT * P)
            with sp.If(missed != 0):
                with sp.Fori(0, NT) as t:
                    sp.wait_ge(n_acc, MCH * t + 1)
                    sp.dma_start(rows[0][:, 0, :], rows_d[ds(t * P, P), :]).then_inc(n_ld, 16)
            sp.wait_ge(o_out, NCH)
            sp.dma_start(out, xT[:, :, :]).then_inc(stored, 16)
            sp.wait_ge(stored, 16)

        @block.gpsimd
        def _(gp):
            nc.gpsimd.memset(wo1v[:, :, :], 0.0).then_inc(zeroed, 1)
            nc.gpsimd.iota(lane[:, :], pattern=[[0, 1]], base=0, channel_multiplier=1).then_inc(iota_done, 1)
            nc.gpsimd.iota(iota_i, pattern=[[1, N]], base=0, channel_multiplier=0).then_inc(iota_done, 1)
            gp.wait_ge(edges_loaded, 16 * EL)
            def scatter(i):
                for q in range(2):
                    g = 2 * i + q
                    gp.wait_ge(t_place, NG)
                    gp.wait_ge(f_roww, g + 2)
                    gp.wait_ge(f_rowy, g + 2)
                    nc.gpsimd.tensor_copy(idx[:, q, :], place[:, ds(g * GT, GT)]).then_inc(f_idx, 1)
                    gp.wait_ge(f_idx, g + 1)
                    gp.sem_inc(pool_passed, 1)
                    for j in range(GT):
                        gp.indirect_dma_start(rows_d[:, :], bass.IndirectOffsetOnAxis(ap=idx[:, q, j:j + 1], axis=0),
                                              frow[q][:, j, :], None).then_inc(f_st[q], 16)

            with gp.Fori(0, NG // 2) as i:
                scatter(i)

            for q in range(2):
                gp.wait_ge(tb[0][f"st{q}"], 16 * (NTT // 2))
                gp.wait_ge(f_st[q], 64 * (NG // 2))

            def gather(i, first):
                for q in range(2):
                    g = 2 * i + q
                    if not first:
                        gp.wait_ge(c_seg, g - 1)
                    nc.gpsimd.tensor_copy(idx[:, q, :], src0[:, ds(g * GT, GT)]).then_inc(c_idx, 1)
                    gp.wait_ge(c_idx, g + 1)
                    gp.sem_inc(pool_passed, 1)
                    for j in range(GT):
                        s = GT * q + j
                        gp.indirect_dma_start(work[:, s, :], None, P_d[:, :],
                                              bass.IndirectOffsetOnAxis(ap=idx[:, q, j:j + 1], axis=0)).then_inc(gathered[s], 16)

            gather(0, True)
            with gp.Fori(1, NG // 2) as i:
                gather(i, False)

            gp.wait_ge(flag_set, 1)
            missed = gp.value_load(flag[0:1, 0:1], min_val=0, max_val=NT * P)
            with gp.If(missed != 0):
                gp.wait_ge(c_seg, NG)
                with gp.Fori(0, NT) as t:
                    gp.wait_ge(l_acc, LCH * t + 1)
                    nc.gpsimd.tensor_copy(idx[:, 0, 0:1], src0[:, ds(t, 1)]).then_inc(l_idx, 1)
                    gp.wait_ge(l_idx, t + 1)
                    gp.sem_inc(pool_passed, 1)
                    gp.indirect_dma_start(work[:, 0, :], None, P_d[:, :],
                                          bass.IndirectOffsetOnAxis(ap=idx[:, 0, 0:1], axis=0)).then_inc(l_gat, 16)

            for q in range(2):
                gp.wait_ge(tb[1][f"st{q}"], 16 * (NTT // 2))
            def gather2(i, first):
                for q in range(2):
                    g = 2 * i + q
                    if not first:
                        gp.wait_ge(m_msg, g - 1)
                    gp.wait_ge(m_ld[q], 16 * (i + 1))
                    gp.sem_inc(pool_passed, 1)
                    nc.gpsimd.tensor_copy(idx[:, q, :], rows[q][:, :, P + 5]).then_inc(m_idx, 1)
                    gp.wait_ge(m_idx, g + 1)
                    gp.sem_inc(pool_passed, 1)
                    for j in range(GT):
                        gp.indirect_dma_start(feat[q][:, j, :], None, G_d[:, :],
                                              bass.IndirectOffsetOnAxis(ap=idx[:, q, j:j + 1], axis=0)).then_inc(m_gat[q], 16)

            gather2(0, True)
            with gp.Fori(1, NG // 2) as i:
                gather2(i, False)

            gp.wait_ge(flag2_set, 1)
            missed = gp.value_load(flag2[0:1, 0:1], min_val=0, max_val=NT * P)
            with gp.If(missed != 0):
                with gp.Fori(0, NT) as t:
                    gp.wait_ge(n_acc, MCH * t + 1)
                    gp.wait_ge(n_ld, 16 * (t + 1))
                    gp.sem_inc(pool_passed, 1)
                    nc.gpsimd.tensor_copy(idx[:, 0, 0:1], rows[0][:, 0, P + 5:P + 6]).then_inc(n_idx, 1)
                    gp.wait_ge(n_idx, t + 1)
                    gp.sem_inc(pool_passed, 1)
                    gp.indirect_dma_start(feat[0][:, 0, :], None, G_d[:, :],
                                          bass.IndirectOffsetOnAxis(ap=idx[:, 0, 0:1], axis=0)).then_inc(n_gat, 16)

        @block.scalar
        def _(act):
            def layer_norm(l):
                with act.Fori(0, NCH) as c:
                    act.wait_ge(ln[l]["dev"], c + 1)
                    nc.scalar.activation(sq, dev, ACT.Square).then_inc(ln[l]["sq"], 1)
                    act.wait_ge(ln[l]["var"], c + 1)
                    nc.scalar.activation(std, banks[1][:, 0:NC], ACT.Sqrt, bias=epsb[:, :]).then_inc(ln[l]["std"], 1)

            def table_stage(l):
                def body(i, first):
                    for q in range(2):
                        if not first:
                            act.wait_ge(tb[l]["mm"], 2 * i + q - 1)
                        nc.scalar.activation(stage[q][:, :, 0:NTL], hT[:, :, ds((2 * i + q) * NTL, NTL)], ACT.Copy).then_inc(tb[l]["stage"], 1)
                act.wait_ge(ln[l]["done"], NCH + 1)
                body(0, True)
                with act.Fori(1, NTT // 2) as i:
                    body(i, False)

            act.wait_ge(prep_done, 1)
            layer_norm(0)
            table_stage(0)
            act.wait_ge(bn_var, 1)
            nc.scalar.activation(bn_scale[:, :], bn_scale[:, :], ACT.Sqrt).then_inc(bn_std, 1)
            act.wait_ge(weights_loaded, 16 * WL)

            def count_out(i):
                for q in range(2):
                    g = 2 * i + q
                    act.wait_ge(s_count, g + 1)
                    nc.scalar.activation(counts.rearrange("p (l t) -> p l t", l=LO)[:, :, ds(g * GT, GT)],
                                         banks[q][0:HI, 0:GT * LO].rearrange("p (t l) -> p l t", l=LO), ACT.Copy).then_inc(s_hist, 1)

            with act.Fori(0, NG // 2) as i:
                count_out(i)

            def high_out(i, first):
                for q in range(2):
                    g = 2 * i + q
                    act.wait_ge(t_tr, g + 1)
                    if not first:
                        act.wait_ge(t_look, g - 1)
                    nc.scalar.activation(high_T[q], tr_bank(q), ACT.Copy).then_inc(t_hT, 1)

            high_out(0, True)
            with act.Fori(1, NG // 2) as i:
                high_out(i, False)

            def filter_act(i, first):
                for q in range(2):
                    g = 2 * i + q
                    act.wait_ge(f_h, g + 1)
                    if not first:
                        act.wait_ge(f_hid, g - 1)
                    nc.scalar.activation(hid_abs[q], banks[q][0:F, :], ACT.Abs, bias=fb1[:, :]).then_inc(f_abs, 1)
                    act.wait_ge(f_abs, g + 1)
                    nc.scalar.activation(hid_abs[q], hid_abs[q], ACT.Exp, scale=-1.0).then_inc(f_exp, 1)
                    act.wait_ge(f_exp, g + 1)
                    nc.scalar.activation(hid_abs[q], hid_abs[q], ACT.Ln, bias=1.0).then_inc(f_ln, 1)
                    if not first or q:
                        filter_out(i if q else i - 1, 1 - q, first)

            def filter_out(i, q, first):
                act.wait_ge(f_w, 2 * i + q + 1)
                if not first:
                    act.wait_ge(f_st[q], 64 * i)
                nc.scalar.activation(frow[q][:, :, 0:P], banks[2 + q][:, :].rearrange("p (t r) -> p t r", t=GT), ACT.Copy).then_inc(f_roww, 1)

            act.wait_ge(tb[0]["mm"], NTT)
            act.sem_inc(f_roww, 1)
            filter_act(0, True)
            with act.Fori(1, NG // 2) as i:
                filter_act(i, False)
            filter_out(NG // 2 - 1, 1, False)

            with act.Fori(0, NG // 2) as i:
                for q in range(2):
                    for j in range(GT):
                        act.wait_ge(c_add, GT * (2 * i + q) + j + 1)
                        nc.scalar.activation(work[:, GT * q + j, :], work[:, GT * q + j, :], ACT.Relu).then_inc(c_relu, 1)

            act.wait_ge(flag_set, 1)
            missed = act.value_load(flag[0:1, 0:1], min_val=0, max_val=NT * P)
            with act.If(missed != 0):
                with act.Fori(0, NT) as t:
                    act.wait_ge(l_add, t + 1)
                    nc.scalar.activation(work[:, 0, :], work[:, 0, :], ACT.Relu).then_inc(l_relu, 1)

            with act.Fori(0, NCH) as c:
                act.wait_ge(d_mm2, c + 1)
                for j in range(KC):
                    last = nc.scalar.activation(agg2[:, j, :], banks[j][:, 0:NC], ACT.Copy)
                last.then_inc(d_agg2, 1)
                for j in range(KC):
                    q = j % 2
                    act.wait_ge(d_rz, KC * c + j + 1)
                    if j >= 2:
                        act.wait_ge(d_x1, KC * c + j - 1)
                    nc.scalar.activation(gate[q][0], banks[4 + 2 * q][:, 0:NC], ACT.Sigmoid, bias=b_rz[:, j:j + 1])
                    nc.scalar.activation(gate[q][1], banks[4 + 2 * q][:, 256:256 + NC], ACT.Sigmoid,
                                         bias=b_rz[:, KC + j:KC + j + 1]).then_inc(d_sig, 1)
                    act.wait_ge(d_t, KC * c + j + 1)
                    nc.scalar.activation(cand[q][0], cand[q][0], ACT.Tanh, bias=b_ih[:, 2 * KC + j:2 * KC + j + 1]).then_inc(d_tanh, 1)
                act.wait_ge(d_x1, KC * c + KC)

            layer_norm(1)
            table_stage(1)

            with act.Fori(0, NCH) as c:
                act.wait_ge(o_mm1, c + 1)
                nc.scalar.activation(work[:, 0, 0:NC], banks[0][:, 0:NC], ACT.Abs, scale=0.125).then_inc(o_abs, 1)
                act.wait_ge(o_abs, c + 1)
                nc.scalar.activation(work[:, 0, 0:NC], work[:, 0, 0:NC], ACT.Exp, scale=-1.0).then_inc(o_exp, 1)
                act.wait_ge(o_exp, c + 1)
                nc.scalar.activation(work[:, 0, 0:NC], work[:, 0, 0:NC], ACT.Ln, bias=1.0).then_inc(o_ln, 1)
                for k in range(3):
                    last = nc.scalar.activation(work[:, 2 + k, 0:NC], banks[1 + k][:, 0:NC], ACT.Copy, scale=0.125)
                last.then_inc(o_ev, 1)
                act.wait_ge(o_out, c + 1)

        @block.vector
        def _(dve):
            v = nc.vector
            chain = [0]

            def link(ins):
                chain[0] += 1
                ins.then_inc(dve_link, 1)
                dve.wait_ge(dve_link, chain[0])

            v.memset(ones[:, :], 1.0)
            v.memset(onesm[:, :], 1.0 / HD)
            v.memset(zero[:, :], 0.0)
            v.memset(degree[:, :], 0.0)
            v.memset(epsb[:, :], LN_EPS)
            link(v.memset(work[:, :, :], 0.0))
            v.memset(idx[:, :, :], 0).then_inc(prep_done, 1)

            def layer_norm(l):
                v.memset(work[:, 4, :], 0.0).then_inc(ln[l]["done"], 1)
                with dve.Fori(0, NCH) as c:
                    dve.wait_ge(ln[l]["mean"], c + 1)
                    v.tensor_tensor(dev, xT[:, :, ds(c * NC, NC)], banks[0][:, 0:NC].unsqueeze(1).broadcast_to([P, KC, NC]),
                                    ALU.subtract).then_inc(ln[l]["dev"], 1)
                    dve.wait_ge(ln[l]["std"], c + 1)
                    v.reciprocal(rstd, std).then_inc(ln[l]["rstd"], 1)
                    dve.wait_ge(ln[l]["rstd"], c + 1)
                    v.tensor_tensor(dev, dev, rstd.unsqueeze(1).broadcast_to([P, KC, NC]), ALU.mult).then_inc(ln[l]["norm"], 1)
                    dve.wait_ge(ln[l]["norm"], c + 1)
                    v.tensor_scalar(hT[:, :, ds(c * NC, NC)], dev, 0.0, None, ALU.max).then_inc(ln[l]["done"], 1)
                dve.wait_ge(ln[l]["done"], NCH + 1)

            dve.wait_ge(x_loaded, 16)
            layer_norm(0)
            dve.wait_ge(weights_loaded, 16 * WL)

            def table_out(l):
                def body(i, first):
                    for q in range(2):
                        dve.wait_ge(tb[l]["mm"], 2 * i + q + 1)
                        if not first:
                            dve.wait_ge(tb[l][f"st{q}"], 16 * i)
                        if l == 0:
                            v.tensor_tensor(tab[q][0:NTL, :], banks[2 + q][0:NTL, :], b1_all[0:NTL, :], ALU.add).then_inc(tb[l]["out"], 1)
                        else:
                            v.tensor_scalar(tab[q][0:NTL, 0:P], banks[2 + q][0:NTL, 0:P], float(P) ** -0.5, None, ALU.mult).then_inc(tb[l]["out"], 1)
                body(0, True)
                with dve.Fori(1, NTT // 2) as i:
                    body(i, False)

            table_out(0)

            dve.wait_ge(edges_loaded, 16 * EL)
            dve.wait_ge(iota_done, 2)
            v.tensor_copy(iota[:, :], iota_i)
            v.tensor_copy(src_f[:, :], srck[:, :])
            v.tensor_copy(lane_f[:, :], lane[:, :])
            v.tensor_scalar(place[:, :], srck[:, :], 5, None, ALU.arith_shift_right)
            link(v.tensor_scalar(idx_tab, srck[:, :], LO - 1, None, ALU.bitwise_and))
            v.tensor_copy(high[:, :], place[:, :])
            link(v.tensor_copy(low[:, :], idx_tab))
            v.tensor_copy(dst_f[:, :], dstm[:, :])
            v.tensor_tensor(y4[:, :, :], y4[:, :, :], rcut[:, :].unsqueeze(2).broadcast_to([P, NT, 4]), ALU.mult)
            link(v.tensor_copy(base_f[:, :], base_i[:, :]))
            link(v.tensor_tensor(rel[:, :].rearrange("p (g t) -> p g t", t=GT), dst_f[:, :].rearrange("p (g t) -> p g t", t=GT),
                                 base_f[:, :].unsqueeze(2).broadcast_to([P, NG, GT]), ALU.subtract))
            v.tensor_scalar(in_win[:, :], rel[:, :], 0.0, None, ALU.is_ge)
            link(v.tensor_scalar(tmp_e[:, :], rel[:, :], float(W), None, ALU.is_lt))
            link(v.tensor_tensor(in_win[:, :], in_win[:, :], tmp_e[:, :], ALU.mult))
            link(v.tensor_scalar(tmp_e[:, :], dst_f[:, :], 0.0, None, ALU.is_ge))
            link(v.tensor_tensor(in_win[:, :], tmp_e[:, :], in_win[:, :], ALU.subtract))
            v.tensor_reduce(n_left[:, :], in_win[:, :], AX.X, ALU.add).then_inc(miss_sum, 1)
            link(v.tensor_scalar(left_key[:, :], dst_f[:, :], 1.0, None, ALU.add))
            link(v.tensor_tensor(left_key[:, :], left_key[:, :], in_win[:, :], ALU.mult))
            link(v.tensor_scalar(left_key[:, :], left_key[:, :], -1.0, None, ALU.add))
            for part in range(1, 4):
                v.tensor_scalar(wo1s[part * F:part * F + F, :], wo1s[part * F:part * F + F, :], 3.0 ** -0.5, None, ALU.mult)
            v.tensor_tensor(b_rz[:, :], b_ih[:, 0:2 * KC], b_hh[:, 0:2 * KC], ALU.add)
            v.tensor_scalar(bn_scale[:, :], bn[:, 3, :], BN_EPS, None, ALU.add).then_inc(bn_var, 1)
            dve.wait_ge(bn_std, 1)
            link(v.reciprocal(bn_shift[:, :], bn_scale[:, :]))
            link(v.tensor_tensor(bn_scale[:, :], bn_shift[:, :], bn[:, 0, :], ALU.mult))
            link(v.tensor_tensor(bn_shift[:, :], bn_scale[:, :], bn[:, 2, :], ALU.mult))
            link(v.tensor_tensor(bn_shift[:, :], bn[:, 1, :], bn_shift[:, :], ALU.subtract))
            dve.wait_ge(miss_total, 1)
            v.tensor_copy(flag[0:1, 0:1], banks[7][0:1, 0:1]).then_inc(flag_set, 1)

            v.tensor_scalar(earlier[:, :], iota[:, 0:P], lane_f[:, :], None, ALU.is_lt)
            v.tensor_scalar(smaller[:, :], iota[:, 0:HI], lane_f[:, :], None, ALU.is_gt)
            link(v.tensor_scalar(ident[:, :], iota[:, 0:P], lane_f[:, :], None, ALU.is_equal))

            def one_hots(g, q, done):
                v.tensor_tensor(oh_high[:, q, :, :], iota[:, 0:HI].unsqueeze(1).broadcast_to([P, GT, HI]),
                                high[:, ds(g * GT, GT)].unsqueeze(2).broadcast_to([P, GT, HI]), ALU.is_equal)
                v.tensor_tensor(oh_low[:, q, :, :], iota[:, 0:LO].unsqueeze(1).broadcast_to([P, GT, LO]),
                                low[:, ds(g * GT, GT)].unsqueeze(2).broadcast_to([P, GT, LO]), ALU.is_equal).then_inc(done, 1)

            def digits(i, first):
                for q in range(2):
                    g = 2 * i + q
                    if not first:
                        dve.wait_ge(s_count, g - 1)
                    one_hots(g, q, s_oh)

            digits(0, True)
            with dve.Fori(1, NG // 2) as i:
                digits(i, False)

            dve.wait_ge(s_hist, NG)
            v.tensor_tensor_scan(offsets, counts, zero[0:HI, :].broadcast_to([HI, SORT]), 0.0, ALU.add, ALU.add).then_inc(s_scan, 1)
            dve.wait_ge(s_scan, 1)
            v.tensor_copy(row_total[0:HI, :], offsets[:, SORT - 1:SORT]).then_inc(s_total, 1)
            dve.wait_ge(s_start, 1)
            link(v.tensor_copy(row_start[0:HI, :], banks[7][0:HI, 0:1]))
            v.scalar_tensor_tensor(offsets, offsets, row_start[0:HI, :], counts, ALU.add, ALU.subtract).then_inc(s_off, 1)

            def places(i, first):
                for q in range(2):
                    g = 2 * i + q
                    if not first:
                        dve.wait_ge(t_tr, g - 1)
                    one_hots(g, q, t_oh)
                    dve.wait_ge(t_key[q], 16 * (i + 1))
                    if not first:
                        dve.wait_ge(t_place, g - 1)
                    for j in range(GT):
                        last = v.scalar_tensor_tensor(eq[:, q, j, :], key_row[q][:, j * P:(j + 1) * P], src_f[:, ds(g * GT + j, 1)],
                                                      earlier[:, :], ALU.is_equal, ALU.mult, accum_out=rank[:, q, j:j + 1])
                    last.then_inc(t_rank, 1)
                    if q or not first:
                        settle(g - 1, 1 - q)

            def settle(g, q):
                dve.wait_ge(t_look, g + 1)
                v.tensor_tensor(lows[:, q, :, :], banks[2 + q][:, 0:GT * LO].rearrange("p (t l) -> p t l", l=LO),
                                oh_low[:, q, :, :], ALU.mult).then_inc(t_low, 1)
                dve.wait_ge(t_low, 2 * g + 1)
                v.tensor_reduce(before[:, q, :], lows[:, q, :, :], AX.X, ALU.add).then_inc(t_low, 1)
                dve.wait_ge(t_low, 2 * g + 2)
                v.tensor_tensor(place[:, ds(g * GT, GT)], before[:, q, :], rank[:, q, :], ALU.add).then_inc(t_place, 1)

            places(0, True)
            with dve.Fori(1, NG // 2) as i:
                places(i, False)
            settle(NG - 1, 1)
            dve.wait_ge(t_place, NG)
            v.memset(hid[F:F + 1, :, :], 1.0)
            v.memset(aggT[:, :, :], 0.0)

            for q in range(2):
                dve.wait_ge(tb[0][f"st{q}"], 16 * (NTT // 2))

            def filter_dve(i, first):
                for q in range(2):
                    g = 2 * i + q
                    dve.wait_ge(f_h, g + 1)
                    if not first:
                        dve.wait_ge(f_w, g - 1)
                    dve.wait_ge(f_abs, g + 1)
                    v.tensor_scalar(hid_pos[q], banks[q][0:F, :], fb1[:, :], 0.0, ALU.add, ALU.max).then_inc(f_pos, 1)
                    dve.wait_ge(f_pos, g + 1)
                    dve.wait_ge(f_ln, g + 1)
                    v.scalar_tensor_tensor(hid[0:F, q, :], hid_pos[q], -LOG2, hid_abs[q], ALU.add, ALU.add).then_inc(f_hid, 1)
                    if not first:
                        dve.wait_ge(f_st[q], 64 * i)
                    v.tensor_copy(frow[q][:, :, P:P + 4], y4[:, ds(g * GT, GT), :])
                    v.tensor_copy(frow[q][:, :, P + 4], src_f[:, ds(g * GT, GT)])
                    v.tensor_copy(frow[q][:, :, P + 5], dst0[:, ds(g * GT, GT)]).then_inc(f_rowy, 1)

            dve.sem_inc(f_rowy, 1)
            filter_dve(0, True)
            with dve.Fori(1, NG // 2) as i:
                filter_dve(i, False)

            def edge_dve(i, first):
                for q in range(2):
                    g = 2 * i + q
                    if not first:
                        dve.wait_ge(c_seg, g - 1)
                    v.tensor_tensor(oh[:, q, :, :], iota[:, 0:W].unsqueeze(1).broadcast_to([P, GT, W]),
                                    rel[:, ds(g * GT, GT)].unsqueeze(2).broadcast_to([P, GT, W]), ALU.is_equal).then_inc(c_oh, 1)
                    for j in range(GT):
                        s = GT * q + j
                        dve.wait_ge(gathered[s], 16 * (i + 1))
                        dve.wait_ge(c_e, GT * g + j + 1)
                        v.tensor_tensor(work[:, s, :], work[:, s, :], banks[j][:, :], ALU.add).then_inc(c_add, 1)
                    if q or not first:
                        take_up(g - 1, 1 - q, first)

            def take_up(g, q, first):
                dve.wait_ge(c_seg, g + 1)
                if not first:
                    dve.wait_ge(c_acc, 2 * g + 1)
                base = dve.value_load(base_i[0:1, ds(g, 1)], min_val=0, max_val=N - 1)
                v.tensor_tensor(aggT[:, :, ds(base, W)], aggT[:, :, ds(base, W)], seg[q], ALU.add).then_inc(c_acc, 1)
                v.tensor_tensor(degree[0:1, ds(base, W)], degree[0:1, ds(base, W)], seg_deg[q], ALU.add).then_inc(c_acc, 1)

            dve.sem_inc(c_acc, 1)
            edge_dve(0, True)
            with dve.Fori(1, NG // 2) as i:
                edge_dve(i, False)
            take_up(NG - 1, 1, False)
            dve.wait_ge(c_acc, 2 * NG + 1)

            missed = dve.value_load(flag[0:1, 0:1], min_val=0, max_val=NT * P)
            with dve.If(missed != 0):
                v.memset(epsb[:, :], LN_EPS).then_inc(l_acc, 1)
                with dve.Fori(0, NT) as t:
                    dve.wait_ge(l_acc, LCH * t + 1)
                    v.tensor_scalar(ohf[:, :], iota[:, :], left_key[:, ds(t, 1)], None, ALU.is_equal).then_inc(l_oh, 1)
                    dve.wait_ge(l_gat, 16 * (t + 1))
                    dve.wait_ge(l_e, t + 1)
                    v.tensor_tensor(work[:, 0, :], work[:, 0, :], banks[0][:, :], ALU.add).then_inc(l_add, 1)
                    for k in range(LCH):
                        dve.wait_ge(l_seg, LCH * t + k + 1)
                        for b, (n0, nn) in enumerate(PIECES):
                            if k < KC:
                                last = v.tensor_tensor(aggT[:, k, n0:n0 + nn], aggT[:, k, n0:n0 + nn], banks[1 + b][:, 0:nn], ALU.add)
                            else:
                                last = v.tensor_tensor(degree[0:1, n0:n0 + nn], degree[0:1, n0:n0 + nn], banks[1 + b][0:1, 0:nn], ALU.add)
                        last.then_inc(l_acc, 1)
                dve.wait_ge(l_acc, LCH * NT + 1)
            v.memset(zero[:, :], 0.0).then_inc(agg_ready, 1)

            with dve.Fori(0, NCH) as c:
                for j in range(KC):
                    q, n = j % 2, KC * c + j
                    x1, h = xT[:, j, ds(c * NC, NC)], hT[:, j, ds(c * NC, NC)]
                    r, z = gate[q]
                    cnd, dif = cand[q]
                    dve.wait_ge(d_sig, n + 1)
                    dve.wait_ge(d_n, n + 1)
                    v.scalar_tensor_tensor(cnd, banks[5 + 2 * q][:, 256:256 + NC], b_hh[:, 2 * KC + j:2 * KC + j + 1], r, ALU.add, ALU.mult).then_inc(d_hn, 1)
                    dve.wait_ge(d_hn, n + 1)
                    v.tensor_tensor(cnd, cnd, banks[5 + 2 * q][:, 0:NC], ALU.add).then_inc(d_t, 1)
                    dve.wait_ge(d_tanh, n + 1)
                    v.tensor_tensor(dif, h, cnd, ALU.subtract).then_inc(d_s[0], 1)
                    dve.wait_ge(d_s[0], n + 1)
                    v.tensor_tensor(dif, dif, z, ALU.mult).then_inc(d_s[1], 1)
                    dve.wait_ge(d_s[1], n + 1)
                    v.tensor_tensor(dif, dif, cnd, ALU.add).then_inc(d_s[2], 1)
                    dve.wait_ge(d_s[2], n + 1)
                    v.scalar_tensor_tensor(dif, dif, bn_scale[:, j:j + 1], x1, ALU.mult, ALU.add).then_inc(d_s[3], 1)
                    dve.wait_ge(d_s[3], n + 1)
                    v.scalar_tensor_tensor(x1, dif, bn_shift[:, j:j + 1], h, ALU.add, ALU.add).then_inc(d_x1, 1)
            dve.wait_ge(d_x1, NCH * KC)

            layer_norm(1)
            link(v.memset(acc2, 0.0))
            table_out(1)
            for q in range(2):
                dve.wait_ge(tb[1][f"st{q}"], 16 * (NTT // 2))

            dve.wait_ge(m_spread, 1)
            link(v.tensor_scalar(base2_f[:, :], banks[7][:, 0:NG], float(N - 1), None, ALU.min))
            link(v.tensor_copy(base2_i[:, :], base2_f[:, :]))

            def messages(row, ft, m, pr, t, prod_sem, prod_n, done):
                def over_c(x):
                    return x.unsqueeze(2).broadcast_to([P, t, 3, F])

                def over_f(x):
                    return x.unsqueeze(3).broadcast_to([P, t, 3, F])

                def by_c(x):
                    return x.rearrange("p t (c f) -> p t c f", c=3)

                s, vec = ft[:, :, 0:F], by_c(ft[:, :, F:P])
                flt = [row[:, :, k * F:(k + 1) * F] for k in range(4)]
                ys, yv = row[:, :, P:P + 1], row[:, :, P + 1:P + 4]
                mb = m[:, :, P:MSG].rearrange("p t (c k f) -> p t c k f", c=3, k=2)
                p0, p2, p1, p3 = pr[:, :, 0:F], pr[:, :, F:2 * F], by_c(pr[:, :, 2 * F:5 * F]), by_c(pr[:, :, 5 * F:8 * F])
                v.tensor_tensor(p0, s, flt[0], ALU.mult)
                v.tensor_tensor(p2, s, flt[2], ALU.mult)
                v.tensor_tensor(p1, vec, over_c(flt[1]), ALU.mult)
                v.tensor_tensor(p3, vec, over_c(flt[3]), ALU.mult).then_inc(prod_sem, 1)
                dve.wait_ge(prod_sem, prod_n)
                v.tensor_tensor(m[:, :, 0:F], p0, ys.broadcast_to([P, t, F]), ALU.mult)
                v.tensor_tensor(by_c(m[:, :, F:P]), p1, over_f(yv), ALU.mult)
                v.tensor_tensor(mb[:, :, :, 0], over_c(p2), over_f(yv), ALU.mult)
                v.tensor_tensor(mb[:, :, :, 1], p3, ys.unsqueeze(3).broadcast_to([P, t, 3, F]), ALU.mult).then_inc(done, 1)

            def message_dve(i, first):
                for q in range(2):
                    g = 2 * i + q
                    dve.wait_ge(m_ld[q], 16 * (i + 1))
                    dve.wait_ge(m_gat[q], 64 * (i + 1))
                    if not first:
                        dve.wait_ge(m_seg, g - 1)
                    if q or not first:
                        dve.wait_ge(m_msg, g)
                    v.tensor_copy(key2[:, ds(g * GT, GT)], rows[q][:, :, P + 4])
                    v.tensor_scalar(rel2[:, ds(g * GT, GT)], rows[q][:, :, P + 4], base2_f[:, ds(g, 1)], None, ALU.subtract).then_inc(m_rel, 1)
                    messages(rows[q], feat[q], msg[q], prod, GT, m_prod, g + 1, m_msg)
                    dve.wait_ge(m_rel, g + 1)
                    v.tensor_tensor(oh[:, q, :, :], iota[:, 0:W].unsqueeze(1).broadcast_to([P, GT, W]),
                                    rel2[:, ds(g * GT, GT)].unsqueeze(2).broadcast_to([P, GT, W]), ALU.is_equal).then_inc(m_oh, 1)
                    if q or not first:
                        take_up2(g - 1, 1 - q)

            def take_up2(g, q):
                dve.wait_ge(m_seg, g + 1)
                dve.wait_ge(m_acc, g + 1)
                base = dve.value_load(base2_i[0:1, ds(g, 1)], min_val=0, max_val=N - 1)
                v.tensor_tensor(acc2[:, :, ds(base, W)], acc2[:, :, ds(base, W)], seg2[q], ALU.add).then_inc(m_acc, 1)

            dve.sem_inc(m_acc, 1)
            message_dve(0, True)
            with dve.Fori(1, NG // 2) as i:
                message_dve(i, False)
            take_up2(NG - 1, 1)
            dve.wait_ge(m_acc, NG + 1)

            v.tensor_scalar(in_win[:, :], rel2[:, :], float(W), None, ALU.is_ge)
            link(v.tensor_scalar(left2[:, :], key2[:, :], float(N), None, ALU.is_lt))
            link(v.tensor_tensor(in_win[:, :], in_win[:, :], left2[:, :], ALU.mult))
            v.tensor_reduce(n_left[:, :], in_win[:, :], AX.X, ALU.add).then_inc(miss_sum, 1)
            link(v.tensor_scalar(left2[:, :], key2[:, :], 1.0, None, ALU.add))
            link(v.tensor_tensor(left2[:, :], left2[:, :], in_win[:, :], ALU.mult))
            link(v.tensor_scalar(left2[:, :], left2[:, :], -1.0, None, ALU.add))
            dve.wait_ge(miss_total, 2)
            v.tensor_copy(flag2[0:1, 0:1], banks[7][0:1, 0:1]).then_inc(flag2_set, 1)
            dve.wait_ge(flag2_set, 1)
            missed = dve.value_load(flag2[0:1, 0:1], min_val=0, max_val=NT * P)
            with dve.If(missed != 0):
                dve.sem_inc(n_acc, 1)
                with dve.Fori(0, NT) as t:
                    dve.wait_ge(n_gat, 16 * (t + 1))
                    dve.wait_ge(n_acc, MCH * t + 1)
                    messages(rows[0][:, 0:1, :], feat[0][:, 0:1, :], msg[0][:, 0:1, :], prod[:, 0:1, :], 1, n_prod, t + 1, n_msg)
                    v.tensor_scalar(ohf[:, :], iota[:, :], left2[:, ds(t, 1)], None, ALU.is_equal).then_inc(n_oh, 1)
                    for k in range(MCH):
                        dve.wait_ge(n_seg, MCH * t + k + 1)
                        rows_k = slice(0, P if k < 2 else MSG - 2 * P)
                        for b, (n0, nn) in enumerate(PIECES):
                            last = v.tensor_tensor(acc2[rows_k, k, n0:n0 + nn], acc2[rows_k, k, n0:n0 + nn], banks[1 + b][rows_k, 0:nn], ALU.add)
                        last.then_inc(n_acc, 1)
                dve.wait_ge(n_acc, MCH * NT + 1)
            v.memset(zero[:, :], 0.0).then_inc(acc2_ready, 1)

            with dve.Fori(0, NCH) as c:
                dve.wait_ge(o_abs, c + 1)
                v.tensor_scalar(work[:, 1, 0:NC], banks[0][:, 0:NC], 0.125, 0.0, ALU.mult, ALU.max).then_inc(o_pos, 1)
                dve.wait_ge(o_pos, c + 1)
                dve.wait_ge(o_ln, c + 1)
                v.scalar_tensor_tensor(work[:, 1, 0:NC], work[:, 1, 0:NC], -LOG2, work[:, 0, 0:NC], ALU.add, ALU.add).then_inc(o_ssp, 1)
                dve.wait_ge(o_mm2, c + 1)
                for k in range(KC):
                    xk = xT[:, k, ds(c * NC, NC)]
                    last = v.scalar_tensor_tensor(xk, banks[4 + k][:, 0:NC], float(P) ** -0.5, xk, ALU.mult, ALU.add)
                last.then_inc(o_out, 1)

        @block.tensor
        def _(pe):
            mm = nc.tensor.matmul

            def layer_norm(l):
                with pe.Fori(0, NCH) as c:
                    pe.wait_ge(ln[l]["done"], c + 1)
                    for k in range(KC):
                        last = mm(banks[0][:, 0:NC], onesm[:, :], xT[:, k, ds(c * NC, NC)], start=(k == 0), stop=(k == KC - 1))
                    last.then_inc(ln[l]["mean"], 1)
                    pe.wait_ge(ln[l]["sq"], c + 1)
                    for k in range(KC):
                        last = mm(banks[1][:, 0:NC], onesm[:, :], sq[:, k, :], start=(k == 0), stop=(k == KC - 1))
                    last.then_inc(ln[l]["var"], 1)

            def table_product(l):
                def body(i, first):
                    for q in range(2):
                        pe.wait_ge(tb[l]["stage"], 2 * i + q + 1)
                        if not first:
                            pe.wait_ge(tb[l]["out"], 2 * i + q - 1)
                        if l == 0:
                            for k in range(KC):
                                last = mm(banks[2 + q][0:NTL, :], stage[q][:, k, 0:NTL], w1h[:, k, :], start=(k == 0), stop=(k == KC - 1))
                        else:
                            for k in range(KC):
                                last = mm(banks[2 + q][0:NTL, k * F:(k + 1) * F], stage[q][:, k, 0:NTL], w_in[:, min(k, 1), :], start=True, stop=True)
                        last.then_inc(tb[l]["mm"], 1)
                body(0, True)
                with pe.Fori(1, NTT // 2) as i:
                    body(i, False)

            pe.wait_ge(prep_done, 1)
            pe.wait_ge(x_loaded, 16)
            layer_norm(0)
            pe.wait_ge(weights_loaded, 16 * WL)
            table_product(0)
            pe.wait_ge(miss_sum, 1)
            mm(banks[7][:, 0:1], ones[:, :], n_left[:, :], start=True, stop=True).then_inc(miss_total, 1)

            def count_pe(i, first):
                for q in range(2):
                    g = 2 * i + q
                    pe.wait_ge(s_oh, g + 1)
                    if not first:
                        pe.wait_ge(s_hist, g - 1)
                    for j in range(GT):
                        last = mm(banks[q][0:HI, j * LO:(j + 1) * LO], oh_high[:, q, j, :], oh_low[:, q, j, :], start=True, stop=True)
                    last.then_inc(s_count, 1)

            count_pe(0, True)
            with pe.Fori(1, NG // 2) as i:
                count_pe(i, False)
            pe.wait_ge(s_total, 1)
            mm(banks[7][0:HI, 0:1], smaller[0:HI, :], row_total[0:HI, :], start=True, stop=True).then_inc(s_start, 1)
            pe.wait_ge(s_off, 1)
            pe.wait_ge(tb[0]["out"], NTT)
            pe.wait_ge(s_hist, NG)

            def high_pe(i, first):
                for q in range(2):
                    g = 2 * i + q
                    pe.wait_ge(t_oh, g + 1)
                    if not first:
                        pe.wait_ge(t_hT, g - 1)
                    pe.sem_inc(pe_passed, 1)
                    for j in range(GT):
                        last = nc.tensor.transpose(tr_bank(q)[:, j * P:(j + 1) * P], oh_high[:, q, j, :], ident[:, :])
                    last.then_inc(t_tr, 1)
                    if q or not first:
                        look(g - 1, 1 - q, first)

            def look(g, q, first):
                pe.wait_ge(t_hT, g + 1)
                if not first:
                    pe.wait_ge(t_low, 2 * (g - 2) + 2)
                pe.sem_inc(pe_passed, 1)
                for j in range(GT):
                    last = mm(banks[2 + q][:, j * LO:(j + 1) * LO], high_T[q][:, j * P:(j + 1) * P],
                              offsets.rearrange("p (l t) -> p l t", l=LO)[:, :, ds(g * GT + j, 1)].rearrange("p l t -> p (l t)"), start=True, stop=True)
                last.then_inc(t_look, 1)

            high_pe(0, True)
            with pe.Fori(1, NG // 2) as i:
                high_pe(i, False)
            look(NG - 1, 1, False)

            pe.wait_ge(t_hT, NG)
            pe.wait_ge(t_place, NG)

            def filter_pe(i, first):
                for q in range(2):
                    g = 2 * i + q
                    pe.wait_ge(f_ld[q], 16 * (i + 1))
                    if not first:
                        pe.wait_ge(f_hid, g - 1)
                    pe.sem_inc(pe_passed, 1)
                    mm(banks[q][0:F, :], fw1[:, :], ea[0:R, q, :], start=True, stop=True).then_inc(f_h, 1)
                    if q or not first:
                        filter_w(g - 1, 1 - q, first)

            def filter_w(g, q, first):
                pe.wait_ge(f_hid, g + 1)
                if not first:
                    pe.wait_ge(f_roww, g)
                for j in range(GT):
                    last = mm(banks[2 + q][:, j * P:(j + 1) * P], hid[:, q, j * P:(j + 1) * P], fw2[:, :], start=True, stop=True)
                last.then_inc(f_w, 1)

            filter_pe(0, True)
            with pe.Fori(1, NG // 2) as i:
                filter_pe(i, False)
            filter_w(NG - 1, 1, False)
            pe.wait_ge(f_roww, NG + 1)

            def edge_pe(i, first):
                for q in range(2):
                    g = 2 * i + q
                    pe.wait_ge(ea_s[q], 16 * (i + 1))
                    for j in range(GT):
                        if q or not first:
                            pe.wait_ge(c_add, GT * (g - 1) + j + 1)
                        mm(banks[j][:, :], ea[:, q, j * P:(j + 1) * P], w1e[:, :], start=True, stop=True).then_inc(c_e, 1)
                    if q or not first:
                        segment(g - 1, 1 - q, first)

            def segment(g, q, first):
                pe.wait_ge(c_oh, g + 1)
                if not first:
                    pe.wait_ge(c_acc, 2 * (g - 1) + 1)
                for j in range(GT):
                    pe.wait_ge(c_relu, GT * g + j + 1)
                    for k in range(KC):
                        mm(seg[q][:, k, :], work[:, GT * q + j, k * P:(k + 1) * P], oh[:, q, j, :],
                           start=(j == 0 and k == 0), stop=(j == GT - 1), skip_group_check=True)
                    last = mm(seg_deg[q], ones[:, 0:1], oh[:, q, j, :], start=False, stop=(j == GT - 1),
                              skip_group_check=True)
                last.then_inc(c_seg, 1)

            edge_pe(0, True)
            with pe.Fori(1, NG // 2) as i:
                edge_pe(i, False)
            segment(NG - 1, 1, False)

            pe.wait_ge(flag_set, 1)
            missed = pe.value_load(flag[0:1, 0:1], min_val=0, max_val=NT * P)
            with pe.If(missed != 0):
                with pe.Fori(0, NT) as t:
                    pe.wait_ge(l_acc, LCH * t + 1)
                    pe.wait_ge(l_ld, 16 * (t + 1))
                    mm(banks[0][:, :], ea[:, 0, 0:P], w1e[:, :], start=True, stop=True).then_inc(l_e, 1)
                    pe.wait_ge(l_oh, t + 1)
                    pe.wait_ge(l_relu, t + 1)
                    for k in range(LCH):
                        if k:
                            pe.wait_ge(l_acc, LCH * t + k + 1)
                        for b, (n0, nn) in enumerate(PIECES):
                            if k < KC:
                                last = mm(banks[1 + b][:, 0:nn], work[:, 0, k * P:(k + 1) * P], ohf[:, n0:n0 + nn], start=True, stop=True)
                            else:
                                last = mm(banks[1 + b][0:1, 0:nn], ones[:, 0:1], ohf[:, n0:n0 + nn], start=True, stop=True)
                        last.then_inc(l_seg, 1)

            pe.wait_ge(agg_ready, 1)
            pe.wait_ge(big_loaded, 32)
            with pe.Fori(0, NCH) as c:
                cols = ds(c * NC, NC)
                for j in range(KC):
                    for k in range(KC):
                        mm(banks[j][:, 0:NC], w2[:, k, j * P:(j + 1) * P], aggT[:, k, cols], start=(k == 0), stop=False)
                    last = mm(banks[j][:, 0:NC], b2_row[:, j * P:(j + 1) * P], degree[:, cols], start=False, stop=True)
                last.then_inc(d_mm2, 1)
                pe.wait_ge(d_agg2, c + 1)
                for j in range(KC):
                    q, n = j % 2, KC * c + j
                    if j >= 2:
                        pe.wait_ge(d_t, n - 1)
                    for part in range(2):
                        o = banks[4 + 2 * q][:, 256 * part:256 * part + NC]
                        w = slice(part * HD + j * P, part * HD + (j + 1) * P)
                        for k in range(KC):
                            mm(o, wih[:, k, w], agg2[:, k, :], start=(k == 0), stop=False)
                        for k in range(KC):
                            last = mm(o, whh[:, k, w], hT[:, k, cols], start=False, stop=(k == KC - 1))
                    last.then_inc(d_rz, 1)
                    w = slice(2 * HD + j * P, 2 * HD + (j + 1) * P)
                    for k in range(KC):
                        mm(banks[5 + 2 * q][:, 0:NC], wih[:, k, w], agg2[:, k, :], start=(k == 0), stop=(k == KC - 1))
                    for k in range(KC):
                        last = mm(banks[5 + 2 * q][:, 256:256 + NC], whh[:, k, w], hT[:, k, cols], start=(k == 0), stop=(k == KC - 1))
                    last.then_inc(d_n, 1)
                pe.wait_ge(d_t, KC * c + KC)

            pe.wait_ge(d_x1, NCH * KC)
            layer_norm(1)
            table_product(1)
            pe.wait_ge(tb[1]["out"], NTT)

            pe.wait_ge(m_base, 16)
            mm(banks[7][:, 0:NG], ones[0:1, :], first_key[0:1, :, 0], start=True, stop=True).then_inc(m_spread, 1)

            def segment2(i, first):
                for q in range(2):
                    g = 2 * i + q
                    pe.wait_ge(m_msg, g + 1)
                    pe.wait_ge(m_oh, g + 1)
                    if not first:
                        pe.wait_ge(m_acc, g)
                    for j in range(GT):
                        for k in range(MCH):
                            width = P if k < 2 else MSG - 2 * P
                            last = mm(seg2[q][0:width, k, :], msg[q][:, j, k * P:k * P + width], oh[:, q, j, :],
                                      start=(j == 0 and k == 0), stop=(j == GT - 1), skip_group_check=True)
                    last.then_inc(m_seg, 1)

            segment2(0, True)
            with pe.Fori(1, NG // 2) as i:
                segment2(i, False)

            pe.wait_ge(miss_sum, 2)
            mm(banks[7][:, 0:1], ones[:, :], n_left[:, :], start=True, stop=True).then_inc(miss_total, 1)
            pe.wait_ge(flag2_set, 1)
            missed = pe.value_load(flag2[0:1, 0:1], min_val=0, max_val=NT * P)
            with pe.If(missed != 0):
                with pe.Fori(0, NT) as t:
                    pe.wait_ge(n_msg, t + 1)
                    pe.wait_ge(n_oh, t + 1)
                    for k in range(MCH):
                        pe.wait_ge(n_acc, MCH * t + k + 1)
                        width = P if k < 2 else MSG - 2 * P
                        for b, (n0, nn) in enumerate(PIECES):
                            last = mm(banks[1 + b][0:width, 0:nn], left_msg[:, k * P:k * P + width], ohf[:, n0:n0 + nn], start=True, stop=True)
                        last.then_inc(n_seg, 1)
            pe.wait_ge(acc2_ready, 1)

            def output(c, first):
                cols = ds(c * NC, NC)
                mm(banks[0][:, 0:NC], wo1s[:, :], acc2[:, 0, cols], start=True, stop=True)
                mm(banks[1][:, 0:NC], wo1v[:, 0, :], acc2[:, 1, cols], start=True, stop=True)
                mm(banks[2][:, 0:NC], wo1v[:, 1, :], acc2[:, 1, cols], start=True, stop=True)
                mm(banks[3][:, 0:NC], wo1v[:, 0, :], acc2[:, 2, cols], start=True, stop=True).then_inc(o_mm1, 1)
                pe.wait_ge(o_ssp, c + 1)
                mm(banks[4][:, 0:NC], wo2[:, 0, :], work[:, 1, 0:NC], start=True, stop=True)
                pe.wait_ge(o_ev, c + 1)
                for k in range(3):
                    last = mm(banks[5 + k][:, 0:NC], wo2[:, 1, :], work[:, 2 + k, 0:NC], start=True, stop=True)
                last.then_inc(o_mm2, 1)
                pe.wait_ge(o_out, c + 1)
            with pe.Fori(0, NCH) as c:
                output(c, False)


def kernel(**inputs):
    import numpy as np
    import concourse.bacc as bacc
    from concourse import mybir as mb
    from concourse.bass_utils import run_bass_kernel_spmd as run

    g = {k: np.asarray(v) for k, v in inputs.items()}

    def perm(w):
        return np.concatenate([w[..., :P], np.moveaxis(w[..., P:].reshape(*w.shape[:-1], P, 3), -1, -2).reshape(*w.shape[:-1], 3 * P)], axis=-1)

    def chunks(w):
        return w.reshape(KC, P, -1).transpose(1, 0, 2)

    def gates(w):
        return np.concatenate([perm(x) for x in np.split(w, 3, axis=-1)], axis=-1)

    def by_edge(v, fill):
        out = np.full((NT * P,) + v.shape[1:], fill, v.dtype)
        out[:NE] = v
        return out

    def tiles(v):
        return np.moveaxis(v.reshape(NT, P, *v.shape[1:]), 1, 0)

    L0 = {k[7:]: v for k, v in g.items() if k.startswith("L0_gnn_")}
    L1 = {k[7:]: v for k, v in g.items() if k.startswith("L1_gnn_")}
    src, dst = g["src"], g["dst"]
    dst_pad = by_edge(dst, 0)
    arrays = {
        "xT": chunks(perm(g["x"]).T),
        "w1h": chunks(perm(L0["W1"][:, :HD]).T), "w1e": L0["W1"][:, HD:].T, "b1": L0["b1"][None],
        "w2": chunks(L0["W2"].T), "b2": L0["b2"][None],
        "wih": chunks(gates(L0["W_ih"].T)), "whh": chunks(gates(perm(L0["W_hh"]).T)),
        "b_ih": gates(L0["b_ih"]).reshape(3 * KC, P).T, "b_hh": gates(L0["b_hh"]).reshape(3 * KC, P).T,
        **{k: perm(L0[k]).reshape(KC, P).T for k in ("gamma", "beta", "run_mean", "run_var")},
        "w_in_s": L1["w_in2f_s"], "w_in_v": L1["w_in2f_v"],
        "fw1": L1["W1"], "fb1": L1["b1"][:, None],
        "fw2": np.concatenate([L1["W2"], L1["b2"][None]]).reshape(F + 1, F, 6).transpose(0, 2, 1)[:, :4].reshape(F + 1, 4 * F),
        "wo1s": np.concatenate([L1["w_f2o1_s"]] + [L1["w_f2o1_s"][F:]] * 2), "wo1v": L1["w_f2o1_v"],
        "wo2s": L1["w_f2o2_s"], "wo2v": L1["w_f2o2_v"],
        "src0": tiles(by_edge(src, 0)), "dst0": tiles(dst_pad),
        "srck": tiles(by_edge(src, PAD_KEY)), "keys": by_edge(src, PAD_KEY)[None], "dstm": tiles(by_edge(dst, -1)),
        "base": dst_pad[None, ::GE],
        "rcut": tiles(by_edge(g["edge_weight"], 0)), "y4": tiles(by_edge(g["edge_attr_4"], 0)),
        "fT": by_edge(g["edge_attr_20"], 0).T, "eaT": by_edge(g["edge_attr_128"], 0).T,
    }
    nc = bacc.Bacc("TRN2", target_bir_lowering=False, num_devices=1)
    fed, aps = {}, {}
    for name, v in arrays.items():
        v = np.ascontiguousarray(v)
        fed[name + "_in"] = v
        aps[name] = nc.dram_tensor(name + "_in", v.shape, mb.dt.from_np(v.dtype), kind="ExternalInput").ap()
    out = nc.dram_tensor("out_dram", (P, KC, N), mb.dt.float32, kind="ExternalOutput").ap()
    graph_kernel(nc, aps, out)
    r = run(nc, [fed], core_ids=[0])
    y = np.asarray(r.results[0]["out_dram"]).transpose(1, 0, 2).reshape(HD, N).T
    return np.concatenate([y[:, :P], y[:, P:].reshape(N, 3, P).transpose(0, 2, 1).reshape(N, 3 * P)], axis=1)
```

```python
import concourse.bass as bass
from concourse import mybir
from contextlib import ExitStack

P = 128
N, HD, ED = 1250, 512, 128
KC = HD // P
F, R = 32, 20
NE = 41250
GT = 4
GE = GT * P
NG = -(-NE // GE)
NT = NG * GT
CU = 4
CI = NG // CU
MU, MR = 9, 3
W, W2 = 32, 96
NW = N + W2
FINE, COARSE = 32, 40
PAD_KEY = FINE * COARSE - 1
NC = 250
NCH = N // NC
NTL = 125
NTT = N // NTL
CB = 9
ROW = 136
MSG = 320
LCH, MCH = 5, 3
PIECES = [(0, 417), (417, 417), (834, 416)]
LN_EPS, BN_EPS = 1e-5, 1e-5
LOG2 = 0.6931471805599453
INP, HID = 32, 64
GP = 656
GATES = (CI - 1) * GP
assert GATES >= 2 * KC * 3 * HD and NG == CI * CU + 1 and NG % MU == 0 and NG == 2 * CI + 1 + 2 * NCH * KC and NG == CB * (2 * NCH - 1)


def need(engine, semaphore, value):
    if not isinstance(value, int) or value > 0:
        engine.wait_ge(semaphore, value)


def graph_kernel(nc, a, out):
    f32, i32, bf16 = mybir.dt.float32, mybir.dt.int32, mybir.dt.bfloat16
    ALU, ACT, AX = mybir.AluOpType, mybir.ActivationFunctionType, mybir.AxisListType
    ds = bass.ds

    with ExitStack() as ctx:
        def sb(name, shape, dt=f32):
            return ctx.enter_context(nc.sbuf_tensor(name, shape, dt))

        def sem(name):
            return ctx.enter_context(nc.semaphore(name))

        xT = sb("xT", [P, KC, N])
        hT = sb("hT", [P, KC, N])
        aggT = sb("aggT", [P, KC, NW])
        wbuf = sb("wbuf", [P, KC, HD])
        w1e = sb("w1e", [P, HD])
        bias_row = sb("bias_row", [1, HD])
        big = sb("big", [P, GATES])
        wih = big[:, 0:KC * 3 * HD].rearrange("p (k n) -> p k n", k=KC)
        whh = big[:, KC * 3 * HD:2 * KC * 3 * HD].rearrange("p (k n) -> p k n", k=KC)
        b_ih = sb("b_ih", [P, 3 * KC])
        b_hh = sb("b_hh", [P, 3 * KC])
        b_rz = sb("b_rz", [P, 2 * KC])
        bn = sb("bn", [P, 4, KC])
        bn_scale = sb("bn_scale", [P, KC])
        bn_shift = sb("bn_shift", [P, KC])
        w_in = sb("w_in", [P, 2, F])
        fw1 = sb("fw1", [INP + R, F])[INP:INP + R, :]
        fb1 = sb("fb1", [HID + F, 1])[HID:HID + F, :]
        fw2 = sb("fw2", [HID + F + 1, 4 * F])[HID:HID + F + 1, :]
        wo1s = sb("wo1s", [P, P])
        wo1v = sb("wo1v", [P, 2, P])
        wo2 = sb("wo2", [P, 2, P])
        src0 = sb("src0", [P, NT], i32)
        dst0 = sb("dst0", [P, NT], i32)
        dstm = sb("dstm", [P, NT], i32)
        src_f = sb("src_f", [P, NT])
        rel = sb("rel", [P, NT])
        fine = sb("fine", [P, NT])
        coarse = sb("coarse", [P, NT])
        y4 = sb("y4", [P, NT, 4])
        base_i = sb("base_i", [P, NG], i32)
        base_f = sb("base_f", [P, NG])
        base2_f = sb("base2_f", [P, NG])
        base2_i = sb("base2_i", [P, NG], i32)
        first_key = sb("first_key", [1, NG, 2])
        n_left = sb("n_left", [P, 1])
        flag = sb("flag", [1, 1], i32)
        flag2 = sb("flag2", [1, 1], i32)
        iota = sb("iota", [P, N])
        ones = sb("ones", [P, P])
        onesm = sb("onesm", [P, P])
        epsb = sb("epsb", [P, 1])
        zero = sb("zero", [P, 1])
        lane = sb("lane", [P, 1], i32)
        lane_f = sb("lane_f", [P, 1])
        slot_f = sb("slot_f", [P, 1])
        rank_f = sb("rank_f", [P, 1])
        digit_i = sb("digit_i", [P, 4, 1], i32)
        earlier = sb("earlier", [P, P])
        ident = sb("ident", [P, P], bf16)
        own_tile = sb("own_tile", [P, GT])
        offsets = sb("offsets", [P, COARSE, NG])
        oh_fine = sb("oh_fine", [P, 2, GT, FINE], bf16)
        oh_coarse = sb("oh_coarse", [P, 2, GT, COARSE], bf16)
        fine_T = sb("fine_T", [P, 2, P])
        spread = sb("spread", [P, 2, GT, COARSE])
        lows = sb("lows", [P, 2, GT, COARSE])
        rank = sb("rank", [P, 2, GT])
        before = sb("before", [P, 2, GT])
        place = sb("place", [P, 2, GT], i32)
        eq = sb("eq", [P, 2, GT, P], bf16)
        key_row = sb("key_row", [P, 2, GE], i32)
        work = sb("work", [P, 8, HD])
        ea = sb("ea", [P, 2, GE])
        aux = sb("aux", [P, NW])
        degree = aux[0:1, :]
        feat_in = aux[INP:INP + R, 0:2 * GE]
        hid = aux[HID:HID + F + 1, 0:2 * GE]
        hid_ones = aux[HID + F:HID + F + 1, 0:2 * GE]
        scratch = sb("scratch", [P, N])
        hid_abs = scratch[HID:HID + F, 0:2 * GE]
        frow_t = sb("frow_t", [P, 2, GT, ROW])
        oh = sb("oh", [P, 2, GT, W])
        oh_sum = sb("oh_sum", [P, 2, W])
        idx = sb("idx", [P, CU, GT], i32)

        in_win, tmp_e, srck = scratch[:, 0:NT], scratch[:, NT:2 * NT], scratch[:, 2 * NT:3 * NT].bitcast(i32)
        spare = offsets[:, :, :].rearrange("p c g -> p (c g)")
        dst_f, rcut = spare[:, 0:NT], spare[:, NT:2 * NT]
        scratch_i = hT[:, 0, :].bitcast(i32)
        ohf = scratch
        eq_f = frow_t[:, :, :, :].rearrange("p q t r -> p (q t r)")
        second = xT[:, :, :].rearrange("p k n -> p (k n)")[:, 0:8 * HD].rearrange("p (s n) -> p s n", s=8)

        def tile_slot(u, j):
            s = GT * (u % 2) + j
            return work[:, s, :] if u < 2 else second[:, s, :]

        def slots(first, count, width):
            return work[:, first:first + count, :].rearrange("p a b -> p (a b)")[:, 0:width]

        dev = big[:, 0:KC * N].rearrange("p (k n) -> p k n", k=KC)
        sq = big[:, KC * N:2 * KC * N].rearrange("p (k n) -> p k n", k=KC)
        std = big[:, 2 * KC * N:2 * KC * N + N]
        hot_f = [aggT[:, 2 * q:2 * q + 2, :].rearrange("p k n -> p (k n)").bitcast(bf16)[:, 0:CB * GT * FINE].rearrange("p (t k) -> p t k", k=FINE) for q in range(2)]
        hot_c = [aggT[:, 2 * q:2 * q + 2, :].rearrange("p k n -> p (k n)").bitcast(bf16)[:, CB * GT * FINE:CB * GT * (FINE + COARSE)].rearrange("p (t k) -> p t k", k=COARSE) for q in range(2)]
        stage = [work[:, q, :].rearrange("p (k n) -> p k n", k=KC) for q in range(2)]
        tab = [work[:, 2 + q, :] for q in range(2)]
        counts = work[:, 4:8, :].rearrange("p a b -> p (a b)").bitcast(bf16)[:, 0:COARSE * NG].rearrange("p (c g) -> p c g", g=NG)
        setup_i = [key_row[:, 0, 0:P], key_row[:, 0, P:2 * P]]
        order, behind, others = (eq_f[:, k * P:(k + 1) * P] for k in range(3))
        total, start_c, lead = (fine_T[:, 0, 0:COARSE], fine_T[:, 0, 64:64 + COARSE], fine_T[:, 1, 0:COARSE])
        agg2 = slots(2, 2, KC * NC).rearrange("p (k n) -> p k n", k=KC)
        gate = [[work[:, 4 + q, 0:NC], work[:, 4 + q, 256:256 + NC]] for q in range(2)]
        cand = [[work[:, 6 + q, 0:NC], work[:, 6 + q, 256:256 + NC]] for q in range(2)]
        a0 = MU * GT * ROW
        a1 = a0 + MR * GT * P
        a2 = a1 + MR * GT * MSG
        rows = [big[:, u * GT * ROW:(u + 1) * GT * ROW].rearrange("p (t r) -> p t r", t=GT) for u in range(MU)]
        feat = [big[:, a0 + u * GT * P:a0 + (u + 1) * GT * P].rearrange("p (t r) -> p t r", t=GT) for u in range(MR)]
        msg = [big[:, a1 + u * GT * MSG:a1 + (u + 1) * GT * MSG].rearrange("p (t r) -> p t r", t=GT) for u in range(MR)]
        left_msg = msg[0][:, 0, :]
        prod = big[:, a2:a2 + GT * 256].rearrange("p (t m) -> p t m", t=GT)
        oh2 = big[:, a2 + GT * 256:a2 + GT * 256 + MR * GT * W2].rearrange("p (u t w) -> p u t w", u=MR, t=GT)
        key2, rel2, left2 = fine, coarse, src_f
        acc2 = aggT[:, 0:3, :]
        banks = [ctx.enter_context(nc.psum_tensor(f"bank{b}", [P, 512], f32)) for b in range(6)]
        pair_banks = ctx.enter_context(nc.psum_tensor("pair_banks", [P, 1024], f32))
        banks += [pair_banks[:, 0:512], pair_banks[:, 512:1024]]
        seg = [banks[4 + q][:, 0:KC * W].rearrange("p (k w) -> p k w", k=KC) for q in range(2)]
        seg_deg = [banks[4 + q][0:1, KC * W:(KC + 1) * W] for q in range(2)]
        seg2 = [banks[4 + u][:, 0:MCH * W2].rearrange("p (k w) -> p k w", k=MCH) for u in range(MR)]
        turned = pair_banks[:, 0:P].bitcast(bf16)
        looked = pair_banks[:, P:P + 2 * GT * COARSE]

        P_d = nc.dram_tensor("P_d", (N, HD), f32, kind="Internal").ap()
        G_d = nc.dram_tensor("G_d", (N, P), f32, kind="Internal").ap()
        rows_d = nc.dram_tensor("rows_d", (NT * P, ROW), f32, kind="Internal").ap()

        x_loaded, weights_loaded, edges_loaded, w2_loaded, big_loaded, x_again = (
            sem(k) for k in ("x_loaded", "weights_loaded", "edges_loaded", "w2_loaded", "big_loaded", "x_again"))
        keys_loaded = sem("keys_loaded")
        zeroed, prep_done, iota_done, stored = (sem(k) for k in ("zeroed", "prep_done", "iota_done", "stored"))
        bn_var, bn_std, miss_sum, miss_total, flag_set, flag2_set, agg_ready, acc2_ready = (
            sem(k) for k in ("bn_var", "bn_std", "miss_sum", "miss_total", "flag_set", "flag2_set", "agg_ready", "acc2_ready"))
        dve_link, pool_passed, pe_passed = sem("dve_link"), sem("pool_passed"), sem("pe_passed")
        ln = [{k: sem(f"ln{l}_{k}") for k in ("mean", "dev", "sq", "var", "std", "rstd", "norm", "done")} for l in range(2)]
        tb = [{k: sem(f"tab{l}_{k}") for k in ("stage", "mm", "out", "st0", "st1")} for l in range(2)]
        s_oh, s_count, s_hist, s_set, s_corr, s_off = (sem("s_" + k) for k in ("oh", "count", "hist", "set", "corr", "off"))
        s_lead = sem("s_lead")
        agg_zeroed = sem("agg_zeroed")
        t_key, t_oh, t_tr, t_fT, t_spread, t_look, t_low, t_place, t_rank = (
            sem("t_" + k) for k in ("key", "oh", "tr", "fT", "spread", "look", "low", "place", "rank"))
        f_ld, f_h, f_abs, f_exp, f_ln, f_pos, f_hid, f_w, f_roww, f_rowy, f_st = (
            sem("f_" + k) for k in ("ld", "h", "abs", "exp", "ln", "pos", "hid", "w", "roww", "rowy", "st"))
        gathered = [sem(f"gathered{u}") for u in range(CU)]
        ea_s = [sem("ea_s0"), sem("ea_s1")]
        c_idx, c_e, c_add, c_relu, c_oh, c_seg, c_acc = (sem("c_" + k) for k in ("idx", "e", "add", "relu", "oh", "seg", "acc"))
        l_ld, l_e, l_add, l_relu, l_oh, l_seg, l_acc, l_gat, l_idx, l_key = (
            sem("l_" + k) for k in ("ld", "e", "add", "relu", "oh", "seg", "acc", "gat", "idx", "key"))
        n_ld, n_idx, n_gat, n_prod, n_msg, n_oh, n_seg, n_acc = (
            sem("n_" + k) for k in ("ld", "idx", "gat", "prod", "msg", "oh", "seg", "acc"))
        d_mm2, d_agg2, d_rz, d_n, d_sig, d_hn, d_t, d_tanh, d_x1 = (
            sem("d_" + k) for k in ("mm2", "agg2", "rz", "n", "sig", "hn", "t", "tanh", "x1"))
        d_s = [sem(f"d_s{k}") for k in range(4)]
        m_ld, m_gat = [sem(f"m_ld{u}") for u in range(MU)], [sem(f"m_gat{u}") for u in range(MR)]
        m_start = sem("m_start")
        m_base, m_spread, m_idx, m_prod, m_msg, m_rel, m_oh, m_seg, m_acc = (
            sem("m_" + k) for k in ("base", "spread", "idx", "prod", "msg", "rel", "oh", "seg", "acc"))
        o_mm1, o_ev, o_abs, o_exp, o_ln, o_pos, o_ssp, o_mm2, o_out = (
            sem("o_" + k) for k in ("mm1", "ev", "abs", "exp", "ln", "pos", "ssp", "mm2", "out"))
        WL, EL = 19, 6

        def beside_turn(i):
            return i, 2 * i, 2, 128 * i

        last_turn = (CI, NG - 1, 1, 128 * CI)

        def beside_step(n):
            return CI + 1 + n, 2 * CI + 2 * n, 2, 128 * CI + 64 + 128 * n

        def gather_uses(u, n):
            return MU // MR * (n - 1) + u // MR + 1

        block = ctx.enter_context(nc.Block())

        @block.sync
        def _(sp):
            def load(dst, name, done):
                sp.dma_start(dst, a[name]).then_inc(done, 16)

            load(xT[:, :, :], "xT", x_loaded)
            load(wbuf[:, :, :], "w1h", weights_loaded)
            load(bias_row[:, :], "b1", weights_loaded)
            load(b_ih[:, :], "b_ih", weights_loaded)
            load(b_hh[:, :], "b_hh", weights_loaded)
            load(w1e[:, :], "w1e", weights_loaded)
            load(fw1, "fw1", weights_loaded)
            load(fb1, "fb1", weights_loaded)
            for k, name in enumerate(("gamma", "beta", "run_mean", "run_var")):
                load(bn[:, k, :], name, weights_loaded)
            load(w_in[:, 0, :], "w_in_s", weights_loaded)
            load(w_in[:, 1, :], "w_in_v", weights_loaded)
            load(fw2, "fw2", weights_loaded)
            load(wo1s[:, :], "wo1s", weights_loaded)
            sp.wait_ge(zeroed, 1)
            load(wo1v[0:64, 0, :], "wo1v", weights_loaded)
            load(wo1v[64:128, 1, :], "wo1v", weights_loaded)
            load(wo2[:, 0, :], "wo2s", weights_loaded)
            load(wo2[:, 1, :], "wo2v", weights_loaded)

            def store_table(l, dram, width):
                with sp.Fori(0, NTT // 2) as i:
                    for q in range(2):
                        sp.wait_ge(tb[l]["out"], 2 * i + q + 1)
                        sp.dma_start(dram[ds((2 * i + q) * NTL, NTL), :], tab[q][0:NTL, 0:width]).then_inc(tb[l][f"st{q}"], 16)

            store_table(0, P_d, HD)
            load(bias_row[:, :], "b2", w2_loaded)
            load(wbuf[:, :, :], "w2", w2_loaded)

            def filter_load(s, f, nq, st):
                need(sp, f_h, s)
                sp.dma_start(feat_in[:, 0:nq * GE], a["fT"][:, ds(f * GE, nq * GE)]).then_inc(f_ld, 16)
                need(sp, t_rank, s)
                sp.dma_start(key_row[:, 0:nq, :].rearrange("p q e -> p (q e)"),
                             a["keys"][:, ds(f * GE, nq * GE)].broadcast_to([P, nq * GE])).then_inc(t_key, 16)

            def edge_load(g, u):
                need(sp, c_e, GT * (g - 1))
                sp.dma_start(ea[:, u % 2, :], a["eaT"][:, ds(g * GE, GE)]).then_inc(ea_s[u % 2], 16)

            def turn(i):
                for u in range(CU):
                    edge_load(CU * i + u, u)
                    if u == 1:
                        filter_load(*beside_turn(i))

            sp.wait_ge(s_off, 1)
            turn(0)
            with sp.Fori(1, CI) as i:
                turn(i)
            edge_load(NG - 1, 0)
            filter_load(*last_turn)

            sp.wait_ge(c_e, NT)
            sp.wait_ge(flag_set, 1)
            missed = sp.value_load(flag[0:1, 0:1], min_val=0, max_val=NT * P)
            with sp.If(missed != 0):
                with sp.Fori(0, NT) as t:
                    sp.wait_ge(l_acc, LCH * t + 1)
                    sp.dma_start(ea[:, 0, 0:P], a["eaT"][:, ds(t * P, P)]).then_inc(l_ld, 16)

            sp.wait_ge(c_seg, NG)
            load(xT[:, :, :], "xT", x_again)
            with sp.Fori(0, NCH * KC) as n:
                filter_load(*beside_step(n))

            store_table(1, G_d, P)

            sp.wait_ge(f_st, 64 * NG)
            sp.dma_start(first_key[0:1, :, :], rows_d[0:NT * P:GE, P + 4:P + 6].rearrange("(o g) k -> o g k", o=1)).then_inc(m_base, 16)
            sp.wait_ge(ln[1]["done"], NCH)

            def row_load(g, u):
                need(sp, m_msg, g - MU + 1)
                need(sp, m_rel, g - MU + 1)
                sp.dma_start(rows[u], rows_d[ds(g * GE, GE), :].rearrange("(t p) r -> p t r", p=P)).then_inc(m_ld[u], 16)

            for u in range(MU):
                row_load(u, u)
            with sp.Fori(1, NG // MU) as i:
                for u in range(MU):
                    row_load(MU * i + u, u)

            sp.wait_ge(flag2_set, 1)
            missed = sp.value_load(flag2[0:1, 0:1], min_val=0, max_val=NT * P)
            with sp.If(missed != 0):
                with sp.Fori(0, NT) as t:
                    sp.wait_ge(n_acc, MCH * t + 1)
                    sp.dma_start(rows[0][:, 0, :], rows_d[ds(t * P, P), :]).then_inc(n_ld, 16)
            for c, (n0, nn) in enumerate(PIECES):
                sp.wait_ge(o_out, c + 1)
                sp.dma_start(out[:, :, n0:n0 + nn], xT[:, :, n0:n0 + nn]).then_inc(stored, 16)
            sp.wait_ge(stored, 16 * len(PIECES))

        @block.gpsimd
        def _(gp):
            nc.gpsimd.iota(scratch_i, pattern=[[1, N]], base=0, channel_multiplier=0).then_inc(iota_done, 1)
            nc.gpsimd.iota(lane[:, :], pattern=[[0, 1]], base=0, channel_multiplier=1).then_inc(iota_done, 1)
            nc.gpsimd.memset(wo1v[:, :, :], 0.0).then_inc(zeroed, 1)
            gp.wait_ge(s_count, 2 * NCH - 1)
            nc.gpsimd.memset(aggT[:, :, :], 0.0).then_inc(agg_zeroed, 1)
            gp.wait_ge(edges_loaded, 16 * EL)
            for q in range(2):
                gp.wait_ge(tb[0][f"st{q}"], 16 * (NTT // 2))
            gp.wait_ge(s_off, 1)

            def scatter(s, f, nq, st, part):
                if part == 0:
                    gp.wait_ge(t_place, s + 1)
                    gp.wait_ge(f_rowy, s + 1)
                    gp.wait_ge(f_roww, s + 1)
                    gp.sem_inc(pool_passed, 1)
                for j in range(GT):
                    gp.indirect_dma_start(rows_d[:, :], bass.IndirectOffsetOnAxis(ap=place[:, part, j:j + 1], axis=0),
                                          frow_t[:, part, j, :], None).then_inc(f_st, 16)

            def gather(g, u):
                need(gp, c_seg, g - CU + 1)
                nc.gpsimd.tensor_copy(idx[:, u, :], src0[:, ds(g * GT, GT)]).then_inc(c_idx, 1)
                gp.wait_ge(c_idx, g + 1)
                gp.sem_inc(pool_passed, 1)
                for j in range(GT):
                    gp.indirect_dma_start(tile_slot(u, j), None, P_d[:, :],
                                          bass.IndirectOffsetOnAxis(ap=idx[:, u, j:j + 1], axis=0)).then_inc(gathered[u], 16)

            def turn(i):
                for u in range(CU):
                    gather(CU * i + u, u)
                    if u >= 2 and not isinstance(i, int):
                        scatter(*beside_turn(i - 1), u - 2)

            turn(0)
            with gp.Fori(1, CI) as i:
                turn(i)
            gather(NG - 1, 0)
            scatter(*beside_turn(CI - 1), 0)
            scatter(*beside_turn(CI - 1), 1)
            scatter(*last_turn, 0)

            gp.wait_ge(flag_set, 1)
            missed = gp.value_load(flag[0:1, 0:1], min_val=0, max_val=NT * P)
            with gp.If(missed != 0):
                gp.wait_ge(c_seg, NG)
                with gp.Fori(0, NT) as t:
                    gp.wait_ge(l_acc, LCH * t + 1)
                    nc.gpsimd.tensor_copy(idx[:, 0, 0:1], src0[:, ds(t, 1)]).then_inc(l_idx, 1)
                    gp.wait_ge(l_idx, t + 1)
                    gp.sem_inc(pool_passed, 1)
                    gp.indirect_dma_start(work[:, 0, :], None, P_d[:, :],
                                          bass.IndirectOffsetOnAxis(ap=idx[:, 0, 0:1], axis=0)).then_inc(l_gat, 16)

            with gp.Fori(0, NCH * KC) as n:
                for part in range(2):
                    scatter(*beside_step(n), part)

            for q in range(2):
                gp.wait_ge(tb[1][f"st{q}"], 16 * (NTT // 2))

            def gather2(g, u, n):
                need(gp, m_msg, g - MR + 1)
                gp.wait_ge(m_idx, g + 1)
                gp.sem_inc(pool_passed, 1)
                for j in range(GT):
                    gp.indirect_dma_start(feat[u % MR][:, j, :], None, G_d[:, :],
                                          bass.IndirectOffsetOnAxis(ap=idx[:, u % MR, j:j + 1], axis=0)).then_inc(m_gat[u % MR], 16)

            for u in range(MU):
                gather2(u, u, 1)
            with gp.Fori(1, NG // MU) as i:
                for u in range(MU):
                    gather2(MU * i + u, u, i + 1)

            gp.wait_ge(flag2_set, 1)
            missed = gp.value_load(flag2[0:1, 0:1], min_val=0, max_val=NT * P)
            with gp.If(missed != 0):
                with gp.Fori(0, NT) as t:
                    gp.wait_ge(n_acc, MCH * t + 1)
                    gp.wait_ge(n_ld, 16 * (t + 1))
                    gp.sem_inc(pool_passed, 1)
                    nc.gpsimd.tensor_copy(idx[:, 0, 0:1], rows[0][:, 0, P + 5:P + 6]).then_inc(n_idx, 1)
                    gp.wait_ge(n_idx, t + 1)
                    gp.sem_inc(pool_passed, 1)
                    gp.indirect_dma_start(feat[0][:, 0, :], None, G_d[:, :],
                                          bass.IndirectOffsetOnAxis(ap=idx[:, 0, 0:1], axis=0)).then_inc(n_gat, 16)

        @block.scalar
        def _(act):
            s = nc.scalar

            def norm_and_table(l, width, scale):
                def square(c):
                    act.wait_ge(ln[l]["dev"], c + 1)
                    s.activation(sq[:, :, ds(c * NC, NC)], dev[:, :, ds(c * NC, NC)], ACT.Square).then_inc(ln[l]["sq"], 1)

                def root(c):
                    act.wait_ge(ln[l]["var"], c + 1)
                    s.activation(std[:, ds(c * NC, NC)], banks[1][:, 0:NC], ACT.Sqrt, bias=epsb[:, :]).then_inc(ln[l]["std"], 1)

                def rectify(c):
                    act.wait_ge(ln[l]["norm"], c + 1)
                    s.activation(hT[:, :, ds(c * NC, NC)], dev[:, :, ds(c * NC, NC)], ACT.Relu).then_inc(ln[l]["done"], 1)
                    act.wait_ge(ln[l]["done"], c + 1)
                    for q in range(2):
                        need(act, tb[l]["mm"], 2 * c + q - 1)
                        s.activation(stage[q][:, :, 0:NTL], hT[:, :, ds((2 * c + q) * NTL, NTL)], ACT.Copy).then_inc(tb[l]["stage"], 1)

                def tiles_out(c):
                    for q in range(2):
                        act.wait_ge(tb[l]["mm"], 2 * c + q + 1)
                        need(act, tb[l][f"st{q}"], 16 * c)
                        s.activation(tab[q][0:NTL, 0:width], banks[2 + q][0:NTL, 0:width], ACT.Copy, scale=scale).then_inc(tb[l]["out"], 1)

                square(0)
                square(1)
                root(0)
                rectify(0)
                square(2)
                root(1)
                tiles_out(0)
                rectify(1)
                with act.Fori(2, NCH - 1) as c:
                    square(c + 1)
                    root(c)
                    tiles_out(c - 1)
                    rectify(c)
                root(NCH - 1)
                tiles_out(NCH - 2)
                rectify(NCH - 1)
                tiles_out(NCH - 1)

            act.dma_start(srck, a["srck"]).then_inc(keys_loaded, 16)
            for dst, name in ((src0, "src0"), (dst0, "dst0"), (dstm, "dstm")):
                act.dma_start(dst[:, :], a[name]).then_inc(edges_loaded, 16)
            act.dma_start(rcut, a["rcut"]).then_inc(edges_loaded, 16)
            act.dma_start(y4[:, :, :], a["y4"]).then_inc(edges_loaded, 16)
            act.dma_start(base_i[:, :], a["base"].broadcast_to([P, NG])).then_inc(edges_loaded, 16)
            act.wait_ge(prep_done, 1)
            norm_and_table(0, HD, 1.0)
            act.wait_ge(bn_var, 1)
            s.activation(bn_scale[:, :], bn_scale[:, :], ACT.Sqrt).then_inc(bn_std, 1)
            act.wait_ge(weights_loaded, 16 * WL)

            s.preload_act_table_set("natural_log_exp_and_others")

            def fine_out(k, f, nq, st):
                act.wait_ge(t_tr, k + 1)
                need(act, t_look, k)
                s.activation(fine_T[:, 0:nq, :].rearrange("p q e -> p (q e)"), turned[:, 0:nq * P], ACT.Copy).then_inc(t_fT, 1)

            def hidden_abs(k, f, nq, st):
                h = hid_abs[:, 0:nq * GE]
                act.wait_ge(f_h, k + 1)
                need(act, f_hid, k)
                s.activation(h, pair_banks[HID:HID + F, 0:nq * GE], ACT.Abs, bias=fb1).then_inc(f_abs, 1)

            def hidden_exp(k, f, nq, st):
                h = hid_abs[:, 0:nq * GE]
                act.wait_ge(f_abs, k + 1)
                s.activation(h, h, ACT.Exp, scale=-1.0).then_inc(f_exp, 1)

            def hidden_ln(k, f, nq, st):
                h = hid_abs[:, 0:nq * GE]
                act.wait_ge(f_exp, k + 1)
                s.activation(h, h, ACT.Ln, bias=1.0).then_inc(f_ln, 1)

            def filters_out(k, f, nq, st):
                act.wait_ge(f_w, k + 1)
                act.wait_ge(f_rowy, k + 1)
                s.activation(frow_t[:, 0:nq, :, 0:P], pair_banks[:, 0:nq * GE].rearrange("p (q t r) -> p q t r", q=nq, t=GT),
                             ACT.Copy).then_inc(f_roww, 1)

            def relu(g, u, tiles):
                for j in tiles:
                    act.wait_ge(c_add, GT * g + j + 1)
                    s.activation(tile_slot(u, j), tile_slot(u, j), ACT.Relu).then_inc(c_relu, 1)

            def turn(i):
                item = beside_turn(i)
                relu(CU * i, 0, range(2))
                fine_out(*item)
                relu(CU * i, 0, range(2, GT))
                relu(CU * i + 1, 1, range(GT))
                hidden_abs(*item)
                hidden_exp(*item)
                relu(CU * i + 2, 2, range(2))
                hidden_ln(*item)
                relu(CU * i + 2, 2, range(2, GT))
                relu(CU * i + 3, 3, range(GT))
                filters_out(*item)

            turn(0)
            with act.Fori(1, CI) as i:
                act.dma_start(big[:, ds((i - 1) * GP, GP)], a["gates"][:, ds((i - 1) * GP, GP)]).then_inc(big_loaded, 16)
                turn(i)
            relu(NG - 1, 0, range(GT))
            fine_out(*last_turn)
            hidden_abs(*last_turn)
            hidden_exp(*last_turn)
            hidden_ln(*last_turn)
            filters_out(*last_turn)

            act.wait_ge(flag_set, 1)
            missed = act.value_load(flag[0:1, 0:1], min_val=0, max_val=NT * P)
            with act.If(missed != 0):
                with act.Fori(0, NT) as t:
                    act.wait_ge(l_add, t + 1)
                    s.activation(work[:, 0, :], work[:, 0, :], ACT.Relu).then_inc(l_relu, 1)

            with act.Fori(0, NCH) as c:
                act.wait_ge(d_mm2, c + 1)
                for j in range(KC):
                    last = s.activation(agg2[:, j, :], banks[j // 2][:, 256 * (j % 2):256 * (j % 2) + NC], ACT.Copy)
                last.then_inc(d_agg2, 1)
                for j in range(KC):
                    q, n = j % 2, KC * c + j
                    item = beside_step(n)
                    s.preload_act_table_set("natural_log_exp_and_others")
                    fine_out(*item)
                    hidden_abs(*item)
                    hidden_exp(*item)
                    hidden_ln(*item)
                    act.wait_ge(d_rz, n + 1)
                    if j >= 2:
                        act.wait_ge(d_x1, n - 1)
                    s.activation(gate[q][0], banks[2 + 2 * q][:, 0:NC], ACT.Sigmoid, bias=b_rz[:, j:j + 1])
                    s.activation(gate[q][1], banks[2 + 2 * q][:, 256:256 + NC], ACT.Sigmoid,
                                 bias=b_rz[:, KC + j:KC + j + 1]).then_inc(d_sig, 1)
                    act.wait_ge(d_t, n + 1)
                    s.activation(cand[q][0], cand[q][0], ACT.Tanh, bias=b_ih[:, 2 * KC + j:2 * KC + j + 1]).then_inc(d_tanh, 1)
                    filters_out(*item)
                act.wait_ge(d_x1, KC * c + KC)

            norm_and_table(1, P, float(P) ** -0.5)

            s.preload_act_table_set("natural_log_exp_and_others")

            def targets(g, u, n):
                act.wait_ge(m_ld[u], 16 * n)
                need(act, m_gat[u % MR], 64 * (gather_uses(u, n) - 1))
                s.activation(idx[:, u % MR, :], rows[u][:, :, P + 5], ACT.Copy).then_inc(m_idx, 1)
                s.activation(key2[:, ds(g * GT, GT)], rows[u][:, :, P + 4], ACT.Copy)
                s.activation(rel2[:, ds(g * GT, GT)], rows[u][:, :, P + 4], ACT.Identity, bias=base2_f[:, ds(g, 1)]).then_inc(m_rel, 1)

            act.wait_ge(m_start, 1)
            for u in range(MU):
                targets(u, u, 1)
            with act.Fori(1, NG // MU) as i:
                for u in range(MU):
                    targets(MU * i + u, u, i + 1)

            for c, (n0, nn) in enumerate(PIECES):
                act.wait_ge(o_mm1, c + 1)
                need(act, o_ssp, c)
                u = work[:, 0, 0:nn]
                s.activation(u, banks[0][:, 0:nn], ACT.Abs, scale=0.125).then_inc(o_abs, 1)
                act.wait_ge(o_abs, c + 1)
                s.activation(u, u, ACT.Exp, scale=-1.0).then_inc(o_exp, 1)
                act.wait_ge(o_exp, c + 1)
                s.activation(u, u, ACT.Ln, bias=1.0).then_inc(o_ln, 1)
                need(act, o_mm2, c)
                for k in range(3):
                    last = s.activation(work[:, 2 + k, 0:nn], banks[1 + k][:, 0:nn], ACT.Copy, scale=0.125)
                last.then_inc(o_ev, 1)

        @block.vector
        def _(dve):
            v = nc.vector
            chain = [0]

            def link(ins):
                chain[0] += 1
                ins.then_inc(dve_link, 1)
                dve.wait_ge(dve_link, chain[0])

            v.memset(ones[:, :], 1.0)
            v.memset(onesm[:, :], 1.0 / HD)
            v.memset(zero[:, :], 0.0)
            v.memset(epsb[:, :], LN_EPS)
            v.memset(degree, 0.0)
            v.memset(frow_t[:, :, :, :], 0.0)
            v.memset(hid_ones, 1.0).then_inc(prep_done, 1)

            dve.wait_ge(iota_done, 2)
            v.tensor_copy(lane_f[:, :], lane[:, :])
            v.tensor_scalar(digit_i[:, 0, :], lane[:, :], FINE - 1, None, ALU.bitwise_and)
            v.tensor_scalar(digit_i[:, 1, :], lane[:, :], 5, None, ALU.arith_shift_right)
            v.tensor_scalar(setup_i[0], scratch_i[:, 0:P], FINE - 1, None, ALU.bitwise_and)
            v.tensor_scalar(setup_i[1], scratch_i[:, 0:P], 5, None, ALU.arith_shift_right)
            link(v.tensor_copy(iota[:, :], scratch_i))

            def layer_norm(l, beside):
                def less_mean(c):
                    dve.wait_ge(ln[l]["mean"], c + 1)
                    v.tensor_tensor(dev[:, :, ds(c * NC, NC)], xT[:, :, ds(c * NC, NC)], banks[0][:, 0:NC].unsqueeze(1).broadcast_to([P, KC, NC]),
                                    ALU.subtract).then_inc(ln[l]["dev"], 1)

                def scaled(c):
                    r = std[:, ds(c * NC, NC)]
                    dve.wait_ge(ln[l]["std"], c + 1)
                    v.reciprocal(r, r).then_inc(ln[l]["rstd"], 1)
                    dve.wait_ge(ln[l]["rstd"], c + 1)
                    v.tensor_tensor(dev[:, :, ds(c * NC, NC)], dev[:, :, ds(c * NC, NC)], r.unsqueeze(1).broadcast_to([P, KC, NC]), ALU.mult).then_inc(ln[l]["norm"], 1)

                less_mean(0)
                beside(0)
                less_mean(1)
                scaled(0)
                with dve.Fori(1, NCH - 1) as c:
                    beside(c)
                    less_mean(c + 1)
                    scaled(c)
                beside(NCH - 1)
                scaled(NCH - 1)

            dve.wait_ge(keys_loaded, 16)
            v.tensor_copy(src_f[:, :], srck)
            v.tensor_scalar(in_win.bitcast(i32), srck, FINE - 1, None, ALU.bitwise_and)
            link(v.tensor_scalar(tmp_e.bitcast(i32), srck, 5, None, ALU.arith_shift_right))
            v.tensor_copy(fine[:, :], in_win.bitcast(i32))
            link(v.tensor_copy(coarse[:, :], tmp_e.bitcast(i32)))
            dve.wait_ge(edges_loaded, 16 * EL)
            v.tensor_copy(dst_f, dstm[:, :])
            v.tensor_copy(base_f[:, :], base_i[:, :])
            link(v.tensor_tensor(y4[:, :, :], y4[:, :, :], rcut.unsqueeze(2).broadcast_to([P, NT, 4]), ALU.mult))
            link(v.tensor_tensor(rel[:, :].rearrange("p (g t) -> p g t", t=GT), dst_f.rearrange("p (g t) -> p g t", t=GT),
                                 base_f[:, :].unsqueeze(2).broadcast_to([P, NG, GT]), ALU.subtract))
            v.tensor_scalar(in_win, rel[:, :], 0.0, None, ALU.is_ge)
            link(v.tensor_scalar(tmp_e, rel[:, :], float(W), None, ALU.is_lt))
            link(v.tensor_tensor(in_win, in_win, tmp_e, ALU.mult))
            link(v.tensor_scalar(tmp_e, dst_f, 0.0, None, ALU.is_ge))
            link(v.tensor_tensor(in_win, tmp_e, in_win, ALU.subtract))
            v.tensor_reduce(n_left[:, :], in_win, AX.X, ALU.add).then_inc(miss_sum, 1)
            dve.wait_ge(weights_loaded, 16 * WL)
            for part in range(1, 4):
                v.tensor_scalar(wo1s[part * F:part * F + F, :], wo1s[part * F:part * F + F, :], 3.0 ** -0.5, None, ALU.mult)
            v.tensor_tensor(b_rz[:, :], b_ih[:, 0:2 * KC], b_hh[:, 0:2 * KC], ALU.add)
            v.tensor_scalar(bn_scale[:, :], bn[:, 3, :], BN_EPS, None, ALU.add).then_inc(bn_var, 1)
            dve.wait_ge(x_loaded, 16)

            def batch_hots(n, q):
                need(dve, s_count, n - 1)
                tiles = ds(n * CB * GT, CB * GT)
                v.tensor_tensor(hot_f[q], iota[:, 0:FINE].unsqueeze(1).broadcast_to([P, CB * GT, FINE]),
                                fine[:, tiles].unsqueeze(2).broadcast_to([P, CB * GT, FINE]), ALU.is_equal)
                v.tensor_tensor(hot_c[q], iota[:, 0:COARSE].unsqueeze(1).broadcast_to([P, CB * GT, COARSE]),
                                coarse[:, tiles].unsqueeze(2).broadcast_to([P, CB * GT, COARSE]), ALU.is_equal).then_inc(s_oh, 1)

            def count_out(n, q):
                dve.wait_ge(s_count, n + 1)
                v.tensor_copy(counts[:, :, ds(n * CB, CB)], banks[4 + q][:, 0:CB * COARSE].rearrange("p (g c) -> p c g", c=COARSE)).then_inc(s_hist, 1)

            def count_beside(c):
                batch_hots(2 * c, 0)
                if not isinstance(c, int) or c > 0:
                    count_out(2 * c - 1, 1)
                if not isinstance(c, int) or c < NCH - 1:
                    batch_hots(2 * c + 1, 1)
                count_out(2 * c, 0)

            layer_norm(0, count_beside)

            v.tensor_copy(slot_f[:, :], digit_i[:, 1, :])
            link(v.scalar_tensor_tensor(rank_f[:, :], digit_i[:, 0, :], float(GT), digit_i[:, 1, :], ALU.mult, ALU.add))
            v.scalar_tensor_tensor(order, setup_i[0], float(GT), setup_i[1], ALU.mult, ALU.add)
            v.tensor_scalar(earlier[:, :], iota[:, 0:P], lane_f[:, :], None, ALU.is_lt)
            v.tensor_scalar(own_tile[:, :], iota[:, 0:GT], slot_f[:, :], None, ALU.is_equal)
            link(v.tensor_scalar(ident[:, :], iota[:, 0:P], lane_f[:, :], None, ALU.is_equal))
            v.tensor_scalar(behind, order, rank_f[:, :], None, ALU.is_gt)
            link(v.tensor_scalar(others, iota[:, 0:P], lane_f[:, :], None, ALU.not_equal))

            def one_hots(g, q, nq, done):
                v.tensor_tensor(oh_fine[:, q:q + nq, :, :].rearrange("p q t k -> p (q t) k"), iota[:, 0:FINE].unsqueeze(1).broadcast_to([P, nq * GT, FINE]),
                                fine[:, ds(g * GT, nq * GT)].unsqueeze(2).broadcast_to([P, nq * GT, FINE]), ALU.is_equal)
                v.tensor_tensor(oh_coarse[:, q:q + nq, :, :].rearrange("p q t k -> p (q t) k"), iota[:, 0:COARSE].unsqueeze(1).broadcast_to([P, nq * GT, COARSE]),
                                coarse[:, ds(g * GT, nq * GT)].unsqueeze(2).broadcast_to([P, nq * GT, COARSE]), ALU.is_equal).then_inc(done, 1)

            dve.wait_ge(s_hist, 2 * NCH - 1)

            flat_off, flat_cnt = offsets[:, :, :].rearrange("p c g -> p (c g)"), counts.rearrange("p c g -> p (c g)")
            v.tensor_reduce(total, counts, AX.X, ALU.add)
            link(v.tensor_tensor_scan(flat_off, flat_cnt, zero[:, :].broadcast_to([P, COARSE * NG]), 0.0, ALU.add, ALU.add))
            link(v.tensor_tensor(flat_off, flat_off, flat_cnt, ALU.subtract))
            v.tensor_copy(start_c, offsets[:, :, 0]).then_inc(s_set, 1)
            dve.wait_ge(s_corr, 1)
            v.tensor_copy(lead, banks[7][:, 0:COARSE]).then_inc(s_lead, 1)
            dve.wait_ge(s_lead, 1)
            link(v.tensor_tensor(offsets[:, :, :], offsets[:, :, :], lead.unsqueeze(2).broadcast_to([P, COARSE, NG]), ALU.add))

            dve.wait_ge(bn_std, 1)
            link(v.reciprocal(bn_shift[:, :], bn_scale[:, :]))
            link(v.tensor_tensor(bn_scale[:, :], bn_shift[:, :], bn[:, 0, :], ALU.mult))
            link(v.tensor_tensor(bn_shift[:, :], bn_scale[:, :], bn[:, 2, :], ALU.mult))
            link(v.tensor_tensor(bn_shift[:, :], bn[:, 1, :], bn_shift[:, :], ALU.subtract))
            dve.wait_ge(miss_total, 1)
            v.tensor_copy(flag[0:1, 0:1], banks[7][0:1, 64:65]).then_inc(flag_set, 1)
            v.memset(zero[:, :], 0.0).then_inc(s_off, 1)

            def hots(s, f, nq, st):
                need(dve, t_tr, s)
                need(dve, t_low, 2 * s)
                one_hots(f, 0, nq, t_oh)
                need(dve, t_look, s)
                v.tensor_tensor(spread[:, 0:nq, :, :], offsets[:, :, ds(f, nq)].rearrange("p c g -> p g c").unsqueeze(2).broadcast_to([P, nq, GT, COARSE]),
                                own_tile[:, :].unsqueeze(1).unsqueeze(3).broadcast_to([P, nq, GT, COARSE]), ALU.mult).then_inc(t_spread, 1)

            def ranks(s, f, nq, st, q):
                if q == 0:
                    need(dve, t_place, s)
                    dve.wait_ge(t_key, 16 * s + 16)
                for j in range(GT):
                    last = v.scalar_tensor_tensor(eq[:, q, j, :], key_row[:, q, j * P:(j + 1) * P], src_f[:, ds((f + q) * GT + j, 1)],
                                                  earlier[:, :], ALU.is_equal, ALU.mult, accum_out=rank[:, q, j:j + 1])
                if q == nq - 1:
                    last.then_inc(t_rank, 1)

            def own_offset(s, f, nq, st):
                dve.wait_ge(t_look, s + 1)
                v.tensor_tensor(lows[:, 0:nq, :, :], looked[:, 0:nq * GT * COARSE].rearrange("p (q t l) -> p q t l", q=nq, l=COARSE),
                                oh_coarse[:, 0:nq, :, :], ALU.mult).then_inc(t_low, 1)
                dve.wait_ge(t_low, 2 * s + 1)
                v.tensor_reduce(before[:, 0:nq, :], lows[:, 0:nq, :, :], AX.X, ALU.add).then_inc(t_low, 1)

            def hidden_max(s, f, nq, st):
                dve.wait_ge(f_abs, s + 1)
                need(dve, f_w, s)
                v.tensor_scalar(hid[0:F, 0:nq * GE], pair_banks[HID:HID + F, 0:nq * GE], fb1, 0.0, ALU.add, ALU.max).then_inc(f_pos, 1)

            def hidden_sum(s, f, nq, st):
                dve.wait_ge(f_pos, s + 1)
                dve.wait_ge(f_ln, s + 1)
                h = hid[0:F, 0:nq * GE]
                v.scalar_tensor_tensor(h, h, -LOG2, hid_abs[:, 0:nq * GE], ALU.add, ALU.add).then_inc(f_hid, 1)

            def settle(s, f, nq, st):
                need(dve, f_st, st)
                row = frow_t[:, 0:nq, :, :].rearrange("p q t r -> p (q t) r")
                v.tensor_copy(row[:, :, P:P + 4], y4[:, ds(f * GT, nq * GT), :])
                v.tensor_copy(row[:, :, P + 4], src_f[:, ds(f * GT, nq * GT)])
                v.tensor_copy(row[:, :, P + 5], dst0[:, ds(f * GT, nq * GT)]).then_inc(f_rowy, 1)
                dve.wait_ge(t_low, 2 * s + 2)
                dve.wait_ge(t_rank, s + 1)
                v.tensor_tensor(place[:, 0:nq, :], before[:, 0:nq, :], rank[:, 0:nq, :], ALU.add).then_inc(t_place, 1)

            def windows(g, u):
                need(dve, c_seg, g - 1)
                v.tensor_tensor(oh[:, u % 2, :, :], iota[:, 0:W].unsqueeze(1).broadcast_to([P, GT, W]),
                                rel[:, ds(g * GT, GT)].unsqueeze(2).broadcast_to([P, GT, W]), ALU.is_equal).then_inc(c_oh, 1)
                dve.wait_ge(c_oh, 2 * g + 1)
                v.tensor_reduce(oh_sum[:, u % 2, :], oh[:, u % 2, :, :].rearrange("p t w -> p w t"), AX.X, ALU.add).then_inc(c_oh, 1)

            def add(g, u, n, tiles):
                for j in tiles:
                    if j == 0:
                        dve.wait_ge(gathered[u], 64 * n)
                    dve.wait_ge(c_e, GT * g + j + 1)
                    v.tensor_tensor(tile_slot(u, j), tile_slot(u, j), banks[j][:, :], ALU.add).then_inc(c_add, 1)

            def take_up(g, u):
                dve.wait_ge(c_seg, g + 1)
                need(dve, c_acc, 2 * g)
                if isinstance(g, int) and g == 0:
                    dve.wait_ge(agg_zeroed, 1)
                base = dve.value_load(base_i[0:1, ds(g, 1)], min_val=0, max_val=N - 1)
                v.tensor_tensor(aggT[:, :, ds(base, W)], aggT[:, :, ds(base, W)], seg[u % 2], ALU.add).then_inc(c_acc, 1)
                v.tensor_tensor(degree[:, ds(base, W)], degree[:, ds(base, W)], seg_deg[u % 2], ALU.add).then_inc(c_acc, 1)

            def block_of(g, u, n, begin, middle, end, first=False):
                windows(g, u)
                begin()
                add(g, u, n, range(2))
                middle()
                add(g, u, n, range(2, GT))
                if not first:
                    take_up(g - 1, u - 1)
                end()

            def nothing():
                pass

            def turn(i):
                item = beside_turn(i)
                block_of(CU * i, 0, i + 1, lambda: hots(*item), nothing, lambda: ranks(*item, 0), isinstance(i, int))
                block_of(CU * i + 1, 1, i + 1, lambda: own_offset(*item), nothing, lambda: ranks(*item, 1))
                block_of(CU * i + 2, 2, i + 1, lambda: hidden_max(*item), nothing, nothing)
                block_of(CU * i + 3, 3, i + 1, lambda: hidden_sum(*item), lambda: settle(*item), nothing)

            turn(0)
            with dve.Fori(1, CI) as i:
                turn(i)
            block_of(NG - 1, 0, CI + 1, lambda: hots(*last_turn), nothing, lambda: ranks(*last_turn, 0))
            take_up(NG - 1, 0)
            own_offset(*last_turn)
            hidden_max(*last_turn)
            hidden_sum(*last_turn)
            settle(*last_turn)
            dve.wait_ge(c_acc, 2 * NG)

            missed = dve.value_load(flag[0:1, 0:1], min_val=0, max_val=NT * P)
            with dve.If(missed != 0):
                dve.wait_ge(t_place, CI + 1)
                dve.wait_ge(f_hid, CI + 1)
                dve.sem_inc(l_acc, 1)
                with dve.Fori(0, NT) as t:
                    dve.wait_ge(l_acc, LCH * t + 1)
                    rel_t, dst_t = rel[:, ds(t, 1)], dstm[:, ds(t, 1)]
                    v.tensor_scalar(before[:, 0, 0:1], rel_t, 0.0, None, ALU.is_lt)
                    v.tensor_scalar(before[:, 0, 1:2], rel_t, float(W), None, ALU.is_ge)
                    v.tensor_scalar(before[:, 0, 2:3], dst_t, 1.0, None, ALU.add).then_inc(l_key, 1)
                    dve.wait_ge(l_key, 3 * t + 1)
                    v.tensor_tensor(before[:, 0, 3:4], before[:, 0, 0:1], before[:, 0, 1:2], ALU.add).then_inc(l_key, 1)
                    dve.wait_ge(l_key, 3 * t + 2)
                    v.tensor_scalar(before[:, 1, 0:1], before[:, 0, 2:3], before[:, 0, 3:4], -1.0, ALU.mult, ALU.add).then_inc(l_key, 1)
                    dve.wait_ge(l_key, 3 * t + 3)
                    v.tensor_scalar(ohf[:, :], iota[:, :], before[:, 1, 0:1], None, ALU.is_equal).then_inc(l_oh, 1)
                    dve.wait_ge(l_gat, 16 * (t + 1))
                    dve.wait_ge(l_e, t + 1)
                    v.tensor_tensor(work[:, 0, :], work[:, 0, :], banks[0][:, :], ALU.add).then_inc(l_add, 1)
                    for k in range(LCH):
                        dve.wait_ge(l_seg, LCH * t + k + 1)
                        for b, (n0, nn) in enumerate(PIECES):
                            if k < KC:
                                last = v.tensor_tensor(aggT[:, k, n0:n0 + nn], aggT[:, k, n0:n0 + nn], banks[1 + b][:, 0:nn], ALU.add)
                            else:
                                last = v.tensor_tensor(degree[:, n0:n0 + nn], degree[:, n0:n0 + nn], banks[1 + b][0:1, 0:nn], ALU.add)
                        last.then_inc(l_acc, 1)
                dve.wait_ge(l_acc, LCH * NT + 1)
            v.memset(zero[:, :], 0.0).then_inc(agg_ready, 1)
            dve.wait_ge(x_again, 16)

            with dve.Fori(0, NCH) as c:
                for j in range(KC):
                    q, n = j % 2, KC * c + j
                    x1, h = xT[:, j, ds(c * NC, NC)], hT[:, j, ds(c * NC, NC)]
                    r, z = gate[q]
                    cnd, dif = cand[q]
                    item = beside_step(n)
                    hots(*item)
                    ranks(*item, 0)
                    own_offset(*item)
                    ranks(*item, 1)
                    hidden_max(*item)
                    hidden_sum(*item)
                    settle(*item)
                    dve.wait_ge(d_sig, n + 1)
                    dve.wait_ge(d_n, n + 1)
                    v.scalar_tensor_tensor(cnd, banks[3 + 2 * q][:, 256:256 + NC], b_hh[:, 2 * KC + j:2 * KC + j + 1], r, ALU.add, ALU.mult).then_inc(d_hn, 1)
                    dve.wait_ge(d_hn, n + 1)
                    v.tensor_tensor(cnd, cnd, banks[3 + 2 * q][:, 0:NC], ALU.add).then_inc(d_t, 1)
                    dve.wait_ge(d_tanh, n + 1)
                    v.tensor_tensor(dif, h, cnd, ALU.subtract).then_inc(d_s[0], 1)
                    dve.wait_ge(d_s[0], n + 1)
                    v.tensor_tensor(dif, dif, z, ALU.mult).then_inc(d_s[1], 1)
                    dve.wait_ge(d_s[1], n + 1)
                    v.tensor_tensor(dif, dif, cnd, ALU.add).then_inc(d_s[2], 1)
                    dve.wait_ge(d_s[2], n + 1)
                    v.scalar_tensor_tensor(dif, dif, bn_scale[:, j:j + 1], x1, ALU.mult, ALU.add).then_inc(d_s[3], 1)
                    dve.wait_ge(d_s[3], n + 1)
                    v.scalar_tensor_tensor(x1, dif, bn_shift[:, j:j + 1], h, ALU.add, ALU.add).then_inc(d_x1, 1)
            dve.wait_ge(d_x1, NCH * KC)

            layer_norm(1, lambda c: None)
            link(v.memset(acc2, 0.0))
            dve.wait_ge(m_spread, 1)
            link(v.tensor_scalar(base2_f[:, :], banks[7][:, 0:NG], float(N - 1), None, ALU.min))
            link(v.tensor_copy(base2_i[:, :], base2_f[:, :]))
            v.tensor_scalar(base2_f[:, :], base2_f[:, :], -1.0, None, ALU.mult).then_inc(m_start, 1)

            def messages(row, ft, m, pr, t, prod_sem, prod_n, done):
                def over_c(x):
                    return x.unsqueeze(2).broadcast_to([P, t, 3, F])

                def over_f(x):
                    return x.unsqueeze(3).broadcast_to([P, t, 3, F])

                def by_c(x):
                    return x.rearrange("p t (c f) -> p t c f", c=3)

                s, vec = ft[:, :, 0:F], by_c(ft[:, :, F:P])
                flt = [row[:, :, k * F:(k + 1) * F] for k in range(4)]
                ys, yv = row[:, :, P:P + 1], row[:, :, P + 1:P + 4]
                mb = m[:, :, P:MSG].rearrange("p t (c k f) -> p t c k f", c=3, k=2)
                p0, p2, p1, p3 = pr[:, :, 0:F], pr[:, :, F:2 * F], by_c(pr[:, :, 2 * F:5 * F]), by_c(pr[:, :, 5 * F:8 * F])
                v.tensor_tensor(p0, s, flt[0], ALU.mult)
                v.tensor_tensor(p2, s, flt[2], ALU.mult)
                v.tensor_tensor(p1, vec, over_c(flt[1]), ALU.mult)
                v.tensor_tensor(p3, vec, over_c(flt[3]), ALU.mult).then_inc(prod_sem, 1)
                dve.wait_ge(prod_sem, prod_n)
                v.tensor_tensor(m[:, :, 0:F], p0, ys.broadcast_to([P, t, F]), ALU.mult)
                v.tensor_tensor(by_c(m[:, :, F:P]), p1, over_f(yv), ALU.mult)
                v.tensor_tensor(mb[:, :, :, 0], over_c(p2), over_f(yv), ALU.mult)
                v.tensor_tensor(mb[:, :, :, 1], p3, ys.unsqueeze(3).broadcast_to([P, t, 3, F]), ALU.mult).then_inc(done, 1)

            def message_dve(g, u, n):
                dve.wait_ge(m_rel, g + 1)
                need(dve, m_seg, g - MR + 1)
                v.tensor_tensor(oh2[:, u % MR, :, :], iota[:, 0:W2].unsqueeze(1).broadcast_to([P, GT, W2]),
                                rel2[:, ds(g * GT, GT)].unsqueeze(2).broadcast_to([P, GT, W2]), ALU.is_equal).then_inc(m_oh, 1)
                dve.wait_ge(m_ld[u], 16 * n)
                dve.wait_ge(m_gat[u % MR], 64 * gather_uses(u, n))
                need(dve, m_msg, g)
                messages(rows[u], feat[u % MR], msg[u % MR], prod, GT, m_prod, g + 1, m_msg)

            def take_up2(g, u):
                dve.wait_ge(m_seg, g + 1)
                need(dve, m_acc, g)
                base = dve.value_load(base2_i[0:1, ds(g, 1)], min_val=0, max_val=N - 1)
                v.tensor_tensor(acc2[:, :, ds(base, W2)], acc2[:, :, ds(base, W2)], seg2[u % MR], ALU.add).then_inc(m_acc, 1)

            for u in range(MU):
                message_dve(u, u, 1)
                if u >= 2:
                    take_up2(u - 2, u - 2)
            with dve.Fori(1, NG // MU) as i:
                for u in range(MU):
                    message_dve(MU * i + u, u, i + 1)
                    take_up2(MU * i + u - 2, (u - 2) % MU)
            take_up2(NG - 2, MU - 2)
            take_up2(NG - 1, MU - 1)
            dve.wait_ge(m_acc, NG)

            v.tensor_scalar(in_win, rel2[:, :], float(W2), None, ALU.is_ge)
            link(v.tensor_scalar(left2[:, :], key2[:, :], float(N), None, ALU.is_lt))
            link(v.tensor_tensor(in_win, in_win, left2[:, :], ALU.mult))
            v.tensor_reduce(n_left[:, :], in_win, AX.X, ALU.add).then_inc(miss_sum, 1)
            link(v.tensor_scalar(left2[:, :], key2[:, :], 1.0, None, ALU.add))
            link(v.tensor_tensor(left2[:, :], left2[:, :], in_win, ALU.mult))
            link(v.tensor_scalar(left2[:, :], left2[:, :], -1.0, None, ALU.add))
            dve.wait_ge(miss_total, 2)
            v.tensor_copy(flag2[0:1, 0:1], banks[7][0:1, 0:1]).then_inc(flag2_set, 1)
            dve.wait_ge(flag2_set, 1)
            missed = dve.value_load(flag2[0:1, 0:1], min_val=0, max_val=NT * P)
            with dve.If(missed != 0):
                dve.sem_inc(n_acc, 1)
                with dve.Fori(0, NT) as t:
                    dve.wait_ge(n_gat, 16 * (t + 1))
                    dve.wait_ge(n_acc, MCH * t + 1)
                    messages(rows[0][:, 0:1, :], feat[0][:, 0:1, :], msg[0][:, 0:1, :], prod[:, 0:1, :], 1, n_prod, t + 1, n_msg)
                    v.tensor_scalar(ohf[:, :], iota[:, :], left2[:, ds(t, 1)], None, ALU.is_equal).then_inc(n_oh, 1)
                    for k in range(MCH):
                        dve.wait_ge(n_seg, MCH * t + k + 1)
                        rows_k = slice(0, P if k < 2 else MSG - 2 * P)
                        for b, (n0, nn) in enumerate(PIECES):
                            last = v.tensor_tensor(acc2[rows_k, k, n0:n0 + nn], acc2[rows_k, k, n0:n0 + nn], banks[1 + b][rows_k, 0:nn], ALU.add)
                        last.then_inc(n_acc, 1)
                dve.wait_ge(n_acc, MCH * NT + 1)
            v.memset(zero[:, :], 0.0).then_inc(acc2_ready, 1)

            for c, (n0, nn) in enumerate(PIECES):
                dve.wait_ge(o_abs, c + 1)
                need(dve, o_mm2, c)
                u = work[:, 1, 0:nn]
                v.tensor_scalar(u, banks[0][:, 0:nn], 0.125, 0.0, ALU.mult, ALU.max).then_inc(o_pos, 1)
                dve.wait_ge(o_pos, c + 1)
                dve.wait_ge(o_ln, c + 1)
                v.scalar_tensor_tensor(u, u, -LOG2, work[:, 0, 0:nn], ALU.add, ALU.add).then_inc(o_ssp, 1)
                dve.wait_ge(o_mm2, c + 1)
                for k in range(KC):
                    xk = xT[:, k, n0:n0 + nn]
                    last = v.scalar_tensor_tensor(xk, banks[4 + k][:, 0:nn], float(P) ** -0.5, xk, ALU.mult, ALU.add)
                last.then_inc(o_out, 1)

        @block.tensor
        def _(pe):
            mm = nc.tensor.matmul

            def chunk_mean(l, c):
                need(pe, ln[l]["dev"], c)
                for k in range(KC):
                    last = mm(banks[0][:, 0:NC], onesm[:, :], xT[:, k, ds(c * NC, NC)], start=(k == 0), stop=(k == KC - 1))
                last.then_inc(ln[l]["mean"], 1)

            def chunk_variance(l, c):
                pe.wait_ge(ln[l]["sq"], c + 1)
                need(pe, ln[l]["std"], c)
                for k in range(KC):
                    last = mm(banks[1][:, 0:NC], onesm[:, :], sq[:, k, ds(c * NC, NC)], start=(k == 0), stop=(k == KC - 1))
                last.then_inc(ln[l]["var"], 1)

            def table_tile(l, t, q):
                pe.wait_ge(tb[l]["stage"], t + 1)
                need(pe, tb[l]["out"], t - 1)
                if l == 0:
                    for k in range(KC):
                        mm(banks[2 + q][0:NTL, :], stage[q][:, k, 0:NTL], wbuf[:, k, :], start=(k == 0), stop=False)
                    last = mm(banks[2 + q][0:NTL, :], ones[0:1, 0:NTL], bias_row[:, :], start=False, stop=True)
                else:
                    for k in range(KC):
                        last = mm(banks[2 + q][0:NTL, k * F:(k + 1) * F], stage[q][:, k, 0:NTL], w_in[:, min(k, 1), :], start=True, stop=True)
                last.then_inc(tb[l]["mm"], 1)

            def count(n, q):
                pe.wait_ge(s_oh, n + 1)
                need(pe, s_hist, n - 1)
                for g in range(CB):
                    for j in range(GT):
                        last = mm(banks[4 + q][FINE * j:FINE * (j + 1), g * COARSE:(g + 1) * COARSE],
                                  hot_f[q][:, g * GT + j, :], hot_c[q][:, g * GT + j, :], start=True, stop=True)
                last.then_inc(s_count, 1)

            def norm_and_table(l, beside):
                def body(c, has_next, has_last):
                    beside(c, 0)
                    if has_next:
                        chunk_mean(l, c + 1)
                    chunk_variance(l, c)
                    if has_last:
                        table_tile(l, 2 * c - 2, 0)
                        table_tile(l, 2 * c - 1, 1)
                    if has_next:
                        beside(c, 1)

                chunk_mean(l, 0)
                body(0, True, False)
                body(1, True, True)
                with pe.Fori(2, NCH - 1) as c:
                    body(c, True, True)
                body(NCH - 1, False, True)
                table_tile(l, 2 * NCH - 2, 0)
                table_tile(l, 2 * NCH - 1, 1)

            pe.wait_ge(prep_done, 1)
            pe.wait_ge(x_loaded, 16)
            pe.wait_ge(weights_loaded, 16 * WL)
            norm_and_table(0, lambda c, half: count(2 * c + half, half))

            pe.wait_ge(s_set, 1)
            mm(banks[7][:, 0:COARSE], others, start_c, start=True, stop=False)
            mm(banks[7][:, 0:COARSE], behind, total, start=False, stop=True).then_inc(s_corr, 1)
            pe.wait_ge(miss_sum, 1)
            pe.wait_ge(s_lead, 1)
            mm(banks[7][:, 64:65], ones[:, :], n_left[:, :], start=True, stop=True).then_inc(miss_total, 1)
            pe.wait_ge(flag_set, 1)
            pe.wait_ge(tb[0]["out"], NTT)
            pe.wait_ge(s_hist, 2 * NCH - 1)

            def turn_fine(s, f, nq, st):
                pe.wait_ge(t_oh, s + 1)
                need(pe, f_roww, s)
                for q in range(nq):
                    last = nc.tensor.transpose(turned[:, q * P:(q + 1) * P], oh_fine[:, q, :, :].rearrange("p t k -> p (t k)"), ident[:, :])
                last.then_inc(t_tr, 1)

            def look(s, f, nq, st):
                pe.wait_ge(t_spread, s + 1)
                pe.wait_ge(t_fT, s + 1)
                for q in range(nq):
                    last = mm(looked[:, q * GT * COARSE:(q + 1) * GT * COARSE], fine_T[:, q, :],
                              spread[:, q, :, :].rearrange("p t c -> p (t c)"), start=True, stop=True)
                last.then_inc(t_look, 1)

            def hidden_product(s, f, nq, st):
                pe.wait_ge(t_low, 2 * s + 1)
                pe.wait_ge(f_ld, 16 * s + 16)
                pe.sem_inc(pe_passed, 1)
                for q in range(nq):
                    last = mm(pair_banks[HID:HID + F, q * GE:(q + 1) * GE], fw1, feat_in[:, q * GE:(q + 1) * GE], start=True, stop=True)
                last.then_inc(f_h, 1)

            def filter_product(s, f, nq, st):
                pe.wait_ge(f_hid, s + 1)
                for j in range(nq * GT):
                    last = mm(pair_banks[:, j * P:(j + 1) * P], hid[:, j * P:(j + 1) * P], fw2, start=True, stop=True)
                last.then_inc(f_w, 1)

            def edge_product(g, u, n, j):
                if j == 0:
                    pe.wait_ge(ea_s[u % 2], 16 * n)
                need(pe, c_add, GT * (g - 1) + j + 1)
                mm(banks[j][:, :], ea[:, u % 2, j * P:(j + 1) * P], w1e[:, :], start=True, stop=True).then_inc(c_e, 1)

            def segment(g, u, j):
                if j == 0:
                    pe.wait_ge(c_oh, 2 * g + 2)
                    need(pe, c_acc, 2 * (g - 1))
                pe.wait_ge(c_relu, GT * g + j + 1)
                for k in range(KC):
                    mm(seg[u % 2][:, k, :], tile_slot(u, j)[:, k * P:(k + 1) * P], oh[:, u % 2, j, :],
                       start=(j == 0 and k == 0), stop=(j == GT - 1), skip_group_check=True)
                if j == GT - 1:
                    mm(seg_deg[u % 2], ones[:, 0:1], oh_sum[:, u % 2, :], start=False, stop=True, skip_group_check=True).then_inc(c_seg, 1)

            def block_of(g, u, n, tiles, first=False):
                for j in tiles:
                    edge_product(g, u, n, j)
                    if not first:
                        segment(g - 1, (u - 1) % CU, j)

            def turn(i):
                item = beside_turn(i)
                first = isinstance(i, int)
                block_of(CU * i, 0, 2 * i + 1, range(2), first)
                turn_fine(*item)
                block_of(CU * i, 0, 2 * i + 1, range(2, GT), first)
                look(*item)
                block_of(CU * i + 1, 1, 2 * i + 1, range(2))
                hidden_product(*item)
                block_of(CU * i + 1, 1, 2 * i + 1, range(2, GT))
                block_of(CU * i + 2, 2, 2 * i + 2, range(GT))
                block_of(CU * i + 3, 3, 2 * i + 2, range(2))
                filter_product(*item)
                block_of(CU * i + 3, 3, 2 * i + 2, range(2, GT))

            turn(0)
            with pe.Fori(1, CI) as i:
                turn(i)
            block_of(NG - 1, 0, 2 * CI + 1, range(GT))
            turn_fine(*last_turn)
            for j in range(GT):
                segment(NG - 1, 0, j)
            look(*last_turn)
            hidden_product(*last_turn)
            filter_product(*last_turn)

            pe.wait_ge(flag_set, 1)
            missed = pe.value_load(flag[0:1, 0:1], min_val=0, max_val=NT * P)
            with pe.If(missed != 0):
                with pe.Fori(0, NT) as t:
                    pe.wait_ge(l_acc, LCH * t + 1)
                    pe.wait_ge(l_ld, 16 * (t + 1))
                    mm(banks[0][:, :], ea[:, 0, 0:P], w1e[:, :], start=True, stop=True).then_inc(l_e, 1)
                    pe.wait_ge(l_oh, t + 1)
                    pe.wait_ge(l_relu, t + 1)
                    for k in range(LCH):
                        if k:
                            pe.wait_ge(l_acc, LCH * t + k + 1)
                        for b, (n0, nn) in enumerate(PIECES):
                            if k < KC:
                                last = mm(banks[1 + b][:, 0:nn], work[:, 0, k * P:(k + 1) * P], ohf[:, n0:n0 + nn], start=True, stop=True)
                            else:
                                last = mm(banks[1 + b][0:1, 0:nn], ones[:, 0:1], ohf[:, n0:n0 + nn], start=True, stop=True)
                        last.then_inc(l_seg, 1)

            pe.wait_ge(agg_ready, 1)
            pe.wait_ge(w2_loaded, 32)
            pe.wait_ge(big_loaded, 16 * (CI - 1))
            with pe.Fori(0, NCH) as c:
                cols = ds(c * NC, NC)
                for j in range(KC):
                    o = banks[j // 2][:, 256 * (j % 2):256 * (j % 2) + NC]
                    for k in range(KC):
                        mm(o, wbuf[:, k, j * P:(j + 1) * P], aggT[:, k, cols], start=(k == 0), stop=False)
                    last = mm(o, bias_row[:, j * P:(j + 1) * P], degree[:, cols], start=False, stop=True)
                last.then_inc(d_mm2, 1)
                for j in range(KC):
                    q, n = j % 2, KC * c + j
                    item = beside_step(n)

                    def gate_sum(o, kernel, part, x, start, stop):
                        w = slice(part * HD + j * P, part * HD + (j + 1) * P)
                        for k in range(KC):
                            last = mm(o, kernel[:, k, w], x[:, k, :], start=(start and k == 0), stop=(stop and k == KC - 1))
                        return last

                    if j == 0:
                        pe.wait_ge(d_agg2, c + 1)
                    if j >= 2:
                        pe.wait_ge(d_t, n - 1)
                    h = hT[:, :, cols]
                    rz, nn = banks[2 + 2 * q], banks[3 + 2 * q]
                    gate_sum(nn[:, 0:NC], wih, 2, agg2, True, True)
                    if j:
                        filter_product(*beside_step(n - 1))
                    gate_sum(nn[:, 256:256 + NC], whh, 2, h, True, True).then_inc(d_n, 1)
                    turn_fine(*item)
                    gate_sum(rz[:, 0:NC], wih, 0, agg2, True, False)
                    look(*item)
                    gate_sum(rz[:, 0:NC], whh, 0, h, False, True)
                    hidden_product(*item)
                    gate_sum(rz[:, 256:256 + NC], wih, 1, agg2, True, False)
                    gate_sum(rz[:, 256:256 + NC], whh, 1, h, False, True).then_inc(d_rz, 1)
                    if j == KC - 1:
                        filter_product(*item)
                pe.wait_ge(d_t, KC * c + KC)

            pe.wait_ge(d_x1, NCH * KC)
            norm_and_table(1, lambda c, half: None)
            pe.wait_ge(tb[1]["out"], NTT)

            pe.wait_ge(m_base, 16)
            mm(banks[7][:, 0:NG], ones[0:1, :], first_key[0:1, :, 0], start=True, stop=True).then_inc(m_spread, 1)

            def segment2(g, u):
                pe.wait_ge(m_msg, g + 1)
                pe.wait_ge(m_oh, g + 1)
                need(pe, m_acc, g - MR + 1)
                for j in range(GT):
                    for k in range(MCH):
                        width = P if k < 2 else MSG - 2 * P
                        last = mm(seg2[u % MR][0:width, k, :], msg[u % MR][:, j, k * P:k * P + width], oh2[:, u % MR, j, :],
                                  start=(j == 0 and k == 0), stop=(j == GT - 1), skip_group_check=True)
                last.then_inc(m_seg, 1)

            for u in range(MU):
                segment2(u, u)
            with pe.Fori(1, NG // MU) as i:
                for u in range(MU):
                    segment2(MU * i + u, u)

            pe.wait_ge(miss_sum, 2)
            mm(banks[7][:, 0:1], ones[:, :], n_left[:, :], start=True, stop=True).then_inc(miss_total, 1)
            pe.wait_ge(flag2_set, 1)
            missed = pe.value_load(flag2[0:1, 0:1], min_val=0, max_val=NT * P)
            with pe.If(missed != 0):
                with pe.Fori(0, NT) as t:
                    pe.wait_ge(n_msg, t + 1)
                    pe.wait_ge(n_oh, t + 1)
                    for k in range(MCH):
                        pe.wait_ge(n_acc, MCH * t + k + 1)
                        width = P if k < 2 else MSG - 2 * P
                        for b, (n0, nn) in enumerate(PIECES):
                            last = mm(banks[1 + b][0:width, 0:nn], left_msg[:, k * P:k * P + width], ohf[:, n0:n0 + nn], start=True, stop=True)
                        last.then_inc(n_seg, 1)
            pe.wait_ge(acc2_ready, 1)

            def feature_sums(c):
                cols = slice(PIECES[c][0], sum(PIECES[c]))
                need(pe, o_ev, c)
                need(pe, o_pos, c)
                for b, (w, k) in enumerate(((wo1s[:, :], 0), (wo1v[:, 0, :], 1), (wo1v[:, 1, :], 1), (wo1v[:, 0, :], 2))):
                    last = mm(banks[b][:, 0:PIECES[c][1]], w, acc2[:, k, cols], start=True, stop=True)
                last.then_inc(o_mm1, 1)

            feature_sums(0)
            for c, (n0, nn) in enumerate(PIECES):
                if c + 1 < len(PIECES):
                    feature_sums(c + 1)
                pe.wait_ge(o_ssp, c + 1)
                pe.wait_ge(o_ev, c + 1)
                need(pe, o_out, c)
                mm(banks[4][:, 0:nn], wo2[:, 0, :], work[:, 1, 0:nn], start=True, stop=True)
                for k in range(3):
                    last = mm(banks[5 + k][:, 0:nn], wo2[:, 1, :], work[:, 2 + k, 0:nn], start=True, stop=True)
                last.then_inc(o_mm2, 1)


def kernel(**inputs):
    import numpy as np
    import concourse.bacc as bacc
    from concourse import mybir as mb
    from concourse.bass_utils import run_bass_kernel_spmd as run

    g = {k: np.asarray(v) for k, v in inputs.items()}

    def perm(w):
        return np.concatenate([w[..., :P], np.moveaxis(w[..., P:].reshape(*w.shape[:-1], P, 3), -1, -2).reshape(*w.shape[:-1], 3 * P)], axis=-1)

    def chunks(w):
        return w.reshape(KC, P, -1).transpose(1, 0, 2)

    def gates(w):
        return np.concatenate([perm(x) for x in np.split(w, 3, axis=-1)], axis=-1)

    def by_edge(v, fill):
        out = np.full((NT * P,) + v.shape[1:], fill, v.dtype)
        out[:NE] = v
        return out

    def tiles(v):
        return np.moveaxis(v.reshape(NT, P, *v.shape[1:]), 1, 0)

    L0 = {k[7:]: v for k, v in g.items() if k.startswith("L0_gnn_")}
    L1 = {k[7:]: v for k, v in g.items() if k.startswith("L1_gnn_")}
    src, dst = g["src"], g["dst"]
    dst_pad = by_edge(dst, 0)
    arrays = {
        "xT": chunks(perm(g["x"]).T),
        "w1h": chunks(perm(L0["W1"][:, :HD]).T), "w1e": L0["W1"][:, HD:].T, "b1": L0["b1"][None],
        "w2": chunks(L0["W2"].T), "b2": L0["b2"][None],
        "gates": np.concatenate([chunks(w).reshape(P, -1) for w in (gates(L0["W_ih"].T), gates(perm(L0["W_hh"]).T))]
                                + [np.zeros((P, GATES - 2 * KC * 3 * HD), np.float32)], axis=1),
        "b_ih": gates(L0["b_ih"]).reshape(3 * KC, P).T, "b_hh": gates(L0["b_hh"]).reshape(3 * KC, P).T,
        **{k: perm(L0[k]).reshape(KC, P).T for k in ("gamma", "beta", "run_mean", "run_var")},
        "w_in_s": L1["w_in2f_s"], "w_in_v": L1["w_in2f_v"],
        "fw1": L1["W1"], "fb1": L1["b1"][:, None],
        "fw2": np.concatenate([L1["W2"], L1["b2"][None]]).reshape(F + 1, F, 6).transpose(0, 2, 1)[:, :4].reshape(F + 1, 4 * F),
        "wo1s": np.concatenate([L1["w_f2o1_s"]] + [L1["w_f2o1_s"][F:]] * 2), "wo1v": L1["w_f2o1_v"],
        "wo2s": L1["w_f2o2_s"], "wo2v": L1["w_f2o2_v"],
        "src0": tiles(by_edge(src, 0)), "dst0": tiles(dst_pad),
        "srck": tiles(by_edge(src, PAD_KEY)), "keys": by_edge(src, PAD_KEY)[None], "dstm": tiles(by_edge(dst, -1)),
        "base": dst_pad[None, ::GE],
        "rcut": tiles(by_edge(g["edge_weight"], 0)), "y4": tiles(by_edge(g["edge_attr_4"], 0)),
        "fT": by_edge(g["edge_attr_20"], 0).T, "eaT": by_edge(g["edge_attr_128"], 0).T,
    }
    nc = bacc.Bacc("TRN2", target_bir_lowering=False, num_devices=1)
    fed, aps = {}, {}
    for name, v in arrays.items():
        v = np.ascontiguousarray(v)
        fed[name + "_in"] = v
        aps[name] = nc.dram_tensor(name + "_in", v.shape, mb.dt.from_np(v.dtype), kind="ExternalInput").ap()
    out = nc.dram_tensor("out_dram", (P, KC, N), mb.dt.float32, kind="ExternalOutput").ap()
    graph_kernel(nc, aps, out)
    r = run(nc, [fed], core_ids=[0])
    y = np.asarray(r.results[0]["out_dram"]).transpose(1, 0, 2).reshape(HD, N).T
    return np.concatenate([y[:, :P], y[:, P:].reshape(N, 3, P).transpose(0, 2, 1).reshape(N, 3 * P)], axis=1)
```
